# Optimizing a Trainium2 kernel written in Bass

```python
import numpy as np
import jax
import jax.numpy as jnp

def _softmax(x, axis=-1):
    return jax.nn.softmax(x, axis=axis)

def _gelu(x):
    return jax.nn.gelu(x, approximate=True)

def _silu(x):
    return jax.nn.silu(x)

def _sigmoid(x):
    return jax.nn.sigmoid(x)

def _layernorm(x, axis=-1, eps=1e-05):
    m = jnp.mean(x, axis=axis, keepdims=True)
    v = jnp.var(x, axis=axis, keepdims=True)
    return (x - m) / jnp.sqrt(v + eps)

def _scatter_add(tgt, idx, src, axis=0):
    return tgt.at[idx].add(src)

def _segment_sum(src, seg, n):
    return jax.ops.segment_sum(src, seg, n)
kernel_name = 'mk_flamingo_gated_d1_seqx_r4_5ca045'

def setup_inputs(seed: int=0):
    np.random.seed(seed)
    _w = jnp.asarray

    def _rec_inputs():
        import jax
        import jax.numpy as jnp
        _rk = jax.random.key(seed)
        x = -0.000125 + 0.9999 * jax.random.normal(jax.random.fold_in(_rk, 1), (8, 256, 256), jnp.float32)
        _lenS = 256 - jax.random.randint(jax.random.fold_in(_rk, 7), (8,), 0, max(1, 256 // 4) + 1, jnp.int32)
        _lenS2 = 77 - jax.random.randint(jax.random.fold_in(_rk, 8), (8,), 0, max(1, 77 // 4) + 1, jnp.int32)
        _ctx_768P = jax.random.normal(jax.random.fold_in(_rk, 11), (8, 16, 192), jnp.float32)
        _ctx_768c = jax.random.dirichlet(jax.random.fold_in(_rk, 511), 0.3 * jnp.ones((16,), jnp.float32), (8, 77))
        _ctx_768t = jnp.einsum('bsk,bkd->bsd', _ctx_768c, _ctx_768P)
        _ctx_768t = _ctx_768t * jax.lax.rsqrt(jnp.mean(jnp.square(_ctx_768t)) + 1e-12) * 0.953939
        ctx_768 = 0.00272024 + 0.999456 * (_ctx_768t + 0.3 * jax.random.normal(jax.random.fold_in(_rk, 611), (8, 77, 192), jnp.float32))
        _g = jax.random.normal(jax.random.fold_in(_rk, 9001), (2, 1), jnp.float32)
        _g = jnp.sign(_g) * jnp.maximum(jnp.abs(_g), 1.0) + (_g == 0) * 1.0
        g_xattn = _g[0]
        g_ffn = _g[1]
        return (x, ctx_768, g_xattn, g_ffn)
    x, ctx_768, g_xattn, g_ffn = _rec_inputs()

    def _L0_xattn_setup():
        import jax, jax.numpy as jnp
        import numpy as np
        N_HEADS = 16
        DIM_EMBED = 256
        DIM_CROSS = 192
        DIM_HEAD = DIM_EMBED // N_HEADS
        key = jax.random.key(seed)
        ks = jax.random.split(key, 10)
        B, Sq, Sk = (8, 1024, 77)
        s_e = 1.0 / np.sqrt(DIM_EMBED)
        s_c = 1.0 / np.sqrt(DIM_CROSS)
        return {'x': jax.random.normal(ks[0], (B, Sq, DIM_EMBED), jnp.float32), 'y': jax.random.normal(ks[1], (B, Sk, DIM_CROSS), jnp.float32), 'wq': jax.random.normal(ks[2], (DIM_EMBED, DIM_EMBED), jnp.float32) * s_e, 'bq': jax.random.normal(ks[3], (DIM_EMBED,), jnp.float32) * 0.01, 'wk': jax.random.normal(ks[4], (DIM_CROSS, DIM_EMBED), jnp.float32) * s_c, 'bk': jax.random.normal(ks[5], (DIM_EMBED,), jnp.float32) * 0.01, 'wv': jax.random.normal(ks[6], (DIM_CROSS, DIM_EMBED), jnp.float32) * s_c, 'bv': jax.random.normal(ks[7], (DIM_EMBED,), jnp.float32) * 0.01, 'wo': jax.random.normal(ks[8], (DIM_EMBED, DIM_EMBED), jnp.float32) * s_e, 'bo': jax.random.normal(ks[9], (DIM_EMBED,), jnp.float32) * 0.01}
    _L0_xattn_all = _L0_xattn_setup()
    _L0_xattn_in = {k: v for k, v in _L0_xattn_all.items() if k in ('wq', 'bq', 'wk', 'bk', 'wv', 'bv', 'wo', 'bo')}
    del _L0_xattn_all

    def _L0_ffn_setup():
        import jax, jax.numpy as jnp
        import numpy as np
        D_MODEL = 256
        HIDDEN = 1024
        N_ROUTING = 2
        key = jax.random.key(seed)
        ks = jax.random.split(key, 10)
        s = 0.02
        x = jax.random.normal(ks[0], (4, 1024, D_MODEL), dtype=jnp.float32)
        gate_w = jax.random.normal(ks[1], (N_ROUTING, D_MODEL), dtype=jnp.float32) * s
        w1 = jax.random.normal(ks[2], (N_ROUTING, D_MODEL, HIDDEN), dtype=jnp.float32) * s
        b1 = jax.random.normal(ks[3], (N_ROUTING, HIDDEN), dtype=jnp.float32) * s
        w2 = jax.random.normal(ks[4], (N_ROUTING, HIDDEN, D_MODEL), dtype=jnp.float32) * s
        b2 = jax.random.normal(ks[5], (N_ROUTING, D_MODEL), dtype=jnp.float32) * s
        sw1 = jax.random.normal(ks[6], (D_MODEL, HIDDEN), dtype=jnp.float32) * s
        sb1 = jax.random.normal(ks[7], (HIDDEN,), dtype=jnp.float32) * s
        sw2 = jax.random.normal(ks[8], (HIDDEN, D_MODEL), dtype=jnp.float32) * s
        sb2 = jax.random.normal(ks[9], (D_MODEL,), dtype=jnp.float32) * s
        return {'x': x, 'gate_w': gate_w, 'w1': w1, 'b1': b1, 'w2': w2, 'b2': b2, 'sw1': sw1, 'sb1': sb1, 'sw2': sw2, 'sb2': sb2}
    _L0_ffn_all = _L0_ffn_setup()
    _L0_ffn_in = {k: v for k, v in _L0_ffn_all.items() if k in ('gate_w', 'w1', 'b1', 'w2', 'b2', 'sw1', 'sb1', 'sw2', 'sb2')}
    del _L0_ffn_all
    return {'x': x, 'ctx_768': ctx_768, 'g_xattn': g_xattn, 'g_ffn': g_ffn, 'L0_xattn_wq': _L0_xattn_in['wq'], 'L0_xattn_bq': _L0_xattn_in['bq'], 'L0_xattn_wk': _L0_xattn_in['wk'], 'L0_xattn_bk': _L0_xattn_in['bk'], 'L0_xattn_wv': _L0_xattn_in['wv'], 'L0_xattn_bv': _L0_xattn_in['bv'], 'L0_xattn_wo': _L0_xattn_in['wo'], 'L0_xattn_bo': _L0_xattn_in['bo'], 'L0_ffn_gate_w': _L0_ffn_in['gate_w'], 'L0_ffn_w1': _L0_ffn_in['w1'], 'L0_ffn_b1': _L0_ffn_in['b1'], 'L0_ffn_w2': _L0_ffn_in['w2'], 'L0_ffn_b2': _L0_ffn_in['b2'], 'L0_ffn_sw1': _L0_ffn_in['sw1'], 'L0_ffn_sb1': _L0_ffn_in['sb1'], 'L0_ffn_sw2': _L0_ffn_in['sw2'], 'L0_ffn_sb2': _L0_ffn_in['sb2']}

def reference(x, ctx_768, g_xattn, g_ffn, L0_xattn_wq, L0_xattn_bq, L0_xattn_wk, L0_xattn_bk, L0_xattn_wv, L0_xattn_bv, L0_xattn_wo, L0_xattn_bo, L0_ffn_gate_w, L0_ffn_w1, L0_ffn_b1, L0_ffn_w2, L0_ffn_b2, L0_ffn_sw1, L0_ffn_sb1, L0_ffn_sw2, L0_ffn_sb2):
    import jax
    import jax.numpy as jnp

    def _L0_xattn_ref(x, y, wq, bq, wk, bk, wv, bv, wo, bo):
        import jax, jax.numpy as jnp
        import numpy as np
        N_HEADS = 16
        DIM_EMBED = 256
        DIM_CROSS = 192
        DIM_HEAD = DIM_EMBED // N_HEADS
        B, Sq, E = x.shape
        H, D = (N_HEADS, DIM_HEAD)
        q = (x @ wq + bq).reshape(B, Sq, H, D).transpose(0, 2, 1, 3)
        k = (y @ wk + bk).reshape(B, -1, H, D).transpose(0, 2, 1, 3)
        v = (y @ wv + bv).reshape(B, -1, H, D).transpose(0, 2, 1, 3)
        scores = jnp.einsum('bhqd,bhkd->bhqk', q, k) / jnp.sqrt(jnp.asarray(D, x.dtype))
        attn = jax.nn.softmax(scores, axis=-1)
        out = jnp.einsum('bhqk,bhkd->bhqd', attn, v)
        out = out.transpose(0, 2, 1, 3).reshape(B, Sq, E)
        return out @ wo + bo

    def _L0_ffn_ref(x, gate_w, w1, b1, w2, b2, sw1, sb1, sw2, sb2):
        import jax, jax.numpy as jnp
        import numpy as np
        D_MODEL = 256
        HIDDEN = 1024
        N_ROUTING = 2
        B, S, D = x.shape
        xf = x.reshape(-1, D)
        gate_scores = xf @ gate_w.T
        gate_probs = jax.nn.softmax(gate_scores, axis=-1)
        top1 = jnp.argmax(gate_probs, axis=-1)
        one_hot = jax.nn.one_hot(top1, N_ROUTING, dtype=xf.dtype)
        masked = xf[None, :, :] * one_hot.T[:, :, None]
        h = jax.nn.relu(jnp.einsum('end,edh->enh', masked, w1) + b1[:, None, :])
        expert_out = jnp.einsum('enh,ehd->end', h, w2) + b2[:, None, :]
        routing_output = expert_out.sum(axis=0)
        shared = jax.nn.relu(xf @ sw1 + sb1) @ sw2 + sb2
        return (routing_output + shared).reshape(B, S, D)
    x = x + jnp.tanh(g_xattn[0]) * _L0_xattn_ref(_layernorm(x, axis=-1), ctx_768, L0_xattn_wq, L0_xattn_bq, L0_xattn_wk, L0_xattn_bk, L0_xattn_wv, L0_xattn_bv, L0_xattn_wo, L0_xattn_bo)
    x = x + jnp.tanh(g_ffn[0]) * _L0_ffn_ref(_layernorm(x, axis=-1), L0_ffn_gate_w, L0_ffn_w1, L0_ffn_b1, L0_ffn_w2, L0_ffn_b2, L0_ffn_sw1, L0_ffn_sb1, L0_ffn_sw2, L0_ffn_sb2)
    return x

_drawn_inputs = setup_inputs


def setup_inputs(seed=0):
    import zlib

    import numpy as np

    out = dict(_drawn_inputs(seed))
    spreads = {}
    factors = {'L0_xattn_bq': 30.958,
     'L0_xattn_bk': 64.0,
     'L0_xattn_bv': 6.788,
     'L0_xattn_bo': 6.511,
     'L0_ffn_b1': 5.842,
     'L0_ffn_sb1': 7.667,
     'L0_ffn_sb2': 3.199}
    for name, (base, spread) in spreads.items():
        noise = np.random.default_rng([zlib.crc32(name.encode()), seed]).standard_normal(out[name].shape)
        drawn = base * np.exp(spread * noise) if base else spread * noise
        out[name] = jnp.asarray(drawn.astype(out[name].dtype))
    for name, factor in factors.items():
        out[name] = (out[name] * factor).astype(out[name].dtype)
    return out
```

```python
from contextlib import ExitStack

import concourse.bass as bass
from concourse import mybir

F32 = mybir.dt.float32
F32R = mybir.dt.float32r
I32 = mybir.dt.int32
U32 = mybir.dt.uint32
ALU = mybir.AluOpType
ACT = mybir.ActivationFunctionType
AX_X = mybir.AxisListType.X

P = 128
BATCHES, SEQ, DIM = 8, 256, 256
KEYS, CROSS = 77, 192
HEADS = 16
HEAD_DIM = DIM // HEADS
HIDDEN = 1024
EXPERTS = 2
EPS = 1e-5
TOKENS = BATCHES * SEQ
TILES = TOKENS // P
TB = SEQ // P
KC = DIM // P
GROUPS = KC
HG = HEADS // GROUPS
GK = HG * KEYS
HALF = GK // 2
HH = HG // 2
CHUNKS = -(-GK // P)
ROWS = [min(P, GK - c * P) for c in range(CHUNKS)]
PAIRS = BATCHES // 2
TP = 2 * TB
PTOK = TP * P
CK = 96
CKC = CROSS // CK
HC = HIDDEN // P
YH = 4 * KEYS
RT = 2
RTOK = RT * P
RTILES = TOKENS // RTOK + 1
SLOTS = RTILES * RTOK
ROW = DIM + 1
V_B1 = 2 * GROUPS
V_GATE = V_B1 + (1 + EXPERTS) * HC
VECS = V_GATE + EXPERTS * KC
NO_TOKEN = 1 << 14

ATT = ([("in", 0, 0), ("in", 1, 0)] + [("scores", 0, k) for k in range(4)]
       + [("scores", 1, k) for k in range(4)] + [("out", 0, 0), ("out", 1, 0), ("norm2", 0, 0)])
FFN_AFTER = {3: 0, 4: 1, 5: 2, 6: 3, 7: 4, 8: 5, 9: 6, 10: 7, 11: HC}


def value_pieces():
    for h in range(HG):
        k = 0
        while k < KEYS:
            row = h * KEYS + k
            n = min(KEYS - k, P - row % P)
            yield h, k, k + n, row // P, row % P
            k += n


PIECES = list(value_pieces())


def steps(attention, ffn):
    for n, step in enumerate(ATT):
        if attention:
            yield step
        if ffn and n in FFN_AFTER:
            yield ("ffn", 0, FFN_AFTER[n])


def build(nc, x, ctx_768, g_xattn, g_ffn, wq, bq, wk, bk, wv, bv, wo, bo,
          gate_w, w1, b1, w2, b2, sw1, sb1, sw2, sb2, out):
    values_dram = nc.dram_tensor("values_dram", (BATCHES, KEYS, DIM), F32).ap()
    sorted_dram = nc.dram_tensor("sorted_dram", (SLOTS + RTOK, ROW), F32).ap()
    part_dram = nc.dram_tensor("part_dram", (TOKENS, DIM), F32).ap()

    def tiled(rows):
        return rows.rearrange("(t p) d -> p t d", p=P)

    x_rows = tiled(x.rearrange("b s d -> (b s) d"))

    ctx = ExitStack()
    with ctx:
        def sem(name):
            return ctx.enter_context(nc.semaphore(name))

        def sb(name, shape, dt=F32, scope=ctx):
            return scope.enter_context(nc.sbuf_tensor(name, shape, dt))

        x_all = sb("x_all", [P, TILES, DIM])
        xn2_all = sb("xn2_all", [P, TILES, ROW])
        x2T = [sb(f"x2T_{n}", [P, KC, PTOK], F32R) for n in ("hi", "lo")]
        h32 = sb("h32", [P, 2, PTOK])
        hT = [sb(f"hT_{n}", [P, 2, PTOK], F32R) for n in ("hi", "lo")]
        sw1_sb = [sb(f"sw1_{n}", [P, KC, HIDDEN], F32R) for n in ("hi", "lo")]
        sw2_sb = [sb(f"sw2_{n}", [P, HC, DIM], F32R) for n in ("hi", "lo")]
        stage = sb("stage", [P, 2, KC * HIDDEN])
        ident = sb("ident", [P, P])
        gains = sb("gains", [P, 2])
        vec_rows = sb("vec_rows", [VECS, P])
        vec_cols = sb("vec_cols", [P, VECS])
        bq_sb = vec_cols[:, 0:GROUPS]
        bk_sb = vec_cols[:, GROUPS:2 * GROUPS]
        b1_sb = vec_cols[:, V_B1:V_GATE].rearrange("p (m c) -> p m c", c=HC)
        gw32 = vec_cols[:, V_GATE:VECS].rearrange("p (e k) -> p e k", e=EXPERTS)
        gw = [sb(f"gw_{n}", [P, EXPERTS, KC], F32R) for n in ("hi", "lo")]
        fill = sb("fill", [P, 1])
        eps_sb = sb("eps_sb", [P, 1])
        bias_rows = sb("bias_rows", [P, 2, DIM])
        stats = sb("stats", [P, TILES, 6])
        mv = sb("mv", [P, TILES, 2])
        rstd = sb("rstd", [P, TILES])
        nt = sb("nt", [P, 2, TILES])
        stats2 = sb("stats2", [P, TP, 6])
        mv2 = sb("mv2", [P, TP, 2])
        rstd2 = sb("rstd2", [P, TP])
        nt2 = sb("nt2", [P, 2, TP])
        gate_sb = sb("gate_sb", [P, TILES, EXPERTS])
        relu_b1 = sb("relu_b1", [P, EXPERTS, HC])
        relu_b1p = [sb(f"relu_b1_{n}", [P, EXPERTS, HC], F32R) for n in ("hi", "lo")]

        att = ExitStack()
        wq_sb = sb("wq_sb", [P, KC, DIM], scope=att)
        wo_sb = sb("wo_sb", [P, KC, DIM], scope=att)
        wk_sb = sb("wk_sb", [CK, CKC, DIM], scope=att)
        wv_sb = sb("wv_sb", [CK, CKC, DIM], scope=att)
        bv_row = sb("bv_row", [KEYS, DIM], scope=att)
        y_sb = sb("y_sb", [KEYS, BATCHES, CROSS], scope=att)
        yT = sb("yT", [CK, CKC, BATCHES * KEYS], scope=att)
        kT = sb("kT", [P, GROUPS, BATCHES * KEYS], scope=att)
        v_sb = sb("v_sb", [KEYS, 2, DIM], scope=att)
        k_diag = sb("k_diag", [P, 2, GROUPS, GK], scope=att)
        v_diag = sb("v_diag", [P, 2, GROUPS, CHUNKS, P], scope=att)
        xn = sb("xn", [P, 2, TB, DIM], scope=att)
        xnT = sb("xnT", [P, 2, KC, SEQ], scope=att)
        qT = sb("qT", [P, 2, GROUPS, SEQ], scope=att)
        probs = sb("probs", [P, 2, 4, GK], scope=att)
        pT = sb("pT", [P, GROUPS * CHUNKS, SEQ], scope=att)
        oT = sb("oT", [P, GROUPS, SEQ], scope=att)
        xn2 = sb("xn2", [P, TP, DIM], scope=att)
        smax = sb("smax", [P, 2, 4, HG], scope=att)
        rsum = sb("rsum", [P, 2, 4, HG], scope=att)
        rinv = sb("rinv", [P, 2, 4, HG], scope=att)
        att.close()

        ew1_sb = [sb(f"ew1_{n}", [P, EXPERTS, KC, HIDDEN], F32R) for n in ("hi", "lo")]
        ew2_sb = [sb(f"ew2_{n}", [P, EXPERTS, HC, DIM], F32R) for n in ("hi", "lo")]
        xs = sb("xs", [P, RT, ROW])
        xsT = [sb(f"xsT_{n}", [P, 2, KC, RTOK], F32R) for n in ("hi", "lo")]
        slot_token = sb("slot_token", [P, RT], U32)
        part = sb("part", [P, RT, DIM])
        final = sb("final", [P, RT, DIM])
        other_row = sb("other_row", [P, EXPERTS, DIM])
        before = sb("before", [P, P])
        ones = sb("ones", [P, P])
        chosen = sb("chosen", [P, TILES])
        tile_sum = sb("tile_sum", [P, TILES])
        prefix = sb("prefix", [P, TILES])
        rank1 = sb("rank1", [P, TILES])
        count0 = sb("count0", [P, 1])
        seams = sb("seams", [P, RTILES - 2])
        past = sb("past", [P, RTILES - 2])
        tiles0 = sb("tiles0", [P, 1])
        tiles0_int = sb("tiles0_int", [P, 1], I32)
        base1 = sb("base1", [P, 1])
        number = sb("number", [P, TILES])
        rank0 = sb("rank0", [P, TILES])
        moved = sb("moved", [P, TILES])
        place = sb("place", [P, TILES])
        place_int = sb("place_int", [P, TILES], U32)
        zero_tile = sb("zero_tile", [P, TILES])

        bank = [ctx.enter_context(nc.psum_tensor(f"bank{n}", [P, 512], F32)) for n in range(4)]
        h_ps = ctx.enter_context(nc.psum_tensor("h_ps", [P, 2, 512], F32))
        y_ps = ctx.enter_context(nc.psum_tensor("y_ps", [P, TP, DIM], F32))

        consts_made = sem("consts_made")
        x_in = sem("x_in")
        small_in = sem("small_in")
        context_in = sem("context_in")
        vecs_in = sem("vecs_in")
        vecs_ps = sem("vecs_ps")
        vecs_rdy = sem("vecs_rdy")
        stage_in = [sem(f"stage_in{n}") for n in range(2)]
        gains_ready = sem("gains_ready")
        rows_ready = sem("rows_ready")
        yT_ps = sem("yT_ps")
        yT_sb = sem("yT_sb")
        kT_ps = sem("kT_ps")
        kT_sb = sem("kT_sb")
        v_ps = sem("v_ps")
        v_rdy = sem("v_rdy")
        v_out = [sem(f"v_out{n}") for n in range(2)]
        cleared = sem("cleared")
        dve_chain = sem("dve_chain")
        var_ready = sem("var_ready")
        rstd_guess = sem("rstd_guess")
        w_hi = sem("w_hi")
        w_lo = sem("w_lo")
        gw_cut = sem("gw_cut")
        k_in = [sem(f"k_in{n}") for n in range(2)]
        v_in = [sem(f"v_in{n}") for n in range(2)]
        xn_ready = sem("xn_ready")
        x_biased = sem("x_biased")
        xnT_ps = sem("xnT_ps")
        xnT_sb = sem("xnT_sb")
        q_ps = sem("q_ps")
        q_sb = sem("q_sb")
        s_ps = sem("s_ps")
        s_max = sem("s_max")
        s_shifted = sem("s_shifted")
        p_exp = sem("p_exp")
        p_sum = sem("p_sum")
        p_rinv = sem("p_rinv")
        p_ready = sem("p_ready")
        pT_ps = sem("pT_ps")
        pT_sb = sem("pT_sb")
        o_ps = sem("o_ps")
        o_sb = sem("o_sb")
        proj_ps = sem("proj_ps")
        x1_ready = sem("x1_ready")
        var2_ready = sem("var2_ready")
        guess2 = sem("guess2")
        xn2_ready = sem("xn2_ready")
        xn2_kept = sem("xn2_kept")
        x1_biased = sem("x1_biased")
        x2T_ps = sem("x2T_ps")
        x2T_hi = sem("x2T_hi")
        x2T_lo = sem("x2T_lo")
        gate_ps = sem("gate_ps")
        gate_rdy = sem("gate_rdy")
        h_in_ps = sem("h_in_ps")
        h_hi = sem("h_hi")
        h_32 = sem("h_32")
        h_lo = sem("h_lo")
        y_used = sem("y_used")
        y_out = sem("y_out")
        part_out = sem("part_out")
        filled = sem("filled")
        chosen_rdy = sem("chosen_rdy")
        counts_ps = sem("counts_ps")
        places_rdy = sem("places_rdy")
        scattered = sem("scattered")
        seam_rdy = sem("seam_rdy")
        rb_cut = sem("rb_cut")
        other_ps = sem("other_ps")
        other_rdy = sem("other_rdy")
        xs_in = sem("xs_in")
        ids_copied = sem("ids_copied")
        xsT_ps = sem("xsT_ps")
        xsT_hi = sem("xsT_hi")
        xsT_lo = sem("xsT_lo")
        gathered = sem("gathered")
        part_rdy = sem("part_rdy")
        final_rdy = sem("final_rdy")
        rows_out = sem("rows_out")
        iotas = sem("iotas")

        SMALL = 16 * 8

        def one_bank(rows, g=4, n=KEYS):
            return rows.rearrange("p (h k) -> p h k", k=n)

        block = ctx.enter_context(nc.Block())

        @block.sync
        def _(sp):
            sp.dma_start(x_all[:, :, :], x_rows).then_inc(x_in, 16)
            sp.dma_start(y_sb[:, :, :], ctx_768.rearrange("b s d -> s b d")).then_inc(context_in, 16)
            sp.dma_start(wk_sb[:, :, :], wk.rearrange("(k p) d -> p k d", p=CK)).then_inc(context_in, 16)
            sp.dma_start(wv_sb[:, :, :], wv.rearrange("(k p) d -> p k d", p=CK)).then_inc(context_in, 16)
            sp.dma_start(wq_sb[:, :, :], wq.rearrange("(k p) d -> p k d", p=P)).then_inc(small_in, 16)
            sp.dma_start(wo_sb[:, :, :], wo.rearrange("(k p) d -> p k d", p=P)).then_inc(small_in, 16)
            sp.dma_start(gains[:, 0:1], g_xattn.partition_broadcast(P)).then_inc(small_in, 16)
            sp.dma_start(gains[:, 1:2], g_ffn.partition_broadcast(P)).then_inc(small_in, 16)
            sp.dma_start(bv_row[:, :], bv.partition_broadcast(KEYS)).then_inc(small_in, 16)
            sp.dma_start(bias_rows[:, 0, :], bo.partition_broadcast(P)).then_inc(small_in, 16)
            sp.dma_start(bias_rows[:, 1, :], sb2.partition_broadcast(P)).then_inc(small_in, 16)
            sp.dma_start(h32[:, 0, 0:2 * DIM],
                         b2.rearrange("e d -> (e d)").partition_broadcast(P)).then_inc(small_in, 16)
            at = 0
            for vec in (bq, bk, sb1, b1.rearrange("e h -> (e h)"), gate_w.rearrange("e d -> (e d)")):
                n = vec.shape[0] // P
                sp.dma_start(vec_rows[at:at + n, :], vec.rearrange("(n p) -> n p", p=P)).then_inc(vecs_in, 16)
                at += n
            sp.dma_start(stage[:, 0, :].rearrange("p (k h) -> p k h", k=KC),
                         sw1.rearrange("(k p) h -> p k h", p=P)).then_inc(stage_in[0], 16)
            sp.dma_start(stage[:, 1, :].rearrange("p (c d) -> p c d", c=HC),
                         sw2.rearrange("(c p) d -> p c d", p=P)).then_inc(stage_in[1], 16)
            for b in range(BATCHES):
                sp.wait_ge(v_rdy, b + 1)
                sp.dma_start(values_dram[b], v_sb[:, b % 2, :]).then_inc(v_out[b % 2], 16)
            sp.wait_ge(kT_sb, 4)
            for n in range(2):
                sp.wait_ge(v_out[n], 16 * BATCHES // 2)
            sp.wait_ge(cleared, 2)

            def diagonals(i, b):
                for h in range(HG):
                    rows = slice(h * HEAD_DIM, (h + 1) * HEAD_DIM)
                    sp.dma_start(k_diag[rows, b, :, h * KEYS:(h + 1) * KEYS],
                                 kT[rows, :, bass.ds((2 * i + b) * KEYS, KEYS)]).then_inc(k_in[b], 16)
                for h, k0, k1, c, p0 in PIECES:
                    cols = slice(h * HEAD_DIM, (h + 1) * HEAD_DIM)
                    src = values_dram[bass.ds(2 * i + b, 1), k0:k1, :].rearrange("o k (g f) -> k (o g) f", g=GROUPS)
                    sp.dma_start(v_diag[p0:p0 + k1 - k0, b, :, c, cols], src[:, :, cols]).then_inc(v_in[b], 16)

            for b in range(2):
                diagonals(0, b)
            for n, (m, at) in enumerate(((w1, 0), (w2, 0))):
                sp.wait_ge(w_lo, n + 1)
                if n == 0:
                    sp.dma_start(stage[:, 0, :].rearrange("p (k h) -> p k h", k=KC),
                                 w1[0].rearrange("(k p) h -> p k h", p=P)).then_inc(stage_in[0], 16)
                else:
                    sp.dma_start(stage[:, 1, :].rearrange("p (c d) -> p c d", c=HC),
                                 w2[0].rearrange("(c p) d -> p c d", p=P)).then_inc(stage_in[1], 16)
            x_out = tiled(part_dram)

            def keep_xn2(i):
                sp.wait_ge(xn2_ready, i + 1)
                sp.dma_start(xn2_all[:, bass.ds(i * TP, TP), 0:DIM], xn2[:, :, :]).then_inc(xn2_kept, 16)

            def store_part(j):
                sp.wait_ge(y_out, j + 1)
                sp.dma_start(x_out[:, bass.ds(j * TP, TP), :], x_all[:, bass.ds(j * TP, TP), :]).then_inc(part_out, 16)

            keep_xn2(0)
            with sp.Fori(1, PAIRS) as i:
                for b in range(2):
                    sp.wait_ge(s_ps, (2 * i + b - 1) * 8)
                    sp.wait_ge(o_ps, 2 * i + b - 1)
                    diagonals(i, b)
                store_part(i - 1)
                keep_xn2(i)
            sp.wait_ge(w_lo, 3)
            sp.dma_start(stage[:, 0, :].rearrange("p (k h) -> p k h", k=KC),
                         w1[1].rearrange("(k p) h -> p k h", p=P)).then_inc(stage_in[0], 16)
            sp.wait_ge(w_lo, 4)
            sp.dma_start(stage[:, 1, :].rearrange("p (c d) -> p c d", c=HC),
                         w2[1].rearrange("(c p) d -> p c d", p=P)).then_inc(stage_in[1], 16)
            store_part(PAIRS - 1)

            def load_sorted(j):
                rows = sorted_dram[bass.ds(j * RTOK, RTOK), :].rearrange("(t p) d -> p t d", p=P)
                sp.dma_start(xs[:, :, :], rows).then_inc(xs_in, 16)

            sp.wait_ge(scattered, 16 * TILES)
            load_sorted(0)
            sp.wait_ge(seam_rdy, 1)
            tiles_of_0 = sp.value_load(tiles0_int[0:1, 0:1], min_val=1, max_val=RTILES - 1)

            def routed(j):
                sp.wait_ge(xsT_ps, j + 1)
                sp.wait_ge(ids_copied, j + 1)
                load_sorted(j + 1)

            with sp.Fori(0, tiles_of_0) as j:
                routed(j)
            with sp.Fori(tiles_of_0, RTILES) as j:
                routed(j)
            sp.wait_ge(xs_in, 16 * (RTILES + 1))

        @block.gpsimd
        def _(pool):
            nc.gpsimd.memset(ident[:, :], 0.0).then_inc(iotas, 1)
            pool.wait_ge(iotas, 1)
            nc.gpsimd.affine_select(out=ident[:, :], in_=ident[:, :], compare_op=ALU.not_equal, fill=1.0, base=0,
                                    pattern=[[-1, P]], channel_multiplier=1).then_inc(consts_made, 1)
            nc.gpsimd.iota(xn2_all[:, :, DIM:ROW].rearrange("p t o -> p (t o)"), pattern=[[P, TILES]], base=0,
                           channel_multiplier=1, allow_small_or_imprecise_dtypes=True).then_inc(iotas, 1)
            nc.gpsimd.memset(k_diag[:, :, :, :], 0.0).then_inc(cleared, 1)
            nc.gpsimd.memset(v_diag[:, :, :, :, :], 0.0).then_inc(cleared, 1)
            for n, (raw, hi, lo) in enumerate((
                    (stage[:, 0, :], sw1_sb[0][:, :, :].rearrange("p k h -> p (k h)"), sw1_sb[1][:, :, :].rearrange("p k h -> p (k h)")),
                    (stage[:, 1, :], sw2_sb[0][:, :, :].rearrange("p k h -> p (k h)"), sw2_sb[1][:, :, :].rearrange("p k h -> p (k h)")))):
                pool.wait_ge(w_hi, n + 1)
                nc.gpsimd.tensor_tensor(lo, raw, hi, ALU.subtract).then_inc(w_lo, 1)

            def iteration(i, attention, ffn):
                for step, b, k in steps(attention, ffn):
                    if step == "in":
                        if isinstance(i, int) and i == 0 and b == 0:
                            pool.wait_ge(rows_ready, 1)
                        for t in range(TB):
                            pool.wait_ge(xn_ready, 2 * i + b + 1)
                            row = x_all[:, bass.ds((2 * i + b) * TB + t, 1), :].rearrange("p o d -> p (o d)")
                            nc.gpsimd.tensor_tensor(row, row, bias_rows[:, 0, :], ALU.add).then_inc(x_biased, 1)
                    if step == "scores":
                        pool.wait_ge(p_rinv, (2 * i + b) * 4 + k + 1)
                        pq = one_bank(probs[:, b, k, :])
                        nc.gpsimd.tensor_tensor(pq, pq, rinv[:, b, k, :].unsqueeze(2).to_broadcast([P, HG, KEYS]),
                                                ALU.mult).then_inc(p_ready, 1)
                    if step == "norm2":
                        pool.wait_ge(xn2_ready, i + 1)
                        for t in range(TP):
                            row = x_all[:, bass.ds(i * TP + t, 1), :].rearrange("p o d -> p (o d)")
                            nc.gpsimd.tensor_tensor(row, row, bias_rows[:, 1, :], ALU.add).then_inc(x1_biased, 1)

            iteration(0, True, False)
            with pool.Fori(1, PAIRS) as i:
                iteration(i, True, True)
            pool.wait_ge(x2T_ps, PAIRS * KC)
            pool.wait_ge(xn2_kept, 16 * PAIRS)
            nc.gpsimd.memset(ones[:, :], 1.0).then_inc(iotas, 1)
            nc.gpsimd.memset(before[:, :], 1.0).then_inc(iotas, 1)
            nc.gpsimd.memset(zero_tile[:, :], 0.0).then_inc(iotas, 1)
            nc.gpsimd.memset(part[:, :, :], 0.0).then_inc(iotas, 1)
            nc.gpsimd.memset(xs[:, :, :], 0.0).then_inc(iotas, 1)
            nc.gpsimd.iota(seams[:, :], pattern=[[RTOK, RTILES - 2]], base=RTOK, channel_multiplier=0,
                           allow_small_or_imprecise_dtypes=True).then_inc(iotas, 1)
            nc.gpsimd.iota(number[:, :], pattern=[[P, TILES]], base=0, channel_multiplier=1,
                           allow_small_or_imprecise_dtypes=True).then_inc(iotas, 1)
            pool.wait_ge(iotas, 9)
            nc.gpsimd.affine_select(out=before[:, :], in_=before[:, :], compare_op=ALU.is_gt, fill=0.0, base=0,
                                    pattern=[[1, P]], channel_multiplier=-1).then_inc(iotas, 1)
            nc.gpsimd.iota(xs[:, :, DIM:ROW].rearrange("p t o -> p (t o)"), pattern=[[P, RT]], base=NO_TOKEN,
                           channel_multiplier=1, allow_small_or_imprecise_dtypes=True).then_inc(iotas, 1)
            pool.wait_ge(iotas, 11)
            for j in range(RTILES + 1):
                rows = sorted_dram[j * RTOK:(j + 1) * RTOK, :].rearrange("(t p) d -> p t d", p=P)
                pool.dma_start(rows, xs[:, :, :]).then_inc(filled, 16)
            pool.wait_ge(filled, 16 * (RTILES + 1))
            pool.wait_ge(places_rdy, 1)
            for t in range(TILES):
                pool.indirect_dma_start(
                    out=sorted_dram[:, :], out_offset=bass.IndirectOffsetOnAxis(ap=place_int[:, t:t + 1], axis=0),
                    in_=xn2_all[:, t, :], in_offset=None, bounds_check=SLOTS - 1,
                    oob_is_err=False).then_inc(scattered, 16)
            pool.wait_ge(other_rdy, 1)
            pool.wait_ge(part_out, 16 * PAIRS)
            pool.wait_ge(seam_rdy, 1)
            tiles_of_0 = pool.value_load(tiles0_int[0:1, 0:1], min_val=1, max_val=RTILES - 1)

            last_token = pool.to_reg(TOKENS - 1)

            def routed(j, e):
                turn = pool.to_reg(j + 1)
                used = j
                pool.wait_ge(seam_rdy, 1)
                pool.wait_ge(ids_copied, turn)
                pool.wait_ge(final_rdy, used)
                for t in range(RT):
                    pool.indirect_dma_start(
                        out=part[:, t, :], out_offset=None, in_=part_dram[:, :],
                        in_offset=bass.IndirectOffsetOnAxis(ap=slot_token[:, t:t + 1], axis=0),
                        bounds_check=last_token, oob_is_err=False).then_inc(gathered, 16)
                pool.wait_ge(gathered, 32 * (j + 1))
                for t in range(RT):
                    nc.gpsimd.tensor_tensor(part[:, t, :], part[:, t, :], other_row[:, 1 - e, :], ALU.add
                                            ).then_inc(part_rdy, 1)
                pool.wait_ge(seam_rdy, 1)
                pool.wait_ge(final_rdy, turn)
                for t in range(RT):
                    pool.indirect_dma_start(
                        out=out[:, :], out_offset=bass.IndirectOffsetOnAxis(ap=slot_token[:, t:t + 1], axis=0),
                        in_=final[:, t, :], in_offset=None, bounds_check=last_token,
                        oob_is_err=False).then_inc(rows_out, 16)

            with pool.Fori(0, tiles_of_0) as j:
                routed(j, 0)
            with pool.Fori(tiles_of_0, RTILES) as j:
                routed(j, 1)
            pool.wait_ge(rows_out, 32 * RTILES)

        @block.scalar
        def _(act):
            act.wait_ge(small_in, SMALL)
            nc.scalar.activation(gains[:, :], gains[:, :], ACT.Tanh).then_inc(gains_ready, 1)
            act.wait_ge(vecs_ps, 1)
            nc.scalar.activation(vec_cols[:, :], h_ps[:, 0, 0:VECS], ACT.Copy).then_inc(vecs_rdy, 1)
            act.wait_ge(vecs_rdy, 1)
            for n in range(CKC * 2):
                act.wait_ge(yT_ps, n + 1)
                nc.scalar.activation(yT[:, n // 2, (n % 2) * YH:(n % 2 + 1) * YH], bank[n][0:CK, 0:YH],
                                     ACT.Copy).then_inc(yT_sb, 1)
            for n, (g, half) in enumerate((g, half) for g in range(GROUPS) for half in range(2)):
                act.wait_ge(kT_ps, n + 1)
                src = h_ps[:, half, 0:YH] if g == 0 else y_ps[:, 2 * half:2 * half + 2, :].rearrange("p a d -> p (a d)")[:, 0:YH]
                nc.scalar.activation(kT[:, g, half * YH:(half + 1) * YH], src, ACT.Identity,
                                     bias=bk_sb[:, g:g + 1]).then_inc(kT_sb, 1)
            act.wait_ge(var_ready, 1)
            nc.scalar.activation(nt[:, 0, :], mv[:, :, 1:2].rearrange("p t o -> p (t o)"), ACT.Ln,
                                 bias=eps_sb[:, :]).then_inc(rstd_guess, 1)
            act.wait_ge(rstd_guess, 1)
            nc.scalar.activation(rstd[:, :], nt[:, 0, :], ACT.Exp, scale=-0.5).then_inc(rstd_guess, 1)
            for n, hi in enumerate((sw1_sb[0], sw2_sb[0])):
                act.wait_ge(stage_in[n], 16)
                nc.scalar.activation(hi[:, :, :].rearrange("p k h -> p (k h)"), stage[:, n, :], ACT.Copy
                                     ).then_inc(w_hi, 1)

            def hidden(q, c, m, width, first):
                act.wait_ge(h_in_ps, q + 1)
                if not first:
                    act.wait_ge(y_used, q - 1)
                nc.scalar.activation(hT[0][:, c % 2, 0:width], h_ps[:, c % 2, 0:width], ACT.Relu,
                                     bias=b1_sb[:, m, c:c + 1]).then_inc(h_hi, 1)
                if not first:
                    act.wait_ge(h_lo, q - 1)
                nc.scalar.activation(h32[:, c % 2, 0:width], h_ps[:, c % 2, 0:width], ACT.Relu,
                                     bias=b1_sb[:, m, c:c + 1]).then_inc(h_32, 1)

            def iteration(i, attention, ffn):
                for step, b, k in steps(attention, ffn):
                    if step == "in":
                        act.wait_ge(xnT_ps, 2 * i + b + 1)
                        nc.scalar.activation(xnT[:, b, :, :].rearrange("p k s -> p (k s)"), bank[2][:, :], ACT.Copy
                                             ).then_inc(xnT_sb, 1)
                        act.wait_ge(q_ps, 2 * i + b + 1)
                        for g in range(GROUPS):
                            nc.scalar.activation(qT[:, b, g, :], bank[3][:, g * SEQ:(g + 1) * SEQ], ACT.Identity,
                                                 bias=bq_sb[:, g:g + 1]).then_inc(q_sb, 1)
                    if step == "scores":
                        act.wait_ge(s_shifted, ((2 * i + b) * 4 + k + 1) * 2)
                        nc.scalar.activation(probs[:, b, k, :], probs[:, b, k, :], ACT.Exp,
                                             scale=HEAD_DIM ** -0.5).then_inc(p_exp, 1)
                    if step == "out":
                        for u in range(CHUNKS):
                            act.wait_ge(pT_ps, (2 * i + b) * CHUNKS + u + 1)
                            if u == 0 and not (b == 0 and not ffn):
                                act.wait_ge(o_ps, 2 * i + b)
                            for v in range(2):
                                r = ROWS[(2 * u + v) % CHUNKS]
                                nc.scalar.activation(pT[0:r, 2 * u + v, :], bank[2 + u % 2][0:r, v * SEQ:(v + 1) * SEQ],
                                                     ACT.Copy).then_inc(pT_sb, 1)
                        act.wait_ge(o_ps, 2 * i + b + 1)
                        if not (b == 0 and not ffn):
                            act.wait_ge(proj_ps, 2 * i + b)
                        nc.scalar.activation(oT[:, :, :].rearrange("p g s -> p (g s)"), bank[3][:, :], ACT.Copy
                                             ).then_inc(o_sb, 1)
                    if step == "norm2":
                        act.wait_ge(var2_ready, i + 1)
                        nc.scalar.activation(nt2[:, 0, :], mv2[:, :, 1:2].rearrange("p t o -> p (t o)"), ACT.Ln,
                                             bias=eps_sb[:, :]).then_inc(guess2, 1)
                        act.wait_ge(guess2, 2 * i + 1)
                        nc.scalar.activation(rstd2[:, :], nt2[:, 0, :], ACT.Exp, scale=-0.5).then_inc(guess2, 1)
                        for kc in range(KC):
                            act.wait_ge(x2T_ps, KC * i + kc + 1)
                            if ffn and kc == 0:
                                act.wait_ge(h_in_ps, HC * i)
                            nc.scalar.activation(x2T[0][:, kc, :], bank[2 + kc][:, :], ACT.Copy).then_inc(x2T_hi, 1)
                        act.wait_ge(gate_ps, i + 1)
                        nc.scalar.activation(
                            gate_sb[:, bass.ds(i * TP, TP), :].rearrange("p t e -> p (t e)"),
                            bank[3][:, 0:TP * EXPERTS], ACT.Copy).then_inc(gate_rdy, 1)
                    if step == "ffn" and k < HC:
                        if isinstance(i, int):
                            hidden((i - 1) * HC + k, k, 0, PTOK, False)
                        else:
                            hidden_loop(i, k)

            def hidden_loop(i, k):
                q = (i - 1) * HC + k
                act.wait_ge(h_in_ps, q + 1)
                if k >= 2:
                    act.wait_ge(y_used, q - 1)
                    act.wait_ge(h_lo, q - 1)
                else:
                    act.wait_ge(y_used, (i - 1) * HC)
                    act.wait_ge(h_lo, (i - 1) * HC)
                nc.scalar.activation(hT[0][:, k % 2, :], h_ps[:, k % 2, :], ACT.Relu,
                                     bias=b1_sb[:, 0, k:k + 1]).then_inc(h_hi, 1)
                nc.scalar.activation(h32[:, k % 2, :], h_ps[:, k % 2, :], ACT.Relu,
                                     bias=b1_sb[:, 0, k:k + 1]).then_inc(h_32, 1)

            iteration(0, True, False)
            with act.Fori(1, PAIRS) as i:
                iteration(i, True, True)

            act.wait_ge(x2T_ps, PAIRS * KC)
            act.wait_ge(xn2_kept, 16 * PAIRS)

            def expert_hi(e, n):
                act.wait_ge(stage_in[n], 16 * (2 + e))
                hi = (ew1_sb[0][:, e, :, :], ew2_sb[0][:, e, :, :])[n].rearrange("p k h -> p (k h)")
                nc.scalar.activation(hi, stage[:, n, :], ACT.Copy).then_inc(w_hi, 1)

            for step, b, k in steps(False, True):
                if k < HC:
                    hidden((PAIRS - 1) * HC + k, k, 0, PTOK, False)
                if k in (0, 1):
                    expert_hi(0, k)
                if k in (4, 6):
                    expert_hi(1, (k - 4) // 2)
            act.wait_ge(other_ps, EXPERTS)
            nc.scalar.activation(other_row[:, :, :].rearrange("p e d -> p (e d)"), bank[3][:, :], ACT.Copy,
                                 scale=gains[:, 1:2]).then_inc(other_rdy, 1)

            def sorted_hi(j):
                act.wait_ge(xsT_ps, j + 1)
                nc.scalar.activation(xsT[0][:, bass.ds(j % 2, 1), :, :].rearrange("p o k s -> p (o k s)"), bank[2][:, :], ACT.Copy
                                     ).then_inc(xsT_hi, 1)

            sorted_hi(0)
            act.wait_ge(seam_rdy, 1)
            tiles_of_0 = act.value_load(tiles0_int[0:1, 0:1], min_val=1, max_val=RTILES - 1)

            def routed(j, e):
                for c in range(HC):
                    hidden(PAIRS * HC + j * HC + c, c, 1 + e, RTOK, False)
                    if c == 5:
                        sorted_hi(j + 1)

            with act.Fori(0, tiles_of_0) as j:
                routed(j, 0)
            with act.Fori(tiles_of_0, RTILES) as j:
                routed(j, 1)

        @block.vector
        def _(dve):
            chain = [0]

            def link(ins):
                chain[0] += 1
                ins.then_inc(dve_chain, 1)
                dve.wait_ge(dve_chain, chain[0])

            nc.vector.memset(eps_sb[:, :], EPS)
            dve.wait_ge(x_in, 16)
            for t in range(TILES):
                ins = nc.vector.bn_stats(stats[:, t, :], x_all[:, t, :])
            link(ins)
            for t in range(TILES):
                ins = nc.vector.bn_aggr(mv[:, t, :], stats[:, t, :])
            ins.then_inc(var_ready, 1)
            dve.wait_ge(small_in, SMALL)
            for b in range(BATCHES):
                dve.wait_ge(v_ps, b + 1)
                if b >= 2:
                    dve.wait_ge(v_out[b % 2], 16 * (b // 2))
                nc.vector.tensor_tensor(v_sb[:, b % 2, :], bank[b % 2][0:KEYS, 0:DIM], bv_row[:, :], ALU.add
                                        ).then_inc(v_rdy, 1)
            dve.wait_ge(gains_ready, 1)
            nc.vector.tensor_scalar(bias_rows[:, 0, :], bias_rows[:, 0, :], gains[:, 0:1], None, ALU.mult)
            link(nc.vector.tensor_tensor(bias_rows[:, 1, :], bias_rows[:, 1, :], h32[:, 0, 0:DIM], ALU.add))
            link(nc.vector.tensor_tensor(bias_rows[:, 1, :], bias_rows[:, 1, :], h32[:, 0, DIM:2 * DIM], ALU.add))
            nc.vector.tensor_scalar(bias_rows[:, 1, :], bias_rows[:, 1, :], gains[:, 1:2], None, ALU.mult
                                    ).then_inc(rows_ready, 1)
            dve.wait_ge(vecs_rdy, 1)
            link(nc.vector.tensor_copy(gw[0][:, :, :], gw32))
            nc.vector.tensor_tensor(gw[1][:, :, :], gw32, gw[0][:, :, :], ALU.subtract).then_inc(gw_cut, 1)
            dve.wait_ge(rstd_guess, 2)
            var = mv[:, :, 1:2].rearrange("p t o -> p (t o)")
            link(nc.vector.scalar_tensor_tensor(out=nt[:, 0, :], in0=var, scalar=EPS, in1=rstd[:, :],
                                                op0=ALU.add, op1=ALU.mult))
            link(nc.vector.scalar_tensor_tensor(out=nt[:, 1, :], in0=nt[:, 0, :], scalar=-0.5, in1=rstd[:, :],
                                                op0=ALU.mult, op1=ALU.mult))
            link(nc.vector.scalar_tensor_tensor(out=rstd[:, :], in0=nt[:, 1, :], scalar=1.5, in1=rstd[:, :],
                                                op0=ALU.add, op1=ALU.mult))
            links = chain[0]

            def sums(i, b, k):
                dve.wait_ge(p_exp, (2 * i + b) * 4 + k + 1)
                nc.vector.tensor_reduce(out=rsum[:, b, k, :], in_=one_bank(probs[:, b, k, :]), axis=AX_X, op=ALU.add
                                        ).then_inc(p_sum, 1)
                dve.wait_ge(p_sum, (2 * i + b) * 4 + k + 1)
                nc.vector.reciprocal(rinv[:, b, k, :], rsum[:, b, k, :]).then_inc(p_rinv, 1)

            def iteration(i, attention, ffn):
                NORM2_LINKS = 4
                for step, b, k in steps(attention, ffn):
                    if step == "in":
                        for t in range(TB):
                            row = x_all[:, bass.ds((2 * i + b) * TB + t, 1), :].rearrange("p o d -> p (o d)")
                            ins = nc.vector.tensor_scalar(
                                xn[:, b, t, :], row,
                                mv[:, bass.ds((2 * i + b) * TB + t, 1), 0:1].rearrange("p t o -> p (t o)"),
                                rstd[:, bass.ds((2 * i + b) * TB + t, 1)], ALU.subtract, ALU.mult)
                        ins.then_inc(xn_ready, 1)
                    if step == "scores":
                        quarter = (2 * i + b) * 4 + k
                        for half in range(2):
                            dve.wait_ge(s_ps, quarter * 2 + half + 1)
                            nc.vector.tensor_reduce(
                                out=smax[:, b, k, half * HH:(half + 1) * HH], in_=one_bank(bank[half][:, 0:HALF]),
                                axis=AX_X, op=ALU.max).then_inc(s_max, 1)
                        if ffn:
                            dve.wait_ge(pT_ps, (2 * i + b - 1) * CHUNKS)
                        for half in range(2):
                            dve.wait_ge(s_max, quarter * 2 + half + 1)
                            m = smax[:, b, k, half * HH:(half + 1) * HH].unsqueeze(2).to_broadcast([P, HH, KEYS])
                            nc.vector.tensor_tensor(one_bank(probs[:, b, k, half * HALF:(half + 1) * HALF]),
                                                    one_bank(bank[half][:, 0:HALF]), m, ALU.subtract
                                                    ).then_inc(s_shifted, 1)
                        if k >= 1:
                            sums(i, b, k - 1)
                        if k == 3:
                            sums(i, b, k)
                    if step == "out":
                        dve.wait_ge(proj_ps, 2 * i + b + 1)
                        dve.wait_ge(x_biased, TB * (2 * i + b + 1))
                        rows = x_all[:, bass.ds((2 * i + b) * TB, TB), :].rearrange("p t d -> p (t d)")
                        nc.vector.scalar_tensor_tensor(out=rows, in0=bank[2][:, :], scalar=gains[:, 0:1], in1=rows,
                                                       op0=ALU.mult, op1=ALU.add).then_inc(x1_ready, 1)
                        dve.wait_ge(gains_ready, 1)
                        dve.wait_ge(x1_ready, 2 * i + b + 1)
                        for t in range(TB):
                            row = x_all[:, bass.ds((2 * i + b) * TB + t, 1), :].rearrange("p o d -> p (o d)")
                            ins = nc.vector.bn_stats(stats2[:, b * TB + t, :], row)
                        ins.then_inc(dve_chain, 1)
                    if step == "norm2":
                        dve.wait_ge(dve_chain, links + 5 * i + 2)
                        nc.vector.memset(fill[:, :], 0.0)
                        for t in range(TP):
                            ins = nc.vector.bn_aggr(mv2[:, t, :], stats2[:, t, :])
                        ins.then_inc(var2_ready, 1)
                        dve.wait_ge(guess2, 2 * i + 2)
                        var = mv2[:, :, 1:2].rearrange("p t o -> p (t o)")
                        nc.vector.scalar_tensor_tensor(out=nt2[:, 0, :], in0=var, scalar=EPS, in1=rstd2[:, :],
                                                       op0=ALU.add, op1=ALU.mult).then_inc(dve_chain, 1)
                        dve.wait_ge(dve_chain, links + 5 * i + 3)
                        nc.vector.scalar_tensor_tensor(out=nt2[:, 1, :], in0=nt2[:, 0, :], scalar=-0.5,
                                                       in1=rstd2[:, :], op0=ALU.mult, op1=ALU.mult
                                                       ).then_inc(dve_chain, 1)
                        dve.wait_ge(dve_chain, links + 5 * i + 4)
                        nc.vector.scalar_tensor_tensor(out=rstd2[:, :], in0=nt2[:, 1, :], scalar=1.5,
                                                       in1=rstd2[:, :], op0=ALU.add, op1=ALU.mult
                                                       ).then_inc(dve_chain, 1)
                        dve.wait_ge(dve_chain, links + 5 * i + 5)
                        if ffn:
                            dve.wait_ge(xn2_kept, 16 * i)
                        for t in range(TP):
                            row = x_all[:, bass.ds(i * TP + t, 1), :].rearrange("p o d -> p (o d)")
                            ins = nc.vector.tensor_scalar(xn2[:, t, :], row, mv2[:, t, 0:1], rstd2[:, t:t + 1],
                                                          ALU.subtract, ALU.mult)
                        ins.then_inc(xn2_ready, 1)
                        for kc in range(KC):
                            dve.wait_ge(x2T_hi, KC * i + kc + 1)
                            nc.vector.tensor_tensor(x2T[1][:, kc, :], bank[2 + kc][:, :], x2T[0][:, kc, :],
                                                    ALU.subtract).then_inc(x2T_lo, 1)
                    if step == "ffn":
                        ffn_step(i - 1, k)

            def hidden_lo(q, c, width):
                dve.wait_ge(h_32, q + 1)
                nc.vector.tensor_tensor(hT[1][:, c % 2, 0:width], h32[:, c % 2, 0:width], hT[0][:, c % 2, 0:width],
                                        ALU.subtract).then_inc(h_lo, 1)

            def ffn_step(j, k):
                if k < HC:
                    hidden_lo(j * HC + k, k, PTOK)
                else:
                    dve.wait_ge(y_used, (j + 1) * HC)
                    dve.wait_ge(x1_biased, TP * (j + 1))
                    for h in range(2):
                        rows = x_all[:, bass.ds(j * TP + h * TB, TB), :].rearrange("p t d -> p (t d)")
                        ins = nc.vector.scalar_tensor_tensor(
                            out=rows, in0=y_ps[:, h * TB:(h + 1) * TB, :].rearrange("p t d -> p (t d)"),
                            scalar=gains[:, 1:2], in1=rows, op0=ALU.mult, op1=ALU.add)
                    ins.then_inc(y_out, 1)

            iteration(0, True, False)
            with dve.Fori(1, PAIRS) as i:
                iteration(i, True, True)
            chain[0] = links + 5 * PAIRS

            dve.wait_ge(gate_rdy, PAIRS)
            dve.wait_ge(iotas, 11)
            nc.vector.tensor_tensor(chosen[:, :], gate_sb[:, :, 1:2].rearrange("p t o -> p (t o)"),
                                    gate_sb[:, :, 0:1].rearrange("p t o -> p (t o)"), ALU.is_gt
                                    ).then_inc(chosen_rdy, 1)
            link(nc.vector.tensor_scalar(relu_b1[:, :, :], b1_sb[:, 1:1 + EXPERTS, :], 0.0, None, ALU.max))
            link(nc.vector.tensor_copy(relu_b1p[0][:, :, :], relu_b1[:, :, :]))
            nc.vector.tensor_tensor(relu_b1p[1][:, :, :], relu_b1[:, :, :], relu_b1p[0][:, :, :], ALU.subtract
                                    ).then_inc(rb_cut, 1)
            dve.wait_ge(counts_ps, 1)
            nc.vector.tensor_copy(rank1[:, :], bank[3][:, 64:64 + TILES])
            link(nc.vector.tensor_copy(tile_sum[:, :], bank[3][:, 128:128 + TILES]))
            link(nc.vector.tensor_tensor_scan(prefix[:, :], tile_sum[:, :], zero_tile[:, :], 0.0, ALU.add, ALU.add))
            link(nc.vector.tensor_tensor(rank1[:, 1:TILES], rank1[:, 1:TILES], prefix[:, 0:TILES - 1], ALU.add))
            link(nc.vector.tensor_tensor(rank0[:, :], number[:, :], rank1[:, :], ALU.subtract))
            link(nc.vector.tensor_scalar(count0[:, :], prefix[:, TILES - 1:TILES], -1.0, float(TOKENS),
                                         ALU.mult, ALU.add))
            link(nc.vector.tensor_scalar(past[:, :], seams[:, :], count0[:, :], None, ALU.is_lt))
            link(nc.vector.tensor_reduce(out=tiles0[:, :], in_=past[:, :], axis=AX_X, op=ALU.add))
            link(nc.vector.tensor_scalar(tiles0[:, :], tiles0[:, :], 1.0, None, ALU.add))
            nc.vector.tensor_copy(tiles0_int[:, :], tiles0[:, :]).then_inc(seam_rdy, 1)
            link(nc.vector.tensor_scalar(base1[:, :], tiles0[:, :], float(RTOK), None, ALU.mult))
            link(nc.vector.scalar_tensor_tensor(out=moved[:, :], in0=rank1[:, :], scalar=base1[:, :],
                                                in1=rank0[:, :], op0=ALU.add, op1=ALU.subtract))
            link(nc.vector.tensor_tensor(moved[:, :], moved[:, :], chosen[:, :], ALU.mult))
            link(nc.vector.tensor_tensor(place[:, :], rank0[:, :], moved[:, :], ALU.add))
            nc.vector.tensor_copy(place_int[:, :], place[:, :]).then_inc(places_rdy, 1)

            def expert_lo(e, n):
                dve.wait_ge(w_hi, 3 + 2 * e + n)
                hi, lo = ((ew1_sb[m][:, e, :, :], ew2_sb[m][:, e, :, :])[n].rearrange("p k h -> p (k h)")
                          for m in range(2))
                nc.vector.tensor_tensor(lo, stage[:, n, :], hi, ALU.subtract).then_inc(w_lo, 1)

            for step, b, k in steps(False, True):
                ffn_step(PAIRS - 1, k)
                if k in (0, 1):
                    expert_lo(0, k)
                if k in (4, 6):
                    expert_lo(1, (k - 4) // 2)
            def sorted_lo(j):
                dve.wait_ge(xsT_hi, j + 1)
                nc.vector.tensor_tensor(xsT[1][:, bass.ds(j % 2, 1), :, :].rearrange("p o k s -> p (o k s)"),
                                        bank[2][:, :],
                                        xsT[0][:, bass.ds(j % 2, 1), :, :].rearrange("p o k s -> p (o k s)"),
                                        ALU.subtract).then_inc(xsT_lo, 1)

            sorted_lo(0)
            tiles_of_0 = dve.value_load(tiles0_int[0:1, 0:1], min_val=1, max_val=RTILES - 1)

            def routed(j, e):
                for c in range(HC):
                    hidden_lo(PAIRS * HC + j * HC + c, c, RTOK)
                    if c == 2:
                        dve.wait_ge(xs_in, 16 * (j + 1))
                        dve.wait_ge(rows_out, 32 * j)
                        nc.vector.tensor_copy(slot_token[:, :], xs[:, :, DIM:ROW].rearrange("p t o -> p (t o)")
                                              ).then_inc(ids_copied, 1)
                    if c == 5:
                        sorted_lo(j + 1)
                dve.wait_ge(y_used, PAIRS * HC + (j + 1) * HC)
                dve.wait_ge(part_rdy, RT * (j + 1))
                dve.wait_ge(rows_out, 32 * j)
                nc.vector.scalar_tensor_tensor(
                    out=final[:, :, :].rearrange("p t d -> p (t d)"),
                    in0=y_ps[:, 0:RT, :].rearrange("p t d -> p (t d)"), scalar=gains[:, 1:2],
                    in1=part[:, :, :].rearrange("p t d -> p (t d)"), op0=ALU.mult, op1=ALU.add
                ).then_inc(final_rdy, 1)

            with dve.Fori(0, tiles_of_0) as j:
                routed(j, 0)
            with dve.Fori(tiles_of_0, RTILES) as j:
                routed(j, 1)

        @block.tensor
        def _(pe):
            def mm(out_, lhsT, rhs, start, stop, **kw):
                return nc.tensor.matmul(out_, lhsT, rhs, start=start, stop=stop, **kw)

            def cut(out_, lhs, rhs, start, stop, **kw):
                for n, (a, b) in enumerate(((0, 0), (1, 0), (0, 1))):
                    ins = mm(out_, lhs(a), rhs(b), start and n == 0, stop and n == 2, **kw)
                return ins

            pe.wait_ge(consts_made, 1)
            pe.wait_ge(vecs_in, 16 * 5)
            nc.tensor.transpose(h_ps[:, 0, 0:VECS], vec_rows[:, :], ident[0:VECS, 0:VECS]).then_inc(vecs_ps, 1)
            pe.wait_ge(vecs_rdy, 1)
            pe.wait_ge(context_in, 48)
            for n in range(CKC * 2):
                for q in range(4):
                    ins = nc.tensor.transpose(bank[n][0:CK, q * KEYS:(q + 1) * KEYS],
                                              y_sb[:, (n % 2) * 4 + q, (n // 2) * CK:(n // 2 + 1) * CK],
                                              ident[0:KEYS, 0:KEYS])
                ins.then_inc(yT_ps, 1)
            pe.wait_ge(yT_sb, CKC * 2)
            for g in range(GROUPS):
                for half in range(2):
                    dst = h_ps[:, half, 0:YH] if g == 0 else y_ps[:, 2 * half:2 * half + 2, :].rearrange("p a d -> p (a d)")[:, 0:YH]
                    for k in range(CKC):
                        ins = mm(dst, wk_sb[:, k, g * P:(g + 1) * P], yT[:, k, half * YH:(half + 1) * YH],
                                 k == 0, k == CKC - 1)
                    ins.then_inc(kT_ps, 1)
            for b in range(BATCHES):
                if b >= 2:
                    pe.wait_ge(v_rdy, b - 1)
                for k in range(CKC):
                    ins = mm(bank[b % 2][0:KEYS, 0:DIM], yT[:, k, b * KEYS:(b + 1) * KEYS], wv_sb[:, k, :],
                             k == 0, k == CKC - 1)
                ins.then_inc(v_ps, 1)
            pe.wait_ge(v_rdy, BATCHES)
            pe.wait_ge(kT_sb, 4)
            pe.wait_ge(small_in, SMALL)

            def iteration(i, attention, ffn):
                for step, b, k in steps(attention, ffn):
                    if step == "in":
                        pe.wait_ge(xn_ready, 2 * i + b + 1)
                        if b == 1:
                            pe.wait_ge(xnT_sb, 2 * i + 1)
                        elif ffn:
                            pe.wait_ge(x2T_lo, KC * i)
                        for kc in range(KC):
                            for t in range(TB):
                                ins = nc.tensor.transpose(bank[2][:, kc * SEQ + t * P:kc * SEQ + (t + 1) * P],
                                                          xn[:, b, t, kc * P:(kc + 1) * P], ident[:, :])
                        ins.then_inc(xnT_ps, 1)
                        pe.wait_ge(xnT_sb, 2 * i + b + 1)
                        if b == 1:
                            pe.wait_ge(q_sb, GROUPS * (2 * i + 1))
                        elif ffn:
                            pe.wait_ge(gate_rdy, i)
                        for g in range(GROUPS):
                            for kc in range(KC):
                                ins = mm(bank[3][:, g * SEQ:(g + 1) * SEQ], wq_sb[:, kc, g * P:(g + 1) * P],
                                         xnT[:, b, kc, :], kc == 0, kc == KC - 1)
                        ins.then_inc(q_ps, 1)
                    if step == "scores":
                        t, g = k % TB, k // TB
                        quarter = (2 * i + b) * 4 + k
                        if k == 0:
                            pe.wait_ge(q_sb, GROUPS * (2 * i + b + 1))
                            pe.wait_ge(k_in[b], 16 * HG * (i + 1))
                        for half in range(2):
                            if ffn or (b, k) != (0, 0):
                                pe.wait_ge(s_shifted, quarter * 2 - 1 + half)
                            mm(bank[half][:, 0:HALF], qT[:, b, g, t * P:(t + 1) * P],
                               k_diag[:, b, g, half * HALF:(half + 1) * HALF], True, True).then_inc(s_ps, 1)
                    if step == "out":
                        for u in range(CHUNKS):
                            if u == 0:
                                pe.wait_ge(p_ready, (2 * i + b) * 4 + 2)
                            if u == 2:
                                pe.wait_ge(p_ready, (2 * i + b) * 4 + 4)
                            if u >= 2:
                                pe.wait_ge(pT_sb, 2 * ((2 * i + b) * CHUNKS + u - 1))
                            elif b == 0:
                                pe.wait_ge(q_sb, GROUPS * (2 * i + 2))
                                pe.wait_ge(xnT_sb, 2 * i + 2)
                            elif u == 0:
                                pe.wait_ge(x1_ready, 2 * i + 1)
                            else:
                                pe.wait_ge(o_sb, 2 * i + 1)
                            for v in range(2):
                                ch = 2 * u + v
                                g, c = ch // CHUNKS, ch % CHUNKS
                                for t in range(TB):
                                    ins = nc.tensor.transpose(
                                        bank[2 + u % 2][0:ROWS[c], v * SEQ + t * P:v * SEQ + (t + 1) * P],
                                        probs[:, b, g * TB + t, c * P:c * P + ROWS[c]], ident[:, :])
                            ins.then_inc(pT_ps, 1)
                        pe.wait_ge(v_in[b], 16 * len(PIECES) * (i + 1))
                        pe.wait_ge(pT_sb, 2 * CHUNKS * (2 * i + b + 1))
                        for g in range(GROUPS):
                            for c in range(CHUNKS):
                                ins = mm(bank[3][:, g * SEQ:(g + 1) * SEQ], v_diag[0:ROWS[c], b, g, c, :],
                                         pT[0:ROWS[c], g * CHUNKS + c, :], c == 0, c == CHUNKS - 1)
                        ins.then_inc(o_ps, 1)
                        pe.wait_ge(o_sb, 2 * i + b + 1)
                        for t in range(TB):
                            for kc in range(KC):
                                ins = mm(bank[2][:, t * DIM:(t + 1) * DIM], oT[:, kc, t * P:(t + 1) * P],
                                         wo_sb[:, kc, :], kc == 0, kc == KC - 1)
                        ins.then_inc(proj_ps, 1)
                    if step == "norm2":
                        pe.wait_ge(xn2_ready, i + 1)
                        pe.wait_ge(x1_ready, 2 * i + 2)
                        pe.wait_ge(o_sb, 2 * i + 2)
                        for kc in range(KC):
                            for t in range(TP):
                                ins = nc.tensor.transpose(bank[2 + kc][:, t * P:(t + 1) * P],
                                                          xn2[:, t, kc * P:(kc + 1) * P], ident[:, :])
                            ins.then_inc(x2T_ps, 1)
                        pe.wait_ge(x2T_lo, KC * (i + 1))
                        pe.wait_ge(gw_cut, 1)
                        for t in range(TP):
                            for kc in range(KC):
                                ins = cut(bank[3][:, t * EXPERTS:(t + 1) * EXPERTS],
                                          lambda m: x2T[m][:, kc, t * P:(t + 1) * P], lambda m: gw[m][:, :, kc],
                                          kc == 0, kc == KC - 1)
                        ins.then_inc(gate_ps, 1)
                    if step == "ffn":
                        ffn_step(i - 1, k)

            def ffn_step(j, k):
                if k < HC:
                    if k == 0:
                        pe.wait_ge(w_lo, 2)
                        pe.wait_ge(x2T_lo, KC * (j + 1))
                    if k >= 2:
                        pe.wait_ge(h_32, j * HC + k - 1)
                    else:
                        pe.wait_ge(h_32, j * HC)
                    for kc in range(KC):
                        ins = cut(h_ps[:, k % 2, :], lambda m: sw1_sb[m][:, kc, k * P:(k + 1) * P],
                                  lambda m: x2T[m][:, kc, :], kc == 0, kc == KC - 1)
                    ins.then_inc(h_in_ps, 1)
                if k >= 1:
                    c = k - 1
                    pe.wait_ge(h_lo, j * HC + k)
                    if c == 0:
                        pe.wait_ge(y_out, j)
                    for t in range(TP):
                        ins = cut(y_ps[:, t, :], lambda m: hT[m][:, c % 2, t * P:(t + 1) * P],
                                  lambda m: sw2_sb[m][:, c, :], c == 0 and t % 2 == 0, c == HC - 1,
                                  skip_group_check=True)
                    ins.then_inc(y_used, 1)

            iteration(0, True, False)
            with pe.Fori(1, PAIRS) as i:
                iteration(i, True, True)

            for step, b, k in steps(False, True):
                ffn_step(PAIRS - 1, k)
                if k == 0:
                    pe.wait_ge(chosen_rdy, 1)
                    pe.wait_ge(iotas, 11)
                    pe.wait_ge(gate_rdy, PAIRS)
                    mm(bank[3][:, 64:64 + TILES], before[:, :], chosen[:, :], True, True)
                    mm(bank[3][:, 128:128 + TILES], ones[:, :], chosen[:, :], True, True).then_inc(counts_ps, 1)
            pe.wait_ge(rb_cut, 1)
            pe.wait_ge(places_rdy, 1)
            for e in range(EXPERTS):
                pe.wait_ge(w_lo, 4 + 2 * e)
                for c in range(HC):
                    ins = cut(bank[3][:, e * DIM:(e + 1) * DIM],
                              lambda m: relu_b1p[m][:, e, c:c + 1].to_broadcast([P, P]),
                              lambda m: ew2_sb[m][:, e, c, :], c == 0, c == HC - 1)
                ins.then_inc(other_ps, 1)

            def sorted_transposed(j):
                pe.wait_ge(xs_in, 16 * (j + 1))
                pe.wait_ge(xsT_lo, j)
                for kc in range(KC):
                    for t in range(RT):
                        ins = nc.tensor.transpose(bank[2][:, kc * RTOK + t * P:kc * RTOK + (t + 1) * P],
                                                  xs[:, t, kc * P:(kc + 1) * P], ident[:, :])
                ins.then_inc(xsT_ps, 1)

            pe.wait_ge(y_out, PAIRS)
            sorted_transposed(0)
            pe.wait_ge(seam_rdy, 1)
            tiles_of_0 = pe.value_load(tiles0_int[0:1, 0:1], min_val=1, max_val=RTILES - 1)

            def routed(j, e):
                q = PAIRS * HC + j * HC
                pe.wait_ge(xsT_lo, j + 1)
                for k in range(HC + 1):
                    if k < HC:
                        pe.wait_ge(h_32, q + k - 1)
                        for kc in range(KC):
                            ins = cut(h_ps[:, k % 2, 0:RTOK], lambda m: ew1_sb[m][:, e, kc, k * P:(k + 1) * P],
                                      lambda m: xsT[m][:, bass.ds(j % 2, 1), kc, :].rearrange("p o s -> p (o s)"),
                                      kc == 0, kc == KC - 1)
                        ins.then_inc(h_in_ps, 1)
                    if k == 5:
                        sorted_transposed(j + 1)
                    if k >= 1:
                        c = k - 1
                        pe.wait_ge(h_lo, q + k)
                        if c == 0:
                            pe.wait_ge(final_rdy, j)
                        for t in range(RT):
                            ins = cut(y_ps[:, t, :], lambda m: hT[m][:, c % 2, t * P:(t + 1) * P],
                                      lambda m: ew2_sb[m][:, e, c, :], c == 0 and t == 0, c == HC - 1,
                                      skip_group_check=True)
                        ins.then_inc(y_used, 1)

            with pe.Fori(0, tiles_of_0) as j:
                routed(j, 0)
            with pe.Fori(tiles_of_0, RTILES) as j:
                routed(j, 1)


_INS = ["x", "ctx_768", "g_xattn", "g_ffn", "L0_xattn_wq", "L0_xattn_bq", "L0_xattn_wk", "L0_xattn_bk",
        "L0_xattn_wv", "L0_xattn_bv", "L0_xattn_wo", "L0_xattn_bo", "L0_ffn_gate_w", "L0_ffn_w1", "L0_ffn_b1",
        "L0_ffn_w2", "L0_ffn_b2", "L0_ffn_sw1", "L0_ffn_sb1", "L0_ffn_sw2", "L0_ffn_sb2"]


def kernel(**inputs):
    import numpy as np
    from concourse import bacc
    from concourse.bass_utils import run_bass_kernel_spmd

    nc = bacc.Bacc("TRN2", target_bir_lowering=False, num_devices=1)
    arrays, args = {}, []
    for name in _INS:
        a = np.ascontiguousarray(inputs[name])
        arrays[f"in_{name}"] = a
        args.append(nc.dram_tensor(f"in_{name}", a.shape, mybir.dt.from_np(a.dtype), kind="ExternalInput").ap())
    out = nc.dram_tensor("out", (TOKENS, DIM), F32, kind="ExternalOutput").ap()
    build(nc, *args, out)
    r = run_bass_kernel_spmd(nc, [arrays], core_ids=[0])
    return r.results[0]["out"].reshape(BATCHES, SEQ, DIM)
```

```python
from contextlib import ExitStack

import concourse.bass as bass
from concourse import mybir

F32 = mybir.dt.float32
F32R = mybir.dt.float32r
I32 = mybir.dt.int32
U32 = mybir.dt.uint32
ALU = mybir.AluOpType
ACT = mybir.ActivationFunctionType
AX_X = mybir.AxisListType.X

P = 128
BATCHES, SEQ, DIM = 8, 256, 256
KEYS, CROSS = 77, 192
HEADS = 16
HEAD_DIM = DIM // HEADS
HIDDEN = 1024
EXPERTS = 2
EPS = 1e-5
ROOT_MAGIC = 0x5F3759DF
NEWTON = 3
ROOT_OPS = 3 + 3 * NEWTON
TOKENS = BATCHES * SEQ
TILES = TOKENS // P
TB = SEQ // P
KC = DIM // P
GROUPS = KC
HG = HEADS // GROUPS
GK = HG * KEYS
HALF = GK // 2
HH = HG // 2
CHUNKS = -(-GK // P)
TURNS = [(0, 1), (2, 3), (4,)]
ROWS = [min(P, GK - c * P) for c in range(CHUNKS)]
PAIRS = BATCHES // 2
TP = 2 * TB
PTOK = TP * P
CK = 96
CKC = CROSS // CK
HC = HIDDEN // P
HB = 4
YH = 4 * KEYS
RT = 2
RTOK = RT * P
RTILES = TOKENS // RTOK + 1
SLOTS = RTILES * RTOK
ROW = DIM + 1
V_B1 = 2 * GROUPS
V_GATE = V_B1 + (1 + EXPERTS) * HC
VECS = V_GATE + EXPERTS * KC
NO_TOKEN = 1 << 14

FIRST = [("scores", 0, 0, 0), ("in", 0, 1, 0), ("scores", 0, 0, 1), ("query", 0, 1, 0), ("scores", 0, 0, 2),
         ("turn", 0, 0, 0), ("scores", 0, 0, 3), ("sums", 0, 0, 3), ("turn", 0, 0, 1), ("turn", 0, 0, 2)]
ORDER = [("scores", 0, 1, 0), ("values", 0, 0, 0), ("norm2", -1, 0, 0), ("norm", 1, 0, 0), ("scores", 0, 1, 1),
         ("out", 0, 0, 0), ("gate", -1, 0, 0), ("h", -1, 0, 0), ("gate_turn", -1, 0, 0), ("h", -1, 0, 1),
         ("scores", 0, 1, 2), ("h", -1, 0, 2), ("y", -1, 0, 0), ("in", 1, 0, 0), ("scores", 0, 1, 3),
         ("query", 1, 0, 0), ("sums", 0, 1, 3), ("h", -1, 0, 3), ("y", -1, 0, 1), ("scores", 1, 0, 0),
         ("turn", 0, 1, 0), ("h", -1, 0, 4), ("turn", 0, 1, 1), ("y", -1, 0, 2), ("turn", 0, 1, 2),
         ("scores", 1, 0, 1), ("norm", 1, 1, 0), ("values", 0, 1, 0), ("h", -1, 0, 5), ("out", 0, 1, 0),
         ("scores", 1, 0, 2), ("y", -1, 0, 3), ("in", 1, 1, 0), ("h", -1, 0, 6), ("scores", 1, 0, 3),
         ("query", 1, 1, 0), ("y", -1, 0, 4), ("h", -1, 0, 7), ("sums", 1, 0, 3), ("root", 0, 0, 0),
         ("turn", 1, 0, 0), ("y", -1, 0, 5), ("turn", 1, 0, 1), ("y", -1, 0, 6), ("turn", 1, 0, 2), ("y", -1, 0, 7)]
LAST = [("norm2", 0, 0, 0), ("gate", 0, 0, 0), ("h", 0, 0, 0), ("gate_turn", 0, 0, 0), ("h", 0, 0, 1)] + [
    (what, 0, 0, k) for n in range(2, HC) for what, k in (("h", n), ("y", n - 2))] + [
    ("y", 0, 0, HC - 2), ("y", 0, 0, HC - 1)]
CUT_AFTER = {1: (0, 0), 2: (0, 1), 4: (1, 0), 6: (1, 1)}


def value_pieces():
    for h in range(HG):
        k = 0
        while k < KEYS:
            row = h * KEYS + k
            n = min(KEYS - k, P - row % P)
            yield h, k, k + n, row // P, row % P
            k += n


PIECES = list(value_pieces())


def steps(order, i, prev, ahead):
    for step, d, b, k in order:
        if (prev or d >= 0) and (ahead or d <= 0):
            yield step, (i if d == 0 else i + 1 if d > 0 else i - 1), b, k, not prev and d == 0


def build(nc, x, ctx_768, g_xattn, g_ffn, wq, bq, wk, bk, wv, bv, wo, bo,
          gate_w, w1, b1, w2, b2, sw1, sb1, sw2, sb2, out):
    values_dram = nc.dram_tensor("values_dram", (BATCHES, KEYS, DIM), F32).ap()
    sorted_dram = nc.dram_tensor("sorted_dram", (SLOTS + RTOK, ROW), F32).ap()
    part_dram = nc.dram_tensor("part_dram", (TOKENS, DIM), F32).ap()

    def tiled(rows):
        return rows.rearrange("(t p) d -> p t d", p=P)

    x_rows = tiled(x.rearrange("b s d -> (b s) d"))

    ctx = ExitStack()
    with ctx:
        def sem(name):
            return ctx.enter_context(nc.semaphore(name))

        def sb(name, shape, dt=F32, scope=ctx):
            return scope.enter_context(nc.sbuf_tensor(name, shape, dt))

        x_all = sb("x_all", [P, TILES, DIM])
        xn2_all = sb("xn2_all", [P, TILES, ROW])
        x2T = [sb(f"x2T_{n}", [P, KC, PTOK], F32R) for n in ("hi", "lo")]
        h32 = sb("h32", [P, 2, PTOK])
        context = ExitStack()
        v_sb = sb("v_sb", [KEYS, BATCHES, DIM], scope=context)
        context.close()
        hT = [sb(f"hT_{n}", [P, HB, PTOK], F32R) for n in ("hi", "lo")]
        sw1_sb = [sb(f"sw1_{n}", [P, KC, HIDDEN], F32R) for n in ("hi", "lo")]
        sw2_sb = [sb(f"sw2_{n}", [P, HC, DIM], F32R) for n in ("hi", "lo")]
        stage = sb("stage", [P, 2, KC * HIDDEN])
        ident = sb("ident", [P, P])
        gains = sb("gains", [P, 2])
        vec_rows = sb("vec_rows", [VECS, P])
        vec_cols = sb("vec_cols", [P, VECS])
        bq_sb = vec_cols[:, 0:GROUPS]
        bk_sb = vec_cols[:, GROUPS:2 * GROUPS]
        b1_sb = vec_cols[:, V_B1:V_GATE].rearrange("p (m c) -> p m c", c=HC)
        gw32 = vec_cols[:, V_GATE:VECS].rearrange("p (e k) -> p e k", e=EXPERTS)
        gw = [sb(f"gw_{n}", [P, EXPERTS, KC], F32R) for n in ("hi", "lo")]
        fill = sb("fill", [P, 1])
        bias_rows = sb("bias_rows", [P, 2, DIM])
        stats = sb("stats", [P, TILES, 6])
        mv = sb("mv", [P, TILES, 2])
        rstd = sb("rstd", [P, TILES])
        nt = sb("nt", [P, 2, TILES])
        stats2 = sb("stats2", [P, TP, 6])
        mv2 = sb("mv2", [P, TP, 2])
        rstd2 = sb("rstd2", [P, TP])
        nt2 = sb("nt2", [P, 2, TP])
        gate_rows = sb("gate_rows", [EXPERTS, PTOK])
        gate_sb = sb("gate_sb", [P, TILES, EXPERTS])
        before = sb("before", [P, P])
        ones = sb("ones", [P, P])
        seams = sb("seams", [P, RTILES - 2])
        number = sb("number", [P, TILES])
        zero_tile = sb("zero_tile", [P, TILES])
        empty_rows = sb("empty_rows", [P, RT, ROW])
        relu_b1 = sb("relu_b1", [P, EXPERTS, HC])
        relu_b1p = [sb(f"relu_b1_{n}", [P, EXPERTS, HC], F32R) for n in ("hi", "lo")]

        att = ExitStack()
        wq_sb = sb("wq_sb", [P, KC, DIM], scope=att)
        wo_sb = sb("wo_sb", [P, KC, DIM], scope=att)
        bv_row = sb("bv_row", [KEYS, DIM], scope=att)
        kT = sb("kT", [P, GROUPS, BATCHES * KEYS], scope=att)
        k_diag = sb("k_diag", [P, 2, GROUPS, GK], scope=att)
        v_diag = sb("v_diag", [P, 2, GROUPS, CHUNKS, P], scope=att)
        xn = sb("xn", [P, 2, TB, DIM], scope=att)
        xnT = sb("xnT", [P, 2, KC, SEQ], scope=att)
        qT = sb("qT", [P, 2, GROUPS, SEQ], scope=att)
        context = ExitStack()
        wk_sb = sb("wk_sb", [CK, CKC, DIM], scope=context)
        y_sb = sb("y_sb", [KEYS, BATCHES, CROSS], scope=context)
        context.close()
        probs = sb("probs", [P, 2, 4, GK], scope=att)
        context = ExitStack()
        wv_sb = sb("wv_sb", [CK, CKC, DIM], scope=context)
        yT = sb("yT", [CK, CKC, BATCHES * KEYS], scope=context)
        context.close()
        pT = sb("pT", [P, GROUPS * CHUNKS, SEQ], scope=att)
        oT = sb("oT", [P, GROUPS, SEQ], scope=att)
        xn2 = sb("xn2", [P, TP, DIM], scope=att)
        smax = sb("smax", [P, 2, 4, HG], scope=att)
        rsum = sb("rsum", [P, 2, 4, HG], scope=att)
        rinv = sb("rinv", [P, 2, 4, HG], scope=att)
        att.close()

        ew1_sb = [sb(f"ew1_{n}", [P, EXPERTS, KC, HIDDEN], F32R) for n in ("hi", "lo")]
        ew2_sb = [sb(f"ew2_{n}", [P, EXPERTS, HC, DIM], F32R) for n in ("hi", "lo")]
        xs = sb("xs", [P, RT, ROW])
        xsT = [sb(f"xsT_{n}", [P, 2, KC, RTOK], F32R) for n in ("hi", "lo")]
        gather_token = sb("gather_token", [P, RT], U32)
        scatter_token = sb("scatter_token", [P, RT], U32)
        part = sb("part", [P, RT, DIM])
        final = sb("final", [P, RT, DIM])
        other_row = sb("other_row", [P, EXPERTS, DIM])
        chosen = sb("chosen", [P, TILES])
        tile_sum = sb("tile_sum", [P, TILES])
        prefix = sb("prefix", [P, TILES])
        rank1 = sb("rank1", [P, TILES])
        count0 = sb("count0", [P, 1])
        past = sb("past", [P, RTILES - 2])
        tiles0 = sb("tiles0", [P, 1])
        tiles0_int = sb("tiles0_int", [P, 1], I32)
        base1 = sb("base1", [P, 1])
        rank0 = sb("rank0", [P, TILES])
        moved = sb("moved", [P, TILES])
        place = sb("place", [P, TILES])
        place_int = sb("place_int", [P, TILES], U32)

        bank = [ctx.enter_context(nc.psum_tensor(f"bank{n}", [P, 512], F32)) for n in range(4)]
        h_ps = ctx.enter_context(nc.psum_tensor("h_ps", [P, 2, 512], F32))
        y_ps = ctx.enter_context(nc.psum_tensor("y_ps", [P, TP, DIM], F32))

        consts_made = sem("consts_made")
        x_in = [sem(f"x_in{n}") for n in range(2)]
        wo_in = sem("wo_in")
        empty_made = sem("empty_made")
        stats2_rdy = sem("stats2_rdy")
        newton = sem("newton")
        scatter_ids = sem("scatter_ids")
        small_in = sem("small_in")
        context_in = sem("context_in")
        vecs_in = sem("vecs_in")
        vecs_ps = sem("vecs_ps")
        vecs_rdy = sem("vecs_rdy")
        stage_in = [sem(f"stage_in{n}") for n in range(2)]
        gains_ready = sem("gains_ready")
        rows_ready = sem("rows_ready")
        yT_ps = sem("yT_ps")
        yT_sb = sem("yT_sb")
        kT_ps = sem("kT_ps")
        kT_sb = sem("kT_sb")
        v_ps = sem("v_ps")
        v_rdy = sem("v_rdy")
        v_out = [sem(f"v_out{n}") for n in range(2)]
        cleared = sem("cleared")
        dve_chain = sem("dve_chain")
        var_ready = sem("var_ready")
        w_hi = sem("w_hi")
        w_lo = sem("w_lo")
        gw_cut = sem("gw_cut")
        k_in = [sem(f"k_in{n}") for n in range(2)]
        v_in = [sem(f"v_in{n}") for n in range(2)]
        xn_ready = sem("xn_ready")
        x_biased = sem("x_biased")
        xnT_ps = sem("xnT_ps")
        xnT_sb = sem("xnT_sb")
        q_ps = sem("q_ps")
        q_sb = sem("q_sb")
        s_ps = sem("s_ps")
        s_max = sem("s_max")
        s_shifted = sem("s_shifted")
        p_exp = sem("p_exp")
        p_sum = sem("p_sum")
        p_rinv = sem("p_rinv")
        p_ready = sem("p_ready")
        pT_ps = sem("pT_ps")
        pT_sb = sem("pT_sb")
        o_ps = sem("o_ps")
        o_sb = sem("o_sb")
        proj_ps = sem("proj_ps")
        x1_ready = sem("x1_ready")
        var2_ready = sem("var2_ready")
        xn2_ready = sem("xn2_ready")
        xn2_kept = sem("xn2_kept")
        x1_biased = sem("x1_biased")
        x2T_ps = sem("x2T_ps")
        x2T_hi = sem("x2T_hi")
        x2T_lo = sem("x2T_lo")
        gate_ps = sem("gate_ps")
        gate_copied = sem("gate_copied")
        gate_turned = sem("gate_turned")
        gate_rdy = sem("gate_rdy")
        h_in_ps = sem("h_in_ps")
        h_hi = sem("h_hi")
        h_32 = sem("h_32")
        h_lo = sem("h_lo")
        y_used = sem("y_used")
        y_out = sem("y_out")
        part_out = sem("part_out")
        filled = sem("filled")
        chosen_rdy = sem("chosen_rdy")
        counts_ps = sem("counts_ps")
        places_rdy = sem("places_rdy")
        scattered = sem("scattered")
        seam_rdy = sem("seam_rdy")
        rb_cut = sem("rb_cut")
        other_ps = sem("other_ps")
        other_rdy = sem("other_rdy")
        xs_in = sem("xs_in")
        ids_copied = sem("ids_copied")
        xsT_ps = sem("xsT_ps")
        xsT_hi = sem("xsT_hi")
        xsT_lo = sem("xsT_lo")
        gathered = sem("gathered")
        part_rdy = sem("part_rdy")
        final_rdy = sem("final_rdy")
        rows_out = sem("rows_out")
        iotas = sem("iotas")

        SMALL = 16 * 7

        def one_bank(rows, g=4, n=KEYS):
            return rows.rearrange("p (h k) -> p h k", k=n)

        def hidden_bank(n):
            return h_ps[:, n, :] if n < 2 else bank[n - 2]

        block = ctx.enter_context(nc.Block())

        @block.sync
        def _(sp):
            sp.dma_start(y_sb[:, :, :], ctx_768.rearrange("b s d -> s b d")).then_inc(context_in, 16)
            sp.dma_start(wk_sb[:, :, :], wk.rearrange("(k p) d -> p k d", p=CK)).then_inc(context_in, 16)
            sp.dma_start(x_all[:, 0:TP, :], x_rows[:, 0:TP, :]).then_inc(x_in[0], 16)
            sp.dma_start(wv_sb[:, :, :], wv.rearrange("(k p) d -> p k d", p=CK)).then_inc(context_in, 16)
            sp.dma_start(wq_sb[:, :, :], wq.rearrange("(k p) d -> p k d", p=P)).then_inc(small_in, 16)
            sp.dma_start(bv_row[:, :], bv.partition_broadcast(KEYS)).then_inc(small_in, 16)
            sp.dma_start(bias_rows[:, 0, :], bo.partition_broadcast(P)).then_inc(small_in, 16)
            sp.dma_start(bias_rows[:, 1, :], sb2.partition_broadcast(P)).then_inc(small_in, 16)
            sp.dma_start(h32[:, 0, 0:2 * DIM],
                         b2.rearrange("e d -> (e d)").partition_broadcast(P)).then_inc(small_in, 16)
            sp.dma_start(x_all[:, TP:TILES, :], x_rows[:, TP:TILES, :]).then_inc(x_in[1], 16)
            sp.dma_start(wo_sb[:, :, :], wo.rearrange("(k p) d -> p k d", p=P)).then_inc(wo_in, 16)
            sp.wait_ge(kT_sb, 4)
            sp.wait_ge(cleared, 1)

            def keys_diagonal(i, b):
                for h in range(HG):
                    rows = slice(h * HEAD_DIM, (h + 1) * HEAD_DIM)
                    sp.dma_start(k_diag[rows, b, :, h * KEYS:(h + 1) * KEYS],
                                 kT[rows, :, bass.ds((2 * i + b) * KEYS, KEYS)]).then_inc(k_in[b], 16)

            def values_diagonal(i, b):
                for h, k0, k1, c, p0 in PIECES:
                    cols = slice(h * HEAD_DIM, (h + 1) * HEAD_DIM)
                    src = values_dram[bass.ds(2 * i + b, 1), k0:k1, :].rearrange("o k (g f) -> k (o g) f", g=GROUPS)
                    sp.dma_start(v_diag[p0:p0 + k1 - k0, b, :, c, cols], src[:, :, cols]).then_inc(v_in[b], 16)

            keys_diagonal(0, 0)
            keys_diagonal(0, 1)
            sp.dma_start(stage[:, 0, :].rearrange("p (k h) -> p k h", k=KC),
                         sw1.rearrange("(k p) h -> p k h", p=P)).then_inc(stage_in[0], 16)
            sp.dma_start(stage[:, 1, :].rearrange("p (c d) -> p c d", c=HC),
                         sw2.rearrange("(c p) d -> p c d", p=P)).then_inc(stage_in[1], 16)
            sp.wait_ge(cleared, 2)
            for n, batches in enumerate((slice(0, 2), slice(2, BATCHES))):
                sp.wait_ge(v_rdy, batches.stop)
                sp.dma_start(values_dram[batches].rearrange("b k d -> k b d"), v_sb[:, batches, :]
                             ).then_inc(v_out[n], 16)
                if n == 0:
                    sp.wait_ge(v_out[0], 16)
                    for b in range(2):
                        values_diagonal(0, b)
            sp.wait_ge(empty_made, 2)
            for j in range(RTILES + 1):
                rows = sorted_dram[j * RTOK:(j + 1) * RTOK, :].rearrange("(t p) d -> p t d", p=P)
                sp.dma_start(rows, empty_rows[:, :, :]).then_inc(filled, 16)
            x_out = tiled(part_dram)

            def keep_xn2(i):
                sp.wait_ge(xn2_ready, i + 1)
                sp.dma_start(xn2_all[:, bass.ds(i * TP, TP), 0:DIM], xn2[:, :, :]).then_inc(xn2_kept, 16)

            def store_part(j):
                sp.wait_ge(y_out, j + 1)
                sp.dma_start(x_out[:, bass.ds(j * TP, TP), :], x_all[:, bass.ds(j * TP, TP), :]).then_inc(part_out, 16)

            def iteration(i, prev, ahead):
                if ahead:
                    sp.wait_ge(s_ps, (2 * i + 1) * 8)
                    keys_diagonal(i + 1, 0)
                if prev:
                    keep_xn2(i - 1)
                if not prev:
                    sp.wait_ge(v_out[1], 16)
                if ahead:
                    sp.wait_ge(o_ps, 2 * i + 1)
                    values_diagonal(i + 1, 0)
                    sp.wait_ge(s_ps, (2 * i + 2) * 8)
                    keys_diagonal(i + 1, 1)
                    sp.wait_ge(o_ps, 2 * i + 2)
                    values_diagonal(i + 1, 1)
                if prev:
                    store_part(i - 1)

            iteration(0, False, True)
            sp.wait_ge(w_lo, 1)
            sp.dma_start(stage[:, 0, :].rearrange("p (k h) -> p k h", k=KC),
                         w1[0].rearrange("(k p) h -> p k h", p=P)).then_inc(stage_in[0], 16)
            sp.wait_ge(w_lo, 2)
            sp.dma_start(stage[:, 1, :].rearrange("p (c d) -> p c d", c=HC),
                         w2[0].rearrange("(c p) d -> p c d", p=P)).then_inc(stage_in[1], 16)
            with sp.Fori(1, PAIRS - 1) as i:
                iteration(i, True, True)
            iteration(PAIRS - 1, True, False)
            keep_xn2(PAIRS - 1)
            sp.wait_ge(w_lo, 3)
            sp.dma_start(stage[:, 0, :].rearrange("p (k h) -> p k h", k=KC),
                         w1[1].rearrange("(k p) h -> p k h", p=P)).then_inc(stage_in[0], 16)
            sp.wait_ge(w_lo, 4)
            sp.dma_start(stage[:, 1, :].rearrange("p (c d) -> p c d", c=HC),
                         w2[1].rearrange("(c p) d -> p c d", p=P)).then_inc(stage_in[1], 16)

            def load_sorted(j):
                rows = sorted_dram[bass.ds(j * RTOK, RTOK), :].rearrange("(t p) d -> p t d", p=P)
                sp.dma_start(xs[:, :, :], rows).then_inc(xs_in, 16)

            sp.wait_ge(scattered, 16 * TILES)
            load_sorted(0)
            store_part(PAIRS - 1)
            sp.wait_ge(seam_rdy, 1)
            tiles_of_0 = sp.value_load(tiles0_int[0:1, 0:1], min_val=1, max_val=RTILES - 1)

            def routed(j):
                sp.wait_ge(xsT_ps, j + 1)
                sp.wait_ge(ids_copied, j + 1)
                load_sorted(j + 1)

            with sp.Fori(0, tiles_of_0) as j:
                routed(j)
            with sp.Fori(tiles_of_0, RTILES) as j:
                routed(j)
            sp.wait_ge(xs_in, 16 * (RTILES + 1))

        @block.gpsimd
        def _(pool):
            nc.gpsimd.memset(ident[:, :], 0.0).then_inc(iotas, 1)
            pool.wait_ge(iotas, 1)
            nc.gpsimd.affine_select(out=ident[:, :], in_=ident[:, :], compare_op=ALU.not_equal, fill=1.0, base=0,
                                    pattern=[[-1, P]], channel_multiplier=1).then_inc(consts_made, 1)
            nc.gpsimd.iota(xn2_all[:, :, DIM:ROW].rearrange("p t o -> p (t o)"), pattern=[[P, TILES]], base=0,
                           channel_multiplier=1, allow_small_or_imprecise_dtypes=True).then_inc(iotas, 1)
            nc.gpsimd.memset(k_diag[:, :, :, :], 0.0).then_inc(cleared, 1)
            nc.gpsimd.memset(v_diag[:, :, :, :, :], 0.0).then_inc(cleared, 1)
            nc.gpsimd.memset(ones[:, :], 1.0).then_inc(iotas, 1)
            nc.gpsimd.memset(before[:, :], 1.0).then_inc(iotas, 1)
            nc.gpsimd.memset(zero_tile[:, :], 0.0).then_inc(iotas, 1)
            nc.gpsimd.memset(empty_rows[:, :, :], 0.0).then_inc(iotas, 1)
            nc.gpsimd.iota(seams[:, :], pattern=[[RTOK, RTILES - 2]], base=RTOK, channel_multiplier=0,
                           allow_small_or_imprecise_dtypes=True).then_inc(iotas, 1)
            nc.gpsimd.iota(number[:, :], pattern=[[P, TILES]], base=0, channel_multiplier=1,
                           allow_small_or_imprecise_dtypes=True).then_inc(iotas, 1)
            pool.wait_ge(iotas, 8)
            nc.gpsimd.affine_select(out=before[:, :], in_=before[:, :], compare_op=ALU.is_gt, fill=0.0, base=0,
                                    pattern=[[1, P]], channel_multiplier=-1).then_inc(empty_made, 1)
            nc.gpsimd.iota(empty_rows[:, :, DIM:ROW].rearrange("p t o -> p (t o)"), pattern=[[P, RT]], base=NO_TOKEN,
                           channel_multiplier=1, allow_small_or_imprecise_dtypes=True).then_inc(empty_made, 1)
            def bias_x(i, b):
                pool.wait_ge(xn_ready, 2 * i + b + 1)
                for t in range(TB):
                    row = x_all[:, bass.ds((2 * i + b) * TB + t, 1), :].rearrange("p o d -> p (o d)")
                    nc.gpsimd.tensor_tensor(row, row, bias_rows[:, 0, :], ALU.add).then_inc(x_biased, 1)

            def iteration(i, prev, ahead, order=ORDER):
                for step, j, b, k, early in steps(order, i, prev, ahead):
                    if step == "in":
                        bias_x(j, b)
                    if step == "scores":
                        pool.wait_ge(p_rinv, (2 * j + b) * 4 + k + 1)
                        pq = one_bank(probs[:, b, k, :])
                        nc.gpsimd.tensor_tensor(pq, pq, rinv[:, b, k, :].unsqueeze(2).to_broadcast([P, HG, KEYS]),
                                                ALU.mult).then_inc(p_ready, 1)
                        if early and b == 1 and k >= 2:
                            n = k - 2
                            hi, lo = ((sw1_sb, sw2_sb)[n][m][:, :, :].rearrange("p k h -> p (k h)") for m in range(2))
                            pool.wait_ge(w_hi, n + 1)
                            nc.gpsimd.tensor_tensor(lo, stage[:, n, :], hi, ALU.subtract).then_inc(w_lo, 1)
                    if step == "y" and k < TP:
                        bias_x1(j, k)

            def bias_x1(i, t):
                pool.wait_ge(xn2_ready, i + 1)
                row = x_all[:, bass.ds(i * TP + t, 1), :].rearrange("p o d -> p (o d)")
                nc.gpsimd.tensor_tensor(row, row, bias_rows[:, 1, :], ALU.add).then_inc(x1_biased, 1)

            pool.wait_ge(rows_ready, 1)
            bias_x(0, 0)
            iteration(0, False, True, FIRST)
            iteration(0, False, True)
            with pool.Fori(1, PAIRS - 1) as i:
                iteration(i, True, True)
            iteration(PAIRS - 1, True, False)
            for t in range(TP):
                bias_x1(PAIRS - 1, t)
            pool.wait_ge(x2T_ps, PAIRS * KC)
            pool.wait_ge(xn2_kept, 16 * PAIRS)
            nc.gpsimd.memset(part[:, :, :], 0.0).then_inc(iotas, 1)
            pool.wait_ge(iotas, 9)
            pool.wait_ge(filled, 16 * (RTILES + 1))
            pool.wait_ge(places_rdy, 1)
            for t in range(TILES):
                pool.indirect_dma_start(
                    out=sorted_dram[:, :], out_offset=bass.IndirectOffsetOnAxis(ap=place_int[:, t:t + 1], axis=0),
                    in_=xn2_all[:, t, :], in_offset=None, bounds_check=SLOTS - 1,
                    oob_is_err=False).then_inc(scattered, 16)
            pool.wait_ge(other_rdy, 1)
            pool.wait_ge(part_out, 16 * PAIRS)
            pool.wait_ge(seam_rdy, 1)
            tiles_of_0 = pool.value_load(tiles0_int[0:1, 0:1], min_val=1, max_val=RTILES - 1)

            last_token = pool.to_reg(TOKENS - 1)

            def routed(j, e):
                turn = pool.to_reg(j + 1)
                used = j
                pool.wait_ge(seam_rdy, 1)
                pool.wait_ge(ids_copied, turn)
                pool.wait_ge(final_rdy, used)
                for t in range(RT):
                    pool.indirect_dma_start(
                        out=part[:, t, :], out_offset=None, in_=part_dram[:, :],
                        in_offset=bass.IndirectOffsetOnAxis(ap=gather_token[:, t:t + 1], axis=0),
                        bounds_check=last_token, oob_is_err=False).then_inc(gathered, 16)
                pool.wait_ge(gathered, 32 * (j + 1))
                for t in range(RT):
                    nc.gpsimd.tensor_tensor(part[:, t, :], part[:, t, :], other_row[:, 1 - e, :], ALU.add
                                            ).then_inc(part_rdy, 1)
                pool.wait_ge(seam_rdy, 1)
                pool.wait_ge(final_rdy, turn)
                pool.wait_ge(scatter_ids, turn)
                for t in range(RT):
                    pool.indirect_dma_start(
                        out=out[:, :], out_offset=bass.IndirectOffsetOnAxis(ap=scatter_token[:, t:t + 1], axis=0),
                        in_=final[:, t, :], in_offset=None, bounds_check=last_token,
                        oob_is_err=False).then_inc(rows_out, 16)

            with pool.Fori(0, tiles_of_0) as j:
                routed(j, 0)
            with pool.Fori(tiles_of_0, RTILES) as j:
                routed(j, 1)
            pool.wait_ge(rows_out, 32 * RTILES)

        @block.scalar
        def _(act):
            at = 0
            for vec in (bq, bk, sb1, b1.rearrange("e h -> (e h)"), gate_w.rearrange("e d -> (e d)")):
                n = vec.shape[0] // P
                act.dma_start(vec_rows[at:at + n, :], vec.rearrange("(n p) -> n p", p=P)).then_inc(vecs_in, 16)
                at += n
            act.dma_start(gains[:, 0:1], g_xattn.partition_broadcast(P)).then_inc(small_in, 16)
            act.dma_start(gains[:, 1:2], g_ffn.partition_broadcast(P)).then_inc(small_in, 16)
            act.wait_ge(vecs_ps, 1)
            nc.scalar.activation(vec_cols[:, :], h_ps[:, 0, 0:VECS], ACT.Copy).then_inc(vecs_rdy, 1)
            act.wait_ge(vecs_rdy, 1)
            for n in range(CKC * 2):
                act.wait_ge(yT_ps, n + 1)
                nc.scalar.activation(yT[:, n // 2, (n % 2) * YH:(n % 2 + 1) * YH], bank[n][0:CK, 0:YH],
                                     ACT.Copy).then_inc(yT_sb, 1)
            for n, (g, half) in enumerate((g, half) for g in range(GROUPS) for half in range(2)):
                act.wait_ge(kT_ps, n + 1)
                src = h_ps[:, half, 0:YH] if g == 0 else y_ps[:, 2 * half:2 * half + 2, :].rearrange("p a d -> p (a d)")[:, 0:YH]
                nc.scalar.activation(kT[:, g, half * YH:(half + 1) * YH], src, ACT.Identity,
                                     bias=bk_sb[:, g:g + 1]).then_inc(kT_sb, 1)
            act.wait_ge(small_in, SMALL)
            nc.scalar.activation(gains[:, :], gains[:, :], ACT.Tanh).then_inc(gains_ready, 1)

            def hidden(q, c, m, width, start, banks=2):
                act.wait_ge(h_in_ps, q + 1)
                act.wait_ge(y_used, q - HB + 1 if c >= HB else start)
                nc.scalar.activation(hT[0][:, c % HB, 0:width], hidden_bank(c % banks)[:, 0:width], ACT.Relu,
                                     bias=b1_sb[:, m, c:c + 1]).then_inc(h_hi, 1)
                act.wait_ge(h_lo, q - 1 if c >= 2 else start)
                nc.scalar.activation(h32[:, c % 2, 0:width], hidden_bank(c % banks)[:, 0:width], ACT.Relu,
                                     bias=b1_sb[:, m, c:c + 1]).then_inc(h_32, 1)

            def inputs(i, b):
                act.wait_ge(xnT_ps, 2 * i + b + 1)
                nc.scalar.activation(xnT[:, b, :, :].rearrange("p k s -> p (k s)"), bank[2][:, :], ACT.Copy
                                     ).then_inc(xnT_sb, 1)

            def queries(i, b):
                act.wait_ge(q_ps, 2 * i + b + 1)
                for g in range(GROUPS):
                    nc.scalar.activation(qT[:, b, g, :], bank[3][:, g * SEQ:(g + 1) * SEQ], ACT.Identity,
                                         bias=bq_sb[:, g:g + 1]).then_inc(q_sb, 1)

            def norm2_copies(i):
                for kc in range(KC):
                    act.wait_ge(x2T_ps, KC * i + kc + 1)
                    if kc == 0:
                        act.wait_ge(h_in_ps, HC * i)
                    nc.scalar.activation(x2T[0][:, kc, :], bank[2 + kc][:, :], ACT.Copy).then_inc(x2T_hi, 1)

            def attention(step, j, b, k, first):
                if step == "turn":
                    for u in TURNS[k]:
                        act.wait_ge(pT_ps, (2 * j + b) * CHUNKS + u + 1)
                        if u == 0 and first:
                            act.wait_ge(v_ps, BATCHES)
                        elif u == 0:
                            act.wait_ge(o_ps, 2 * j + b)
                        for v in range(2):
                            r = ROWS[(2 * u + v) % CHUNKS]
                            nc.scalar.activation(pT[0:r, 2 * u + v, :], bank[2 + u % 2][0:r, v * SEQ:(v + 1) * SEQ],
                                                 ACT.Copy).then_inc(pT_sb, 1)
                if step == "values":
                    act.wait_ge(o_ps, 2 * j + b + 1)
                    if not first:
                        act.wait_ge(proj_ps, 2 * j + b)
                    nc.scalar.activation(oT[:, :, :].rearrange("p g s -> p (g s)"), bank[3][:, :], ACT.Copy
                                         ).then_inc(o_sb, 1)
                if step == "norm2":
                    norm2_copies(j)
                if step == "gate":
                    act.wait_ge(gate_ps, j + 1)
                    nc.scalar.activation(gate_rows[:, :], bank[3][0:EXPERTS, :], ACT.Copy).then_inc(gate_copied, 1)
                if step == "gate_turn":
                    act.wait_ge(gate_turned, j + 1)
                    nc.scalar.activation(
                        gate_sb[:, bass.ds(j * TP, TP), :].rearrange("p t e -> p (t e)"),
                        bank[3][:, 0:TP * EXPERTS], ACT.Copy).then_inc(gate_rdy, 1)

            def iteration(i, prev, ahead, order=ORDER):
                for step, j, b, k, early in steps(order, i, prev, ahead):
                    if step == "in":
                        inputs(j, b)
                    if step == "query":
                        queries(j, b)
                    attention(step, j, b, k, early and b == 0)
                    if step == "scores":
                        act.wait_ge(s_shifted, ((2 * j + b) * 4 + k + 1) * 2)
                        nc.scalar.activation(probs[:, b, k, :], probs[:, b, k, :], ACT.Exp,
                                             scale=HEAD_DIM ** -0.5).then_inc(p_exp, 1)
                        if early and b == 1 and k < 2:
                            act.wait_ge(stage_in[k], 16)
                            hi = (sw1_sb, sw2_sb)[k][0][:, :, :].rearrange("p k h -> p (k h)")
                            nc.scalar.activation(hi, stage[:, k, :], ACT.Copy).then_inc(w_hi, 1)
                    if step == "h":
                        hidden(j * HC + k, k, 0, PTOK, j * HC)

            inputs(0, 0)
            queries(0, 0)
            iteration(0, False, True, FIRST)
            iteration(0, False, True)
            with act.Fori(1, PAIRS - 1) as i:
                iteration(i, True, True)
            iteration(PAIRS - 1, True, False)

            def expert_hi(e, n):
                act.wait_ge(stage_in[n], 16 * (2 + e))
                hi = (ew1_sb[0][:, e, :, :], ew2_sb[0][:, e, :, :])[n].rearrange("p k h -> p (k h)")
                nc.scalar.activation(hi, stage[:, n, :], ACT.Copy).then_inc(w_hi, 1)

            for step, j, b, k, early in steps(LAST, PAIRS - 1, True, False):
                attention(step, j, b, k, False)
                if step == "norm2":
                    act.wait_ge(xn2_kept, 16 * PAIRS)
                if step == "h":
                    hidden((PAIRS - 1) * HC + k, k, 0, PTOK, (PAIRS - 1) * HC)
                    if k in (1, 2, 4, 6):
                        expert_hi(*CUT_AFTER[k])
            act.wait_ge(other_ps, EXPERTS)
            nc.scalar.activation(other_row[:, :, :].rearrange("p e d -> p (e d)"), bank[3][:, :], ACT.Copy,
                                 scale=gains[:, 1:2]).then_inc(other_rdy, 1)

            def sorted_hi(j):
                act.wait_ge(xsT_ps, j + 1)
                nc.scalar.activation(xsT[0][:, bass.ds(j % 2, 1), :, :].rearrange("p o k s -> p (o k s)"), bank[2][:, :], ACT.Copy
                                     ).then_inc(xsT_hi, 1)

            sorted_hi(0)
            act.wait_ge(seam_rdy, 1)
            tiles_of_0 = act.value_load(tiles0_int[0:1, 0:1], min_val=1, max_val=RTILES - 1)

            def routed(j, e):
                for c in range(HC):
                    hidden(PAIRS * HC + j * HC + c, c, 1 + e, RTOK, PAIRS * HC + j * HC, banks=4)
                    if c == 6:
                        sorted_hi(j + 1)

            with act.Fori(0, tiles_of_0) as j:
                routed(j, 0)
            with act.Fori(tiles_of_0, RTILES) as j:
                routed(j, 1)

        @block.vector
        def _(dve):
            chain = [0]

            def link(ins):
                chain[0] += 1
                ins.then_inc(dve_chain, 1)
                dve.wait_ge(dve_chain, chain[0])

            def root(var, r, v, t):
                yield nc.vector.tensor_scalar(v, var, EPS, None, ALU.add)
                yield nc.vector.tensor_scalar(t.bitcast(I32), v.bitcast(I32), 1, None, ALU.logical_shift_right)
                yield nc.vector.tensor_scalar(r.bitcast(I32), t.bitcast(I32), -1, ROOT_MAGIC, ALU.mult, ALU.add)
                for _ in range(NEWTON):
                    yield nc.vector.tensor_tensor(t, v, r, ALU.mult)
                    yield nc.vector.scalar_tensor_tensor(out=t, in0=t, scalar=-0.5, in1=r, op0=ALU.mult, op1=ALU.mult)
                    yield nc.vector.scalar_tensor_tensor(out=r, in0=t, scalar=1.5, in1=r, op0=ALU.add, op1=ALU.mult)


            def statistics(n, tiles):
                dve.wait_ge(x_in[n], 16)
                for t in tiles:
                    ins = nc.vector.bn_stats(stats[:, t, :], x_all[:, t, :])
                link(ins)
                for t in tiles:
                    ins = nc.vector.bn_aggr(mv[:, t, :], stats[:, t, :])
                ins.then_inc(var_ready, 1)

            def refine(n, tiles):
                dve.wait_ge(var_ready, n + 1)
                for ins in root(mv[:, tiles, 1:2].rearrange("p t o -> p (t o)"), rstd[:, tiles],
                                nt[:, 0, tiles], nt[:, 1, tiles]):
                    link(ins)

            def normalise(i, b):
                for t in range(TB):
                    row = x_all[:, bass.ds((2 * i + b) * TB + t, 1), :].rearrange("p o d -> p (o d)")
                    ins = nc.vector.tensor_scalar(
                        xn[:, b, t, :], row,
                        mv[:, bass.ds((2 * i + b) * TB + t, 1), 0:1].rearrange("p t o -> p (t o)"),
                        rstd[:, bass.ds((2 * i + b) * TB + t, 1)], ALU.subtract, ALU.mult)
                ins.then_inc(xn_ready, 1)

            statistics(0, range(TP))
            refine(0, slice(0, TP))
            normalise(0, 0)
            normalise(0, 1)
            def values(b):
                dve.wait_ge(v_ps, b + 1)
                nc.vector.tensor_tensor(v_sb[:, b, :], h_ps[0:KEYS, b % 2, 0:DIM], bv_row[:, :], ALU.add
                                        ).then_inc(v_rdy, 1)

            dve.wait_ge(small_in, SMALL)
            dve.wait_ge(gains_ready, 1)
            nc.vector.tensor_scalar(bias_rows[:, 0, :], bias_rows[:, 0, :], gains[:, 0:1], None, ALU.mult)
            link(nc.vector.tensor_tensor(bias_rows[:, 1, :], bias_rows[:, 1, :], h32[:, 0, 0:DIM], ALU.add))
            link(nc.vector.tensor_tensor(bias_rows[:, 1, :], bias_rows[:, 1, :], h32[:, 0, DIM:2 * DIM], ALU.add))
            nc.vector.tensor_scalar(bias_rows[:, 1, :], bias_rows[:, 1, :], gains[:, 1:2], None, ALU.mult
                                    ).then_inc(rows_ready, 1)
            dve.wait_ge(vecs_rdy, 1)
            link(nc.vector.tensor_copy(gw[0][:, :, :], gw32))
            nc.vector.tensor_tensor(gw[1][:, :, :], gw32, gw[0][:, :, :], ALU.subtract).then_inc(gw_cut, 1)
            statistics(1, range(TP, TILES))
            refine(1, slice(TP, TILES))

            def sums(i, b, k):
                dve.wait_ge(p_exp, (2 * i + b) * 4 + k + 1)
                nc.vector.tensor_reduce(out=rsum[:, b, k, :], in_=one_bank(probs[:, b, k, :]), axis=AX_X, op=ALU.add
                                        ).then_inc(p_sum, 1)
                dve.wait_ge(p_sum, (2 * i + b) * 4 + k + 1)
                nc.vector.reciprocal(rinv[:, b, k, :], rsum[:, b, k, :]).then_inc(p_rinv, 1)

            def norm2(i):
                dve.wait_ge(var2_ready, i + 1)
                for n, ins in enumerate(root(mv2[:, :, 1:2].rearrange("p t o -> p (t o)"), rstd2[:, :],
                                             nt2[:, 0, :], nt2[:, 1, :])):
                    ins.then_inc(newton, 1)
                    dve.wait_ge(newton, ROOT_OPS * i + n + 1)
                dve.wait_ge(xn2_kept, 16 * i)
                for t in range(TP):
                    row = x_all[:, bass.ds(i * TP + t, 1), :].rearrange("p o d -> p (o d)")
                    ins = nc.vector.tensor_scalar(xn2[:, t, :], row, mv2[:, t, 0:1], rstd2[:, t:t + 1],
                                                  ALU.subtract, ALU.mult)
                ins.then_inc(xn2_ready, 1)

            def norm2_lo(i):
                for kc in range(KC):
                    dve.wait_ge(x2T_hi, KC * i + kc + 1)
                    nc.vector.tensor_tensor(x2T[1][:, kc, :], bank[2 + kc][:, :], x2T[0][:, kc, :],
                                            ALU.subtract).then_inc(x2T_lo, 1)

            def iteration(i, prev, ahead, order=ORDER):
                for step, j, b, k, early in steps(order, i, prev, ahead):
                    if step == "norm":
                        normalise(j, b)
                    if step == "sums":
                        sums(j, b, k)
                    second_half(step, j, b)
                    if step == "scores":
                        quarter = (2 * j + b) * 4 + k
                        for half in range(2):
                            dve.wait_ge(s_ps, quarter * 2 + half + 1)
                            nc.vector.tensor_reduce(
                                out=smax[:, b, k, half * HH:(half + 1) * HH], in_=one_bank(bank[half][:, 0:HALF]),
                                axis=AX_X, op=ALU.max).then_inc(s_max, 1)
                        if not early:
                            dve.wait_ge(pT_ps, (2 * j + b - 1) * CHUNKS)
                        for half in range(2):
                            dve.wait_ge(s_max, quarter * 2 + half + 1)
                            m = smax[:, b, k, half * HH:(half + 1) * HH].unsqueeze(2).to_broadcast([P, HH, KEYS])
                            nc.vector.tensor_tensor(one_bank(probs[:, b, k, half * HALF:(half + 1) * HALF]),
                                                    one_bank(bank[half][:, 0:HALF]), m, ALU.subtract
                                                    ).then_inc(s_shifted, 1)
                        if k >= 1:
                            sums(j, b, k - 1)
                        if early and b == 0:
                            values(2 * k)
                            values(2 * k + 1)
                    if step == "h":
                        hidden_lo(j * HC + k, k, PTOK)
                    if step == "y" and k == HC - 1:
                        add_shared(j)

            def second_half(step, j, b):
                if step == "out":
                    dve.wait_ge(proj_ps, 2 * j + b + 1)
                    dve.wait_ge(x_biased, TB * (2 * j + b + 1))
                    rows = x_all[:, bass.ds((2 * j + b) * TB, TB), :].rearrange("p t d -> p (t d)")
                    nc.vector.scalar_tensor_tensor(out=rows, in0=bank[2][:, :], scalar=gains[:, 0:1], in1=rows,
                                                   op0=ALU.mult, op1=ALU.add).then_inc(x1_ready, 1)
                    dve.wait_ge(gains_ready, 1)
                    dve.wait_ge(x1_ready, 2 * j + b + 1)
                    for t in range(TB):
                        row = x_all[:, bass.ds((2 * j + b) * TB + t, 1), :].rearrange("p o d -> p (o d)")
                        ins = nc.vector.bn_stats(stats2[:, b * TB + t, :], row)
                    ins.then_inc(stats2_rdy, 1)
                    if b == 1:
                        dve.wait_ge(stats2_rdy, 2 * j + 2)
                        nc.vector.memset(fill[:, :], 0.0)
                        for t in range(TP):
                            ins = nc.vector.bn_aggr(mv2[:, t, :], stats2[:, t, :])
                        ins.then_inc(var2_ready, 1)
                if step == "root":
                    norm2(j)
                if step == "norm2":
                    norm2_lo(j)

            def hidden_lo(q, c, width):
                dve.wait_ge(h_32, q + 1)
                nc.vector.tensor_tensor(hT[1][:, c % HB, 0:width], h32[:, c % 2, 0:width], hT[0][:, c % HB, 0:width],
                                        ALU.subtract).then_inc(h_lo, 1)

            def add_shared(j):
                dve.wait_ge(y_used, (j + 1) * HC)
                dve.wait_ge(x1_biased, TP * (j + 1))
                for h in range(2):
                    rows = x_all[:, bass.ds(j * TP + h * TB, TB), :].rearrange("p t d -> p (t d)")
                    ins = nc.vector.scalar_tensor_tensor(
                        out=rows, in0=y_ps[:, h * TB:(h + 1) * TB, :].rearrange("p t d -> p (t d)"),
                        scalar=gains[:, 1:2], in1=rows, op0=ALU.mult, op1=ALU.add)
                ins.then_inc(y_out, 1)

            iteration(0, False, True, FIRST)
            iteration(0, False, True)
            with dve.Fori(1, PAIRS - 1) as i:
                iteration(i, True, True)
            iteration(PAIRS - 1, True, False)
            for step, j, b, k, early in steps(LAST, PAIRS - 1, True, False):
                second_half(step, j, b)

            dve.wait_ge(gate_rdy, PAIRS)
            dve.wait_ge(empty_made, 2)
            nc.vector.tensor_tensor(chosen[:, :], gate_sb[:, :, 1:2].rearrange("p t o -> p (t o)"),
                                    gate_sb[:, :, 0:1].rearrange("p t o -> p (t o)"), ALU.is_gt
                                    ).then_inc(chosen_rdy, 1)
            link(nc.vector.tensor_scalar(relu_b1[:, :, :], b1_sb[:, 1:1 + EXPERTS, :], 0.0, None, ALU.max))
            link(nc.vector.tensor_copy(relu_b1p[0][:, :, :], relu_b1[:, :, :]))
            nc.vector.tensor_tensor(relu_b1p[1][:, :, :], relu_b1[:, :, :], relu_b1p[0][:, :, :], ALU.subtract
                                    ).then_inc(rb_cut, 1)
            dve.wait_ge(counts_ps, 1)
            nc.vector.tensor_copy(rank1[:, :], bank[3][:, 64:64 + TILES])
            link(nc.vector.tensor_copy(tile_sum[:, :], bank[3][:, 128:128 + TILES]))
            link(nc.vector.tensor_tensor_scan(prefix[:, :], tile_sum[:, :], zero_tile[:, :], 0.0, ALU.add, ALU.add))
            link(nc.vector.tensor_tensor(rank1[:, 1:TILES], rank1[:, 1:TILES], prefix[:, 0:TILES - 1], ALU.add))
            link(nc.vector.tensor_tensor(rank0[:, :], number[:, :], rank1[:, :], ALU.subtract))
            link(nc.vector.tensor_scalar(count0[:, :], prefix[:, TILES - 1:TILES], -1.0, float(TOKENS),
                                         ALU.mult, ALU.add))
            link(nc.vector.tensor_scalar(past[:, :], seams[:, :], count0[:, :], None, ALU.is_lt))
            link(nc.vector.tensor_reduce(out=tiles0[:, :], in_=past[:, :], axis=AX_X, op=ALU.add))
            link(nc.vector.tensor_scalar(tiles0[:, :], tiles0[:, :], 1.0, None, ALU.add))
            nc.vector.tensor_copy(tiles0_int[:, :], tiles0[:, :]).then_inc(seam_rdy, 1)
            link(nc.vector.tensor_scalar(base1[:, :], tiles0[:, :], float(RTOK), None, ALU.mult))
            link(nc.vector.scalar_tensor_tensor(out=moved[:, :], in0=rank1[:, :], scalar=base1[:, :],
                                                in1=rank0[:, :], op0=ALU.add, op1=ALU.subtract))
            link(nc.vector.tensor_tensor(moved[:, :], moved[:, :], chosen[:, :], ALU.mult))
            link(nc.vector.tensor_tensor(place[:, :], rank0[:, :], moved[:, :], ALU.add))
            nc.vector.tensor_copy(place_int[:, :], place[:, :]).then_inc(places_rdy, 1)

            def expert_lo(e, n):
                dve.wait_ge(w_hi, 3 + 2 * e + n)
                hi, lo = ((ew1_sb[m][:, e, :, :], ew2_sb[m][:, e, :, :])[n].rearrange("p k h -> p (k h)")
                          for m in range(2))
                nc.vector.tensor_tensor(lo, stage[:, n, :], hi, ALU.subtract).then_inc(w_lo, 1)

            for step, j, b, k, early in steps(LAST, PAIRS - 1, True, False):
                if step == "h":
                    hidden_lo((PAIRS - 1) * HC + k, k, PTOK)
                    if k in (1, 2, 4, 6):
                        expert_lo(*CUT_AFTER[k])
            add_shared(PAIRS - 1)

            def sorted_lo(j):
                dve.wait_ge(xsT_hi, j + 1)
                nc.vector.tensor_tensor(xsT[1][:, bass.ds(j % 2, 1), :, :].rearrange("p o k s -> p (o k s)"),
                                        bank[2][:, :],
                                        xsT[0][:, bass.ds(j % 2, 1), :, :].rearrange("p o k s -> p (o k s)"),
                                        ALU.subtract).then_inc(xsT_lo, 1)

            sorted_lo(0)
            tiles_of_0 = dve.value_load(tiles0_int[0:1, 0:1], min_val=1, max_val=RTILES - 1)

            def routed(j, e):
                for c in range(HC):
                    hidden_lo(PAIRS * HC + j * HC + c, c, RTOK)
                    if c == 0:
                        dve.wait_ge(xs_in, 16 * (j + 1))
                        dve.wait_ge(gathered, 32 * j)
                        nc.vector.tensor_copy(gather_token[:, :], xs[:, :, DIM:ROW].rearrange("p t o -> p (t o)")
                                              ).then_inc(ids_copied, 1)
                    if c == 5:
                        dve.wait_ge(ids_copied, j + 1)
                        dve.wait_ge(rows_out, 32 * j)
                        nc.vector.tensor_copy(scatter_token[:, :], gather_token[:, :]).then_inc(scatter_ids, 1)
                    if c == 6:
                        sorted_lo(j + 1)
                dve.wait_ge(y_used, PAIRS * HC + (j + 1) * HC)
                dve.wait_ge(part_rdy, RT * (j + 1))
                dve.wait_ge(rows_out, 32 * j)
                nc.vector.scalar_tensor_tensor(
                    out=final[:, :, :].rearrange("p t d -> p (t d)"),
                    in0=y_ps[:, 0:RT, :].rearrange("p t d -> p (t d)"), scalar=gains[:, 1:2],
                    in1=part[:, :, :].rearrange("p t d -> p (t d)"), op0=ALU.mult, op1=ALU.add
                ).then_inc(final_rdy, 1)

            with dve.Fori(0, tiles_of_0) as j:
                routed(j, 0)
            with dve.Fori(tiles_of_0, RTILES) as j:
                routed(j, 1)

        @block.tensor
        def _(pe):
            def mm(out_, lhsT, rhs, start, stop, **kw):
                return nc.tensor.matmul(out_, lhsT, rhs, start=start, stop=stop, **kw)

            def cut(out_, lhs, rhs, start, stop, **kw):
                for n, (a, b) in enumerate(((0, 0), (1, 0), (0, 1))):
                    ins = mm(out_, lhs(a), rhs(b), start and n == 0, stop and n == 2, **kw)
                return ins

            pe.wait_ge(consts_made, 1)
            pe.wait_ge(vecs_in, 16 * 5)
            nc.tensor.transpose(h_ps[:, 0, 0:VECS], vec_rows[:, :], ident[0:VECS, 0:VECS]).then_inc(vecs_ps, 1)
            pe.wait_ge(vecs_rdy, 1)
            pe.wait_ge(context_in, 48)
            for n in range(CKC * 2):
                for q in range(4):
                    ins = nc.tensor.transpose(bank[n][0:CK, q * KEYS:(q + 1) * KEYS],
                                              y_sb[:, (n % 2) * 4 + q, (n // 2) * CK:(n // 2 + 1) * CK],
                                              ident[0:KEYS, 0:KEYS])
                ins.then_inc(yT_ps, 1)
            pe.wait_ge(yT_sb, 1)
            pe.wait_ge(yT_sb, CKC * 2)
            for g in range(GROUPS):
                for half in range(2):
                    dst = h_ps[:, half, 0:YH] if g == 0 else y_ps[:, 2 * half:2 * half + 2, :].rearrange("p a d -> p (a d)")[:, 0:YH]
                    for k in range(CKC):
                        ins = mm(dst, wk_sb[:, k, g * P:(g + 1) * P], yT[:, k, half * YH:(half + 1) * YH],
                                 k == 0, k == CKC - 1)
                    ins.then_inc(kT_ps, 1)

            def values(b):
                if b >= 2:
                    pe.wait_ge(v_rdy, b - 1)
                for k in range(CKC):
                    ins = mm(h_ps[0:KEYS, b % 2, 0:DIM], yT[:, k, b * KEYS:(b + 1) * KEYS], wv_sb[:, k, :],
                             k == 0, k == CKC - 1)
                ins.then_inc(v_ps, 1)

            pe.wait_ge(small_in, SMALL)

            def inputs(i, b):
                pe.wait_ge(xn_ready, 2 * i + b + 1)
                for kc in range(KC):
                    for t in range(TB):
                        ins = nc.tensor.transpose(bank[2][:, kc * SEQ + t * P:kc * SEQ + (t + 1) * P],
                                                  xn[:, b, t, kc * P:(kc + 1) * P], ident[:, :])
                ins.then_inc(xnT_ps, 1)

            def queries(i, b, prev):
                if b == 0 and prev:
                    pe.wait_ge(gate_rdy, i - 1)
                elif b == 1:
                    pe.wait_ge(q_sb, GROUPS * (2 * i + 1))
                pe.wait_ge(xnT_sb, 2 * i + b + 1)
                for g in range(GROUPS):
                    for kc in range(KC):
                        ins = mm(bank[3][:, g * SEQ:(g + 1) * SEQ], wq_sb[:, kc, g * P:(g + 1) * P],
                                 xnT[:, b, kc, :], kc == 0, kc == KC - 1)
                ins.then_inc(q_ps, 1)

            def attention(step, j, b, k, first, ahead, scores_next):
                if step == "turn":
                    for u in TURNS[k]:
                        if u == 0:
                            pe.wait_ge(p_ready, (2 * j + b) * 4 + 2)
                        if u == 2:
                            pe.wait_ge(p_ready, (2 * j + b) * 4 + 4)
                        if u >= 2:
                            pe.wait_ge(pT_sb, 2 * ((2 * j + b) * CHUNKS + u - 1))
                        elif b == 1 and ahead:
                            pe.wait_ge(*((xnT_sb, 2 * j + 3), (q_sb, GROUPS * (2 * j + 3)))[u])
                        elif b == 1:
                            pe.wait_ge(*((x1_ready, 2 * j + 1), (gate_rdy, j))[u])
                        else:
                            pe.wait_ge(*((xnT_sb, 2 * j + 2), (q_sb, GROUPS * (2 * j + 2)))[u])
                        for v in range(2):
                            ch = 2 * u + v
                            g, c = ch // CHUNKS, ch % CHUNKS
                            for t in range(TB):
                                ins = nc.tensor.transpose(
                                    bank[2 + u % 2][0:ROWS[c], v * SEQ + t * P:v * SEQ + (t + 1) * P],
                                    probs[:, b, g * TB + t, c * P:c * P + ROWS[c]], ident[:, :])
                        ins.then_inc(pT_ps, 1)
                if step == "values":
                    pe.wait_ge(v_in[b], 16 * len(PIECES) * (j + 1))
                    pe.wait_ge(pT_sb, 2 * CHUNKS * (2 * j + b + 1))
                    for g in range(GROUPS):
                        for c in range(CHUNKS):
                            ins = mm(bank[3][:, g * SEQ:(g + 1) * SEQ], v_diag[0:ROWS[c], b, g, c, :],
                                     pT[0:ROWS[c], g * CHUNKS + c, :], c == 0, c == CHUNKS - 1)
                    ins.then_inc(o_ps, 1)
                if step == "out":
                    if first:
                        pe.wait_ge(wo_in, 16)
                    elif b == 0:
                        pe.wait_ge(x2T_lo, KC * j)
                    pe.wait_ge(o_sb, 2 * j + b + 1)
                    for t in range(TB):
                        for kc in range(KC):
                            ins = mm(bank[2][:, t * DIM:(t + 1) * DIM], oT[:, kc, t * P:(t + 1) * P],
                                     wo_sb[:, kc, :], kc == 0, kc == KC - 1)
                    ins.then_inc(proj_ps, 1)
                if step == "norm2":
                    pe.wait_ge(xn2_ready, j + 1)
                    for kc in range(KC):
                        if kc == 1 and scores_next:
                            pe.wait_ge(o_sb, 2 * j + 3)
                        for t in range(TP):
                            ins = nc.tensor.transpose(bank[2 + kc][:, t * P:(t + 1) * P],
                                                      xn2[:, t, kc * P:(kc + 1) * P], ident[:, :])
                        ins.then_inc(x2T_ps, 1)
                if step == "gate":
                    pe.wait_ge(x2T_lo, KC * (j + 1))
                    for kc in range(KC):
                        ins = cut(bank[3][0:EXPERTS, :], lambda m: gw[m][:, :, kc], lambda m: x2T[m][:, kc, :],
                                  kc == 0, kc == KC - 1)
                    ins.then_inc(gate_ps, 1)
                if step == "gate_turn":
                    pe.wait_ge(consts_made, 1)
                    pe.wait_ge(gate_copied, j + 1)
                    for t in range(TP):
                        ins = nc.tensor.transpose(bank[3][:, t * EXPERTS:(t + 1) * EXPERTS],
                                                  gate_rows[:, t * P:(t + 1) * P], ident[0:EXPERTS, 0:EXPERTS])
                    ins.then_inc(gate_turned, 1)

            def iteration(i, prev, ahead, order=ORDER):
                for step, j, b, k, early in steps(order, i, prev, ahead):
                    if step == "in":
                        if not early:
                            pe.wait_ge(x1_ready, 2 * j - 1 + b)
                        inputs(j, b)
                    if step == "query":
                        queries(j, b, prev)
                    if step == "scores":
                        t, g = k % TB, k // TB
                        quarter = (2 * j + b) * 4 + k
                        if k == 0:
                            pe.wait_ge(q_sb, GROUPS * (2 * j + b + 1))
                            pe.wait_ge(k_in[b], 16 * HG * (j + 1))
                        for half in range(2):
                            if not early or (b, k) != (0, 0):
                                pe.wait_ge(s_shifted, quarter * 2 - 1 + half)
                            mm(bank[half][:, 0:HALF], qT[:, b, g, t * P:(t + 1) * P],
                               k_diag[:, b, g, half * HALF:(half + 1) * HALF], True, True).then_inc(s_ps, 1)
                        if early and b == 0:
                            values(2 * k)
                            values(2 * k + 1)
                    attention(step, j, b, k, early and b == 0, ahead, True)
                    if step == "h":
                        shared_h(j, k)
                    if step == "y":
                        shared_y(j, k)

            def shared_h(j, k):
                if k == 0:
                    pe.wait_ge(w_lo, 2)
                    pe.wait_ge(x2T_lo, KC * (j + 1))
                pe.wait_ge(h_32, j * HC + k - 1 if k >= 2 else j * HC)
                for kc in range(KC):
                    ins = cut(h_ps[:, k % 2, :], lambda m: sw1_sb[m][:, kc, k * P:(k + 1) * P],
                              lambda m: x2T[m][:, kc, :], kc == 0, kc == KC - 1)
                ins.then_inc(h_in_ps, 1)

            def shared_y(j, c):
                pe.wait_ge(h_lo, j * HC + c + 1)
                if c == 0:
                    pe.wait_ge(y_out, j)
                for t in range(TP):
                    ins = cut(y_ps[:, t, :], lambda m: hT[m][:, c % HB, t * P:(t + 1) * P],
                              lambda m: sw2_sb[m][:, c, :], c == 0 and t % 2 == 0, c == HC - 1,
                              skip_group_check=True)
                ins.then_inc(y_used, 1)

            inputs(0, 0)
            queries(0, 0, False)
            iteration(0, False, True, FIRST)
            iteration(0, False, True)
            with pe.Fori(1, PAIRS - 1) as i:
                iteration(i, True, True)
            iteration(PAIRS - 1, True, False)

            for step, j, b, k, early in steps(LAST, PAIRS - 1, True, False):
                attention(step, j, b, k, False, False, False)
                if step == "h":
                    shared_h(j, k)
                if step == "y":
                    shared_y(j, k)
                if (step, k) == ("h", 1):
                    pe.wait_ge(chosen_rdy, 1)
                    pe.wait_ge(empty_made, 2)
                    mm(bank[3][:, 64:64 + TILES], before[:, :], chosen[:, :], True, True)
                    mm(bank[3][:, 128:128 + TILES], ones[:, :], chosen[:, :], True, True).then_inc(counts_ps, 1)
            pe.wait_ge(rb_cut, 1)
            pe.wait_ge(places_rdy, 1)
            for e in range(EXPERTS):
                pe.wait_ge(w_lo, 4 + 2 * e)
                for c in range(HC):
                    ins = cut(bank[3][:, e * DIM:(e + 1) * DIM],
                              lambda m: relu_b1p[m][:, e, c:c + 1].to_broadcast([P, P]),
                              lambda m: ew2_sb[m][:, e, c, :], c == 0, c == HC - 1)
                ins.then_inc(other_ps, 1)

            def sorted_transposed(j):
                pe.wait_ge(xs_in, 16 * (j + 1))
                pe.wait_ge(xsT_lo, j)
                for kc in range(KC):
                    for t in range(RT):
                        ins = nc.tensor.transpose(bank[2][:, kc * RTOK + t * P:kc * RTOK + (t + 1) * P],
                                                  xs[:, t, kc * P:(kc + 1) * P], ident[:, :])
                ins.then_inc(xsT_ps, 1)

            pe.wait_ge(y_out, PAIRS)
            sorted_transposed(0)
            pe.wait_ge(seam_rdy, 1)
            tiles_of_0 = pe.value_load(tiles0_int[0:1, 0:1], min_val=1, max_val=RTILES - 1)

            def routed(j, e):
                q = PAIRS * HC + j * HC
                pe.wait_ge(xsT_lo, j + 1)
                for n in range(HC + 2):
                    if n < HC:
                        pe.wait_ge(h_32, q + n - 3)
                        for kc in range(KC):
                            ins = cut(hidden_bank(n % 4)[:, 0:RTOK], lambda m: ew1_sb[m][:, e, kc, n * P:(n + 1) * P],
                                      lambda m: xsT[m][:, bass.ds(j % 2, 1), kc, :].rearrange("p o s -> p (o s)"),
                                      kc == 0, kc == KC - 1)
                        ins.then_inc(h_in_ps, 1)
                    if n == 6:
                        sorted_transposed(j + 1)
                    if n >= 2:
                        c = n - 2
                        pe.wait_ge(h_lo, q + c + 1)
                        if c == 0:
                            pe.wait_ge(final_rdy, j)
                        for t in range(RT):
                            ins = cut(y_ps[:, t, :], lambda m: hT[m][:, c % HB, t * P:(t + 1) * P],
                                      lambda m: ew2_sb[m][:, e, c, :], c == 0 and t == 0, c == HC - 1,
                                      skip_group_check=True)
                        ins.then_inc(y_used, 1)

            with pe.Fori(0, tiles_of_0) as j:
                routed(j, 0)
            with pe.Fori(tiles_of_0, RTILES) as j:
                routed(j, 1)


_INS = ["x", "ctx_768", "g_xattn", "g_ffn", "L0_xattn_wq", "L0_xattn_bq", "L0_xattn_wk", "L0_xattn_bk",
        "L0_xattn_wv", "L0_xattn_bv", "L0_xattn_wo", "L0_xattn_bo", "L0_ffn_gate_w", "L0_ffn_w1", "L0_ffn_b1",
        "L0_ffn_w2", "L0_ffn_b2", "L0_ffn_sw1", "L0_ffn_sb1", "L0_ffn_sw2", "L0_ffn_sb2"]


def kernel(**inputs):
    import numpy as np
    from concourse import bacc
    from concourse.bass_utils import run_bass_kernel_spmd

    nc = bacc.Bacc("TRN2", target_bir_lowering=False, num_devices=1)
    arrays, args = {}, []
    for name in _INS:
        a = np.ascontiguousarray(inputs[name])
        arrays[f"in_{name}"] = a
        args.append(nc.dram_tensor(f"in_{name}", a.shape, mybir.dt.from_np(a.dtype), kind="ExternalInput").ap())
    out = nc.dram_tensor("out", (TOKENS, DIM), F32, kind="ExternalOutput").ap()
    build(nc, *args, out)
    r = run_bass_kernel_spmd(nc, [arrays], core_ids=[0])
    return r.results[0]["out"].reshape(BATCHES, SEQ, DIM)
```

```python
from contextlib import ExitStack

import concourse.bass as bass
from concourse import mybir

F32 = mybir.dt.float32
F32R = mybir.dt.float32r
I32 = mybir.dt.int32
U32 = mybir.dt.uint32
ALU = mybir.AluOpType
ACT = mybir.ActivationFunctionType
AX_X = mybir.AxisListType.X

P = 128
BATCHES, SEQ, DIM = 8, 256, 256
KEYS, CROSS = 77, 192
HEADS = 16
HEAD_DIM = DIM // HEADS
HIDDEN = 1024
EXPERTS = 2
EPS = 1e-5
ROOT_MAGIC = 0x5F3759DF
NEWTON = 3
ROOT_OPS = 3 + 3 * NEWTON
TOKENS = BATCHES * SEQ
TILES = TOKENS // P
TB = SEQ // P
KC = DIM // P
GROUPS = KC
HG = HEADS // GROUPS
GK = HG * KEYS
HALF = GK // 2
HH = HG // 2
CHUNKS = -(-GK // P)
TURNS = [(0, 1), (2, 3), (4,)]
ROWS = [min(P, GK - c * P) for c in range(CHUNKS)]
PAIRS = BATCHES // 2
TP = 2 * TB
PTOK = TP * P
CK = 96
CKC = CROSS // CK
HC = HIDDEN // P
HB = 4
YH = 4 * KEYS
RT = 2
RTOK = RT * P
RTILES = TOKENS // RTOK + 1
SLOTS = RTILES * RTOK
ROW = DIM + 1
V_B1 = 2 * GROUPS
V_GATE = V_B1 + (1 + EXPERTS) * HC
VECS = V_GATE + EXPERTS * KC
NO_TOKEN = 1 << 14

START = [("scores", 0, 0, 0), ("soft", 0, 0, 0), ("exp", 0, 0, 0), ("in", 0, 1, 0), ("scores", 0, 0, 1),
         ("soft", 0, 0, 1), ("exp", 0, 0, 1), ("query", 0, 1, 0), ("scores", 0, 0, 2), ("soft", 0, 0, 2),
         ("exp", 0, 0, 2), ("norm", 1, 0, 0), ("scores", 0, 0, 3), ("soft", 0, 0, 3), ("in", 1, 0, 0),
         ("exp", 0, 0, 3), ("sums", 0, 0, 3), ("scores", 0, 1, 0), ("soft", 0, 1, 0), ("query", 1, 0, 0),
         ("exp", 0, 1, 0), ("turn", 0, 0, 0), ("scores", 0, 1, 1), ("turn", 0, 0, 1), ("soft", 0, 1, 1),
         ("exp", 0, 1, 1), ("norm", 1, 1, 0), ("turn", 0, 0, 2), ("bias", 0, 0, 0), ("bias", 0, 1, 0),
         ("scores", 0, 1, 2), ("soft", 0, 1, 2), ("exp", 0, 1, 2), ("stats", 0, 0, 2), ("values", 0, 0, 0),
         ("in", 1, 1, 0), ("scores", 0, 1, 3), ("soft", 0, 1, 3), ("exp", 0, 1, 3), ("cut", 0, 0, 0),
         ("query", 1, 1, 0), ("sums", 0, 1, 3), ("out", 0, 0, 0), ("scores", 1, 0, 0), ("soft", 1, 0, 0),
         ("exp", 1, 0, 0), ("turn", 0, 1, 0), ("scores", 1, 0, 1), ("soft", 1, 0, 1), ("exp", 1, 0, 1),
         ("turn", 0, 1, 1), ("scores", 1, 0, 2), ("soft", 1, 0, 2), ("exp", 1, 0, 2), ("turn", 0, 1, 2),
         ("scores", 1, 0, 3), ("soft", 1, 0, 3), ("exp", 1, 0, 3), ("sums", 1, 0, 3), ("stats", 0, 0, 3),
         ("values", 0, 1, 0), ("out", 0, 1, 0), ("bias", 1, 0, 0), ("bias", 1, 1, 0), ("turn", 1, 0, 0),
         ("root", 0, 0, 0), ("turn", 1, 0, 1), ("turn", 1, 0, 2), ("cut", 0, 0, 1)]
ORDER = [("scores", 0, 1, 0), ("soft", 0, 1, 0), ("exp", 0, 1, 0), ("values", 0, 0, 0), ("norm2", -1, 0, 0),
         ("scores", 0, 1, 1), ("norm2", -1, 0, 1), ("soft", 0, 1, 1), ("exp", 0, 1, 1), ("norm", 1, 0, 0),
         ("out", 0, 0, 0), ("gate", -1, 0, 0), ("h", -1, 0, 0), ("scores", 0, 1, 2), ("gate_turn", -1, 0, 0),
         ("soft", 0, 1, 2), ("h", -1, 0, 1), ("exp", 0, 1, 2), ("in", 1, 0, 0), ("h", -1, 0, 2), ("y", -1, 0, 0),
         ("scores", 0, 1, 3), ("soft", 0, 1, 3), ("h", -1, 0, 3), ("query", 1, 0, 0), ("exp", 0, 1, 3),
         ("sums", 0, 1, 3), ("y", -1, 0, 1), ("h", -1, 0, 4), ("scores", 1, 0, 0), ("soft", 1, 0, 0),
         ("turn", 0, 1, 0), ("exp", 1, 0, 0), ("y", -1, 0, 2), ("turn", 0, 1, 1), ("scores", 1, 0, 1),
         ("soft", 1, 0, 1), ("turn", 0, 1, 2), ("exp", 1, 0, 1), ("h", -1, 0, 5), ("norm", 1, 1, 0),
         ("values", 0, 1, 0), ("scores", 1, 0, 2), ("soft", 1, 0, 2), ("exp", 1, 0, 2), ("y", -1, 0, 3),
         ("out", 0, 1, 0), ("h", -1, 0, 6), ("in", 1, 1, 0), ("scores", 1, 0, 3), ("soft", 1, 0, 3),
         ("y", -1, 0, 4), ("query", 1, 1, 0), ("exp", 1, 0, 3), ("sums", 1, 0, 3), ("h", -1, 0, 7),
         ("bias", 1, 0, 0), ("bias", 1, 1, 0), ("root", 0, 0, 0), ("turn", 1, 0, 0), ("y", -1, 0, 5),
         ("turn", 1, 0, 1), ("y", -1, 0, 6), ("turn", 1, 0, 2), ("y", -1, 0, 7)]
END = [("scores", 0, 1, 0), ("soft", 0, 1, 0), ("exp", 0, 1, 0), ("values", 0, 0, 0), ("norm2", -1, 0, 0),
       ("scores", 0, 1, 1), ("norm2", -1, 0, 1), ("soft", 0, 1, 1), ("exp", 0, 1, 1), ("out", 0, 0, 0),
       ("gate", -1, 0, 0), ("scores", 0, 1, 2), ("soft", 0, 1, 2), ("exp", 0, 1, 2), ("h", -1, 0, 0),
       ("gate_turn", -1, 0, 0), ("h", -1, 0, 1), ("scores", 0, 1, 3), ("soft", 0, 1, 3), ("exp", 0, 1, 3),
       ("sums", 0, 1, 3), ("h", -1, 0, 2), ("turn", 0, 1, 0), ("y", -1, 0, 0), ("h", -1, 0, 3), ("y", -1, 0, 1),
       ("turn", 0, 1, 1), ("h", -1, 0, 4), ("y", -1, 0, 2), ("turn", 0, 1, 2), ("h", -1, 0, 5), ("values", 0, 1, 0),
       ("y", -1, 0, 3), ("out", 0, 1, 0), ("root", 0, 0, 0), ("h", -1, 0, 6), ("y", -1, 0, 4), ("h", -1, 0, 7),
       ("y", -1, 0, 5), ("norm2", 0, 0, 0), ("norm2", 0, 0, 1), ("y", -1, 0, 6), ("y", -1, 0, 7), ("gate", 0, 0, 0),
       ("h", 0, 0, 0), ("gate_turn", 0, 0, 0), ("h", 0, 0, 1), ("count", 0, 0, 0), ("h", 0, 0, 2), ("y", 0, 0, 0),
       ("h", 0, 0, 3), ("y", 0, 0, 1), ("h", 0, 0, 4), ("y", 0, 0, 2), ("h", 0, 0, 5), ("y", 0, 0, 3),
       ("h", 0, 0, 6), ("y", 0, 0, 4), ("h", 0, 0, 7), ("y", 0, 0, 5), ("y", 0, 0, 6), ("y", 0, 0, 7)]
CUT_AFTER = {1: (0, 0), 2: (0, 1), 4: (1, 0), 6: (1, 1)}


def value_pieces():
    for h in range(HG):
        k = 0
        while k < KEYS:
            row = h * KEYS + k
            n = min(KEYS - k, P - row % P)
            yield h, k, k + n, row // P, row % P
            k += n


PIECES = list(value_pieces())


def steps(order, i, prev, ahead):
    for step, d, b, k in order:
        if (prev or d >= 0) and (ahead or d <= 0):
            yield step, (i if d == 0 else i + 1 if d > 0 else i - 1), b, k, not prev and d == 0


def is_last(j):
    return isinstance(j, int) and j == PAIRS - 1


def build(nc, x, ctx_768, g_xattn, g_ffn, wq, bq, wk, bk, wv, bv, wo, bo,
          gate_w, w1, b1, w2, b2, sw1, sb1, sw2, sb2, out):
    values_dram = nc.dram_tensor("values_dram", (BATCHES, KEYS, DIM), F32).ap()
    sorted_dram = nc.dram_tensor("sorted_dram", (SLOTS + RTOK, ROW), F32).ap()
    part_dram = nc.dram_tensor("part_dram", (TOKENS, DIM), F32).ap()

    def tiled(rows):
        return rows.rearrange("(t p) d -> p t d", p=P)

    x_rows = tiled(x.rearrange("b s d -> (b s) d"))

    ctx = ExitStack()
    with ctx:
        def sem(name):
            return ctx.enter_context(nc.semaphore(name))

        def sb(name, shape, dt=F32, scope=ctx):
            return scope.enter_context(nc.sbuf_tensor(name, shape, dt))

        x_all = sb("x_all", [P, TILES, DIM])
        xn2_all = sb("xn2_all", [P, TILES, ROW])
        x2T = [sb(f"x2T_{n}", [P, KC, PTOK], F32R) for n in ("hi", "lo")]
        h32 = sb("h32", [P, 2, PTOK])
        context = ExitStack()
        v_sb = sb("v_sb", [KEYS, BATCHES, DIM], scope=context)
        context.close()
        hT = [sb(f"hT_{n}", [P, HB, PTOK], F32R) for n in ("hi", "lo")]
        sw1_sb = [sb(f"sw1_{n}", [P, KC, HIDDEN], F32R) for n in ("hi", "lo")]
        sw2_sb = [sb(f"sw2_{n}", [P, HC, DIM], F32R) for n in ("hi", "lo")]
        stage = sb("stage", [P, 2, KC * HIDDEN])
        ident = sb("ident", [P, P])
        gains = sb("gains", [P, 2])
        vec_rows = sb("vec_rows", [VECS, P])
        vec_cols = sb("vec_cols", [P, VECS])
        bq_sb = vec_cols[:, 0:GROUPS]
        bk_sb = vec_cols[:, GROUPS:2 * GROUPS]
        b1_sb = vec_cols[:, V_B1:V_GATE].rearrange("p (m c) -> p m c", c=HC)
        gw32 = vec_cols[:, V_GATE:VECS].rearrange("p (e k) -> p e k", e=EXPERTS)
        gw = [sb(f"gw_{n}", [P, EXPERTS, KC], F32R) for n in ("hi", "lo")]
        fill = sb("fill", [P, 1])
        bias_rows = sb("bias_rows", [P, 2, DIM])
        stats = sb("stats", [P, TILES, 6])
        mv = sb("mv", [P, TILES, 2])
        rstd = sb("rstd", [P, TILES])
        nt = sb("nt", [P, 2, TILES])
        stats2 = sb("stats2", [P, TP, 6])
        mv2 = sb("mv2", [P, TP, 2])
        rstd2 = sb("rstd2", [P, TP])
        nt2 = sb("nt2", [P, 2, TP])
        gate_rows = sb("gate_rows", [EXPERTS, PTOK])
        gate_sb = sb("gate_sb", [P, TILES, EXPERTS])
        before = sb("before", [P, P])
        ones = sb("ones", [P, P])
        seams = sb("seams", [P, RTILES - 2])
        number = sb("number", [P, TILES])
        zero_tile = sb("zero_tile", [P, TILES])
        empty_rows = sb("empty_rows", [P, RT, ROW])
        relu_b1 = sb("relu_b1", [P, EXPERTS, HC])
        relu_b1p = [sb(f"relu_b1_{n}", [P, EXPERTS, HC], F32R) for n in ("hi", "lo")]

        chosen = sb("chosen", [P, TILES])
        tile_sum = sb("tile_sum", [P, TILES])
        prefix = sb("prefix", [P, TILES])
        rank1 = sb("rank1", [P, TILES])
        count0 = sb("count0", [P, 1])
        past = sb("past", [P, RTILES - 2])
        tiles0 = sb("tiles0", [P, 1])
        tiles0_int = sb("tiles0_int", [P, 1], I32)
        base1 = sb("base1", [P, 1])
        rank0 = sb("rank0", [P, TILES])
        moved = sb("moved", [P, TILES])
        place = sb("place", [P, TILES])
        place_int = sb("place_int", [P, TILES], U32)

        att = ExitStack()
        wqo_sb = [sb(f"wqo_{n}", [P, 2, KC, DIM], F32R, scope=att) for n in ("hi", "lo")]
        bv_row = sb("bv_row", [KEYS, DIM], scope=att)
        kT = sb("kT", [P, GROUPS, BATCHES * KEYS], scope=att)
        k_diag = sb("k_diag", [P, 2, GROUPS, GK], scope=att)
        v_diag = sb("v_diag", [P, 2, GROUPS, CHUNKS, P], scope=att)
        xn = sb("xn", [P, 2, TB, DIM], scope=att)
        xnT = [sb(f"xnT_{n}", [P, KC, SEQ], F32R, scope=att) for n in ("hi", "lo")]
        qT = sb("qT", [P, 2, GROUPS, SEQ], scope=att)
        context = ExitStack()
        wk_sb = sb("wk_sb", [CK, CKC, DIM], scope=context)
        y_sb = sb("y_sb", [KEYS, BATCHES, CROSS], scope=context)
        context.close()
        probs = sb("probs", [P, 2, 4, GK], scope=att)
        context = ExitStack()
        wv_sb = sb("wv_sb", [CK, CKC, DIM], scope=context)
        yT = sb("yT", [CK, CKC, BATCHES * KEYS], scope=context)
        context.close()
        pT = sb("pT", [P, GROUPS * CHUNKS, SEQ], scope=att)
        oT = [sb(f"oT_{n}", [P, GROUPS, SEQ], F32R, scope=att) for n in ("hi", "lo")]
        xn2 = sb("xn2", [P, TP, DIM], scope=att)
        smax = sb("smax", [P, 2, 4, HG], scope=att)
        rsum = sb("rsum", [P, 2, 4, HG], scope=att)
        rinv = sb("rinv", [P, 2, 4, HG], scope=att)
        att.close()

        ew1_sb = [sb(f"ew1_{n}", [P, EXPERTS, KC, HIDDEN], F32R) for n in ("hi", "lo")]
        ew2_sb = [sb(f"ew2_{n}", [P, EXPERTS, HC, DIM], F32R) for n in ("hi", "lo")]
        xs = sb("xs", [P, RT, ROW])
        xsT = [sb(f"xsT_{n}", [P, 2, KC, RTOK], F32R) for n in ("hi", "lo")]
        gather_token = sb("gather_token", [P, RT], U32)
        scatter_token = sb("scatter_token", [P, RT], U32)
        part = sb("part", [P, RT, DIM])
        final = sb("final", [P, RT, DIM])
        other_row = sb("other_row", [P, EXPERTS, DIM])

        bank = [ctx.enter_context(nc.psum_tensor(f"bank{n}", [P, 512], F32)) for n in range(4)]
        h_ps = ctx.enter_context(nc.psum_tensor("h_ps", [P, 2, 512], F32))
        y_ps = ctx.enter_context(nc.psum_tensor("y_ps", [P, TP, DIM], F32))

        consts_made = sem("consts_made")
        x_in = [sem(f"x_in{n}") for n in range(3)]
        wo_in = sem("wo_in")
        wqo_hi = sem("wqo_hi")
        wqo_lo = sem("wqo_lo")
        empty_made = sem("empty_made")
        stats2_rdy = sem("stats2_rdy")
        newton = sem("newton")
        scatter_ids = sem("scatter_ids")
        small_in = sem("small_in")
        bv_in = sem("bv_in")
        wk_in = sem("wk_in")
        wv_in = sem("wv_in")
        wq_in = sem("wq_in")
        context_in = sem("context_in")
        vecs_in = sem("vecs_in")
        vecs_ps = sem("vecs_ps")
        vecs_rdy = sem("vecs_rdy")
        stage_in = [sem(f"stage_in{n}") for n in range(2)]
        gains_ready = sem("gains_ready")
        biases = sem("biases")
        rows_ready = sem("rows_ready")
        yT_ps = sem("yT_ps")
        yT_sb = sem("yT_sb")
        kT_ps = sem("kT_ps")
        kT_sb = sem("kT_sb")
        v_ps = sem("v_ps")
        v_rdy = sem("v_rdy")
        v_out = [sem(f"v_out{n}") for n in range(2)]
        cleared = sem("cleared")
        dve_chain = sem("dve_chain")
        var_ready = sem("var_ready")
        w_hi = sem("w_hi")
        w_lo = sem("w_lo")
        gw_cut = sem("gw_cut")
        k_in = [sem(f"k_in{n}") for n in range(2)]
        v_in = [sem(f"v_in{n}") for n in range(2)]
        xn_ready = sem("xn_ready")
        x_biased = sem("x_biased")
        xnT_ps = sem("xnT_ps")
        xnT_hi = sem("xnT_hi")
        xnT_lo = sem("xnT_lo")
        q_ps = sem("q_ps")
        q_sb = sem("q_sb")
        s_ps = sem("s_ps")
        s_max = sem("s_max")
        s_shifted = sem("s_shifted")
        p_exp = sem("p_exp")
        p_sum = sem("p_sum")
        p_rinv = sem("p_rinv")
        p_ready = sem("p_ready")
        pT_ps = sem("pT_ps")
        pT_sb = sem("pT_sb")
        o_ps = sem("o_ps")
        o_hi = sem("o_hi")
        o_lo = sem("o_lo")
        proj_ps = sem("proj_ps")
        x1_ready = sem("x1_ready")
        var2_ready = sem("var2_ready")
        xn2_ready = sem("xn2_ready")
        xn2_kept = sem("xn2_kept")
        x1_biased = sem("x1_biased")
        x2T_ps = sem("x2T_ps")
        x2T_hi = sem("x2T_hi")
        x2T_lo = sem("x2T_lo")
        gate_ps = sem("gate_ps")
        gate_copied = sem("gate_copied")
        gate_turned = sem("gate_turned")
        gate_rdy = sem("gate_rdy")
        h_in_ps = sem("h_in_ps")
        h_hi = sem("h_hi")
        h_32 = sem("h_32")
        h_lo = sem("h_lo")
        y_used = sem("y_used")
        y_out = sem("y_out")
        part_out = sem("part_out")
        filled = sem("filled")
        chosen_rdy = sem("chosen_rdy")
        counts_ps = sem("counts_ps")
        places_rdy = sem("places_rdy")
        scattered = sem("scattered")
        seam_rdy = sem("seam_rdy")
        rb_cut = sem("rb_cut")
        other_ps = sem("other_ps")
        other_rdy = sem("other_rdy")
        xs_in = sem("xs_in")
        ids_copied = sem("ids_copied")
        xsT_ps = sem("xsT_ps")
        xsT_hi = sem("xsT_hi")
        xsT_lo = sem("xsT_lo")
        gathered = sem("gathered")
        part_rdy = sem("part_rdy")
        final_rdy = sem("final_rdy")
        rows_out = sem("rows_out")
        iotas = sem("iotas")

        def by_head(rows):
            return rows.rearrange("p (h k) -> p h k", k=KEYS)

        def hidden_bank(n):
            return h_ps[:, n, :] if n < 2 else bank[n - 2]

        def keys_bank(half, g):
            bank_rows = h_ps[:, half, :] if g == 0 else y_ps[:, 2 * half:2 * half + 2, :].rearrange("p a d -> p (a d)")
            return bank_rows[:, 0:YH]

        block = ctx.enter_context(nc.Block())

        @block.sync
        def _(sp):
            sp.dma_start(y_sb[:, :, :], ctx_768.rearrange("b s d -> s b d")).then_inc(context_in, 16)
            sp.dma_start(wk_sb[:, :, :], wk.rearrange("(k p) d -> p k d", p=CK)).then_inc(wk_in, 16)
            at = 0
            for vec in (bq, bk, sb1, b1.rearrange("e h -> (e h)"), gate_w.rearrange("e d -> (e d)")):
                n = vec.shape[0] // P
                sp.dma_start(vec_rows[at:at + n, :], vec.rearrange("(n p) -> n p", p=P)).then_inc(vecs_in, 16)
                at += n
            sp.dma_start(x_all[:, 0:TP, :], x_rows[:, 0:TP, :]).then_inc(x_in[0], 16)
            wqo = stage[:, 0, 0:2 * KC * DIM].rearrange("p (w k d) -> p w k d", w=2, k=KC)
            sp.dma_start(wqo[:, 0], wq.rearrange("(k p) d -> p k d", p=P)).then_inc(wq_in, 16)
            sp.dma_start(x_all[:, TP:2 * TP, :], x_rows[:, TP:2 * TP, :]).then_inc(x_in[1], 16)
            sp.dma_start(wv_sb[:, :, :], wv.rearrange("(k p) d -> p k d", p=CK)).then_inc(wv_in, 16)
            sp.dma_start(wqo[:, 1], wo.rearrange("(k p) d -> p k d", p=P)).then_inc(wo_in, 16)
            sp.dma_start(x_all[:, 2 * TP:TILES, :], x_rows[:, 2 * TP:TILES, :]).then_inc(x_in[2], 16)

            def keys_diagonal(i, b):
                for h in range(HG):
                    rows = slice(h * HEAD_DIM, (h + 1) * HEAD_DIM)
                    sp.dma_start(k_diag[rows, b, :, h * KEYS:(h + 1) * KEYS],
                                 kT[rows, :, bass.ds((2 * i + b) * KEYS, KEYS)]).then_inc(k_in[b], 16)

            def values_diagonal(i, b):
                for h, k0, k1, c, p0 in PIECES:
                    cols = slice(h * HEAD_DIM, (h + 1) * HEAD_DIM)
                    src = values_dram[bass.ds(2 * i + b, 1), k0:k1, :].rearrange("o k (g f) -> k (o g) f", g=GROUPS)
                    sp.dma_start(v_diag[p0:p0 + k1 - k0, b, :, c, cols], src[:, :, cols]).then_inc(v_in[b], 16)

            sp.wait_ge(kT_sb, GROUPS)
            sp.wait_ge(cleared, 1)
            for b in range(2):
                keys_diagonal(0, b)
            sp.wait_ge(v_rdy, 2)
            sp.dma_start(values_dram[0:2].rearrange("b k d -> k b d"), v_sb[:, 0:2, :]).then_inc(v_out[0], 16)
            sp.wait_ge(cleared, 2)
            sp.wait_ge(v_out[0], 16)
            for b in range(2):
                values_diagonal(0, b)
            sp.wait_ge(v_rdy, BATCHES)
            sp.dma_start(values_dram[2:BATCHES].rearrange("b k d -> k b d"), v_sb[:, 2:BATCHES, :]
                         ).then_inc(v_out[1], 16)
            sp.wait_ge(wqo_lo, 2)
            sp.dma_start(stage[:, 0, :].rearrange("p (k h) -> p k h", k=KC),
                         sw1.rearrange("(k p) h -> p k h", p=P)).then_inc(stage_in[0], 16)
            sp.dma_start(stage[:, 1, :].rearrange("p (c d) -> p c d", c=HC),
                         sw2.rearrange("(c p) d -> p c d", p=P)).then_inc(stage_in[1], 16)
            x_out = tiled(part_dram)

            def keep_xn2(i):
                sp.wait_ge(xn2_ready, i + 1)
                sp.dma_start(xn2_all[:, bass.ds(i * TP, TP), 0:DIM], xn2[:, :, :]).then_inc(xn2_kept, 16)

            def store_part(j):
                sp.wait_ge(y_out, j + 1)
                sp.dma_start(x_out[:, bass.ds(j * TP, TP), :], x_all[:, bass.ds(j * TP, TP), :]
                             ).then_inc(part_out, 16)

            def iteration(i, prev, ahead):
                if not prev:
                    sp.wait_ge(kT_sb, 2 * GROUPS)
                if ahead:
                    sp.wait_ge(s_ps, (2 * i + 1) * 8)
                    keys_diagonal(i + 1, 0)
                if prev:
                    keep_xn2(i - 1)
                if not prev:
                    sp.wait_ge(v_out[1], 16)
                if ahead:
                    sp.wait_ge(o_ps, 2 * i + 1)
                    values_diagonal(i + 1, 0)
                    sp.wait_ge(s_ps, (2 * i + 2) * 8)
                    keys_diagonal(i + 1, 1)
                    sp.wait_ge(o_ps, 2 * i + 2)
                    values_diagonal(i + 1, 1)
                if prev:
                    store_part(i - 1)

            iteration(0, False, True)
            sp.wait_ge(empty_made, 2)
            for j in range(RTILES + 1):
                rows = sorted_dram[j * RTOK:(j + 1) * RTOK, :].rearrange("(t p) d -> p t d", p=P)
                sp.dma_start(rows, empty_rows[:, :, :]).then_inc(filled, 16)
            sp.wait_ge(w_lo, 1)
            sp.dma_start(stage[:, 0, :].rearrange("p (k h) -> p k h", k=KC),
                         w1[0].rearrange("(k p) h -> p k h", p=P)).then_inc(stage_in[0], 16)
            sp.wait_ge(w_lo, 2)
            sp.dma_start(stage[:, 1, :].rearrange("p (c d) -> p c d", c=HC),
                         w2[0].rearrange("(c p) d -> p c d", p=P)).then_inc(stage_in[1], 16)
            with sp.Fori(1, PAIRS - 1) as i:
                iteration(i, True, True)
            keep_xn2(PAIRS - 2)
            keep_xn2(PAIRS - 1)
            store_part(PAIRS - 2)
            sp.wait_ge(w_lo, 3)
            sp.dma_start(stage[:, 0, :].rearrange("p (k h) -> p k h", k=KC),
                         w1[1].rearrange("(k p) h -> p k h", p=P)).then_inc(stage_in[0], 16)
            sp.wait_ge(w_lo, 4)
            sp.dma_start(stage[:, 1, :].rearrange("p (c d) -> p c d", c=HC),
                         w2[1].rearrange("(c p) d -> p c d", p=P)).then_inc(stage_in[1], 16)

            def load_sorted(j):
                rows = sorted_dram[bass.ds(j * RTOK, RTOK), :].rearrange("(t p) d -> p t d", p=P)
                sp.dma_start(xs[:, :, :], rows).then_inc(xs_in, 16)

            sp.wait_ge(scattered, 16 * TILES)
            load_sorted(0)
            store_part(PAIRS - 1)
            sp.wait_ge(seam_rdy, 1)
            tiles_of_0 = sp.value_load(tiles0_int[0:1, 0:1], min_val=1, max_val=RTILES - 1)

            def routed(j):
                sp.wait_ge(xsT_ps, j + 1)
                sp.wait_ge(ids_copied, j + 1)
                load_sorted(j + 1)

            with sp.Fori(0, tiles_of_0) as j:
                routed(j)
            with sp.Fori(tiles_of_0, RTILES) as j:
                routed(j)
            sp.wait_ge(xs_in, 16 * (RTILES + 1))

        @block.gpsimd
        def _(pool):
            nc.gpsimd.memset(ident[:, :], 0.0).then_inc(iotas, 1)
            pool.wait_ge(iotas, 1)
            nc.gpsimd.affine_select(out=ident[:, :], in_=ident[:, :], compare_op=ALU.not_equal, fill=1.0, base=0,
                                    pattern=[[-1, P]], channel_multiplier=1).then_inc(consts_made, 1)
            for n, gain in enumerate((g_xattn, g_ffn)):
                pool.dma_start(gains[:, n:n + 1], gain.partition_broadcast(P)).then_inc(small_in, 16)
            pool.dma_start(bv_row[:, :], bv.partition_broadcast(KEYS)).then_inc(bv_in, 16)
            pool.dma_start(bias_rows[:, 0, :], bo.partition_broadcast(P)).then_inc(small_in, 16)
            pool.dma_start(bias_rows[:, 1, :], sb2.partition_broadcast(P)).then_inc(small_in, 16)
            pool.dma_start(h32[:, 0, 0:2 * DIM], b2.rearrange("e d -> (e d)").partition_broadcast(P)
                           ).then_inc(small_in, 16)
            nc.gpsimd.iota(xn2_all[:, :, DIM:ROW].rearrange("p t o -> p (t o)"), pattern=[[P, TILES]], base=0,
                           channel_multiplier=1, allow_small_or_imprecise_dtypes=True).then_inc(iotas, 1)
            nc.gpsimd.memset(k_diag[:, :, :, :], 0.0).then_inc(cleared, 1)
            nc.gpsimd.memset(v_diag[:, :, :, :, :], 0.0).then_inc(cleared, 1)
            nc.gpsimd.memset(ones[:, :], 1.0).then_inc(iotas, 1)
            nc.gpsimd.memset(before[:, :], 1.0).then_inc(iotas, 1)
            nc.gpsimd.memset(zero_tile[:, :], 0.0).then_inc(iotas, 1)
            nc.gpsimd.memset(empty_rows[:, :, :], 0.0).then_inc(iotas, 1)
            nc.gpsimd.iota(seams[:, :], pattern=[[RTOK, RTILES - 2]], base=RTOK, channel_multiplier=0,
                           allow_small_or_imprecise_dtypes=True).then_inc(iotas, 1)
            nc.gpsimd.iota(number[:, :], pattern=[[P, TILES]], base=0, channel_multiplier=1,
                           allow_small_or_imprecise_dtypes=True).then_inc(iotas, 1)
            pool.wait_ge(iotas, 8)
            nc.gpsimd.affine_select(out=before[:, :], in_=before[:, :], compare_op=ALU.is_gt, fill=0.0, base=0,
                                    pattern=[[1, P]], channel_multiplier=-1).then_inc(empty_made, 1)
            nc.gpsimd.iota(empty_rows[:, :, DIM:ROW].rearrange("p t o -> p (t o)"), pattern=[[P, RT]], base=NO_TOKEN,
                           channel_multiplier=1, allow_small_or_imprecise_dtypes=True).then_inc(empty_made, 1)
            pool.wait_ge(small_in, 16 * 5)
            pool.wait_ge(gains_ready, 1)
            for n in range(EXPERTS):
                nc.gpsimd.tensor_tensor(bias_rows[:, 1, :], bias_rows[:, 1, :], h32[:, 0, n * DIM:(n + 1) * DIM],
                                        ALU.add).then_inc(biases, 1)
                pool.wait_ge(biases, n + 1)
            for n in range(2):
                nc.gpsimd.tensor_scalar(bias_rows[:, n, :], bias_rows[:, n, :], gains[:, n:n + 1], None, ALU.mult
                                        ).then_inc(rows_ready, 1)

            def bias_x(i, b, early):
                pool.wait_ge(xn_ready, 2 * i + b + 1)
                if early:
                    pool.wait_ge(rows_ready, 2)
                for t in range(TB):
                    row = x_all[:, bass.ds((2 * i + b) * TB + t, 1), :].rearrange("p o d -> p (o d)")
                    nc.gpsimd.tensor_tensor(row, row, bias_rows[:, 0, :], ALU.add).then_inc(x_biased, 1)

            def iteration(i, prev, ahead, order=ORDER):
                for step, j, b, k, early in steps(order, i, prev, ahead):
                    if step == "bias":
                        bias_x(j, b, early)
                    if step == "exp":
                        pool.wait_ge(p_rinv, (2 * j + b) * 4 + k + 1)
                        pq = by_head(probs[:, b, k, :])
                        nc.gpsimd.tensor_tensor(pq, pq, rinv[:, b, k, :].unsqueeze(2).to_broadcast([P, HG, KEYS]),
                                                ALU.mult).then_inc(p_ready, 1)
                    if step == "cut":
                        hi, lo = ((sw1_sb, sw2_sb)[k][m][:, :, :].rearrange("p k h -> p (k h)") for m in range(2))
                        pool.wait_ge(w_hi, k + 1)
                        nc.gpsimd.tensor_tensor(lo, stage[:, k, :], hi, ALU.subtract).then_inc(w_lo, 1)
                    if step == "y" and k < TP // 2:
                        for t in range(2 * k, 2 * k + 2):
                            bias_x1(j, t)

            def bias_x1(i, t):
                pool.wait_ge(xn2_ready, i + 1)
                row = x_all[:, bass.ds(i * TP + t, 1), :].rearrange("p o d -> p (o d)")
                nc.gpsimd.tensor_tensor(row, row, bias_rows[:, 1, :], ALU.add).then_inc(x1_biased, 1)

            iteration(0, False, True, START)
            with pool.Fori(1, PAIRS - 1) as i:
                iteration(i, True, True)
            iteration(PAIRS - 1, True, False, END)
            pool.wait_ge(x2T_ps, PAIRS * KC)
            pool.wait_ge(xn2_kept, 16 * PAIRS)
            nc.gpsimd.memset(part[:, :, :], 0.0).then_inc(iotas, 1)
            pool.wait_ge(iotas, 9)
            pool.wait_ge(filled, 16 * (RTILES + 1))
            pool.wait_ge(places_rdy, 1)
            for t in range(TILES):
                pool.indirect_dma_start(
                    out=sorted_dram[:, :], out_offset=bass.IndirectOffsetOnAxis(ap=place_int[:, t:t + 1], axis=0),
                    in_=xn2_all[:, t, :], in_offset=None, bounds_check=SLOTS - 1,
                    oob_is_err=False).then_inc(scattered, 16)
            pool.wait_ge(other_rdy, 1)
            pool.wait_ge(part_out, 16 * PAIRS)
            pool.wait_ge(seam_rdy, 1)
            tiles_of_0 = pool.value_load(tiles0_int[0:1, 0:1], min_val=1, max_val=RTILES - 1)

            last_token = pool.to_reg(TOKENS - 1)

            def routed(j, e):
                turn = pool.to_reg(j + 1)
                used = j
                pool.wait_ge(seam_rdy, 1)
                pool.wait_ge(ids_copied, turn)
                pool.wait_ge(final_rdy, used)
                for t in range(RT):
                    pool.indirect_dma_start(
                        out=part[:, t, :], out_offset=None, in_=part_dram[:, :],
                        in_offset=bass.IndirectOffsetOnAxis(ap=gather_token[:, t:t + 1], axis=0),
                        bounds_check=last_token, oob_is_err=False).then_inc(gathered, 16)
                pool.wait_ge(gathered, 32 * (j + 1))
                for t in range(RT):
                    nc.gpsimd.tensor_tensor(part[:, t, :], part[:, t, :], other_row[:, 1 - e, :], ALU.add
                                            ).then_inc(part_rdy, 1)
                pool.wait_ge(seam_rdy, 1)
                pool.wait_ge(final_rdy, turn)
                pool.wait_ge(scatter_ids, turn)
                for t in range(RT):
                    pool.indirect_dma_start(
                        out=out[:, :], out_offset=bass.IndirectOffsetOnAxis(ap=scatter_token[:, t:t + 1], axis=0),
                        in_=final[:, t, :], in_offset=None, bounds_check=last_token,
                        oob_is_err=False).then_inc(rows_out, 16)

            with pool.Fori(0, tiles_of_0) as j:
                routed(j, 0)
            with pool.Fori(tiles_of_0, RTILES) as j:
                routed(j, 1)
            pool.wait_ge(rows_out, 32 * RTILES)

        @block.scalar
        def _(act):
            for n in range(CKC * 2):
                act.wait_ge(yT_ps, n + 1)
                nc.scalar.activation(yT[:, n // 2, (n % 2) * YH:(n % 2 + 1) * YH], bank[n][0:CK, 0:YH],
                                     ACT.Copy).then_inc(yT_sb, 1)
            act.wait_ge(vecs_ps, 1)
            nc.scalar.activation(vec_cols[:, :], bank[0][:, 0:VECS], ACT.Copy).then_inc(vecs_rdy, 1)
            act.wait_ge(vecs_rdy, 1)
            for n, (half, g) in enumerate((half, g) for half in range(2) for g in range(GROUPS)):
                if half == 1:
                    act.wait_ge((wq_in, wo_in)[g], 16)
                    nc.scalar.activation(wqo_sb[0][:, g, :, :].rearrange("p k d -> p (k d)"),
                                         stage[:, 0, g * KC * DIM:(g + 1) * KC * DIM], ACT.Copy).then_inc(wqo_hi, 1)
                act.wait_ge(kT_ps, n + 1)
                nc.scalar.activation(kT[:, g, half * YH:(half + 1) * YH], keys_bank(half, g), ACT.Identity,
                                     bias=bk_sb[:, g:g + 1]).then_inc(kT_sb, 1)

            def hidden(q, c, m, width, start, banks=2):
                act.wait_ge(h_in_ps, q + 1)
                act.wait_ge(y_used, q - HB + 1 if c >= HB else start)
                nc.scalar.activation(hT[0][:, c % HB, 0:width], hidden_bank(c % banks)[:, 0:width], ACT.Relu,
                                     bias=b1_sb[:, m, c:c + 1]).then_inc(h_hi, 1)
                act.wait_ge(h_lo, q - 1 if c >= 2 else start)
                nc.scalar.activation(h32[:, c % 2, 0:width], hidden_bank(c % banks)[:, 0:width], ACT.Relu,
                                     bias=b1_sb[:, m, c:c + 1]).then_inc(h_32, 1)

            def inputs(i, b, start=False):
                act.wait_ge(xnT_ps, 2 * i + b + 1)
                if not start:
                    act.wait_ge(q_ps, 2 * i + b)
                nc.scalar.activation(xnT[0][:, :, :].rearrange("p k s -> p (k s)"), bank[2][:, :], ACT.Copy
                                     ).then_inc(xnT_hi, 1)

            def queries(i, b):
                act.wait_ge(q_ps, 2 * i + b + 1)
                for g in range(GROUPS):
                    nc.scalar.activation(qT[:, b, g, :], bank[3][:, g * SEQ:(g + 1) * SEQ], ACT.Identity,
                                         bias=bq_sb[:, g:g + 1]).then_inc(q_sb, 1)

            def norm2_copy(i, kc):
                act.wait_ge(x2T_ps, KC * i + kc + 1)
                if kc == 0:
                    act.wait_ge(h_in_ps, HC * i)
                nc.scalar.activation(x2T[0][:, kc, :], bank[2 + kc][:, :], ACT.Copy).then_inc(x2T_hi, 1)

            def attention(step, j, b, k, first):
                if step == "turn":
                    for u in TURNS[k]:
                        act.wait_ge(pT_ps, (2 * j + b) * CHUNKS + u + 1)
                        if u == 0 and first:
                            act.wait_ge(v_ps, BATCHES)
                        elif u == 0:
                            act.wait_ge(o_ps, 2 * j + b)
                        for v in range(2):
                            r = ROWS[(2 * u + v) % CHUNKS]
                            nc.scalar.activation(pT[0:r, 2 * u + v, :], bank[2 + u % 2][0:r, v * SEQ:(v + 1) * SEQ],
                                                 ACT.Copy).then_inc(pT_sb, 1)
                if step == "values":
                    act.wait_ge(o_ps, 2 * j + b + 1)
                    if not first:
                        act.wait_ge(proj_ps, 2 * j + b)
                    nc.scalar.activation(oT[0][:, :, :].rearrange("p g s -> p (g s)"), bank[3][:, :], ACT.Copy
                                         ).then_inc(o_hi, 1)
                if step == "norm2":
                    norm2_copy(j, k)
                if step == "gate":
                    act.wait_ge(gate_ps, j + 1)
                    nc.scalar.activation(gate_rows[:, :], bank[3][0:EXPERTS, :], ACT.Copy).then_inc(gate_copied, 1)
                if step == "gate_turn":
                    act.wait_ge(gate_turned, j + 1)
                    nc.scalar.activation(
                        gate_sb[:, bass.ds(j * TP, TP), :].rearrange("p t e -> p (t e)"),
                        bank[3][:, 0:TP * EXPERTS], ACT.Copy).then_inc(gate_rdy, 1)

            def iteration(i, prev, ahead, order=ORDER):
                for step, j, b, k, early in steps(order, i, prev, ahead):
                    if step == "in":
                        inputs(j, b)
                    if step == "query":
                        queries(j, b)
                    attention(step, j, b, k, early and b == 0)
                    if step == "exp":
                        act.wait_ge(s_shifted, ((2 * j + b) * 4 + k + 1) * 2)
                        nc.scalar.activation(probs[:, b, k, :], probs[:, b, k, :], ACT.Exp,
                                             scale=HEAD_DIM ** -0.5).then_inc(p_exp, 1)
                    if step == "cut":
                        act.wait_ge(stage_in[k], 16)
                        hi = (sw1_sb, sw2_sb)[k][0][:, :, :].rearrange("p k h -> p (k h)")
                        nc.scalar.activation(hi, stage[:, k, :], ACT.Copy).then_inc(w_hi, 1)
                    if step == "h":
                        hidden(j * HC + k, k, 0, PTOK, j * HC)
                        if is_last(j) and k in CUT_AFTER:
                            expert_hi(*CUT_AFTER[k])

            def expert_hi(e, n):
                if (e, n) == (0, 0):
                    act.wait_ge(xn2_kept, 16 * PAIRS)
                act.wait_ge(stage_in[n], 16 * (2 + e))
                hi = (ew1_sb[0][:, e, :, :], ew2_sb[0][:, e, :, :])[n].rearrange("p k h -> p (k h)")
                nc.scalar.activation(hi, stage[:, n, :], ACT.Copy).then_inc(w_hi, 1)

            inputs(0, 0, True)
            queries(0, 0)
            act.wait_ge(small_in, 16 * 5)
            nc.scalar.activation(gains[:, :], gains[:, :], ACT.Tanh).then_inc(gains_ready, 1)
            iteration(0, False, True, START)
            with act.Fori(1, PAIRS - 1) as i:
                iteration(i, True, True)
            iteration(PAIRS - 1, True, False, END)

            def sorted_hi(j):
                act.wait_ge(xsT_ps, j + 1)
                nc.scalar.activation(xsT[0][:, bass.ds(j % 2, 1), :, :].rearrange("p o k s -> p (o k s)"),
                                     bank[2][:, :], ACT.Copy).then_inc(xsT_hi, 1)

            sorted_hi(0)
            act.wait_ge(other_ps, EXPERTS)
            nc.scalar.activation(other_row[:, :, :].rearrange("p e d -> p (e d)"), bank[3][:, :], ACT.Copy,
                                 scale=gains[:, 1:2]).then_inc(other_rdy, 1)
            act.wait_ge(seam_rdy, 1)
            tiles_of_0 = act.value_load(tiles0_int[0:1, 0:1], min_val=1, max_val=RTILES - 1)

            def routed(j, e):
                for c in range(HC):
                    hidden(PAIRS * HC + j * HC + c, c, 1 + e, RTOK, PAIRS * HC + j * HC, banks=4)
                    if c == 6:
                        sorted_hi(j + 1)

            with act.Fori(0, tiles_of_0) as j:
                routed(j, 0)
            with act.Fori(tiles_of_0, RTILES) as j:
                routed(j, 1)

        @block.vector
        def _(dve):
            chain = [0]

            def link(ins):
                chain[0] += 1
                ins.then_inc(dve_chain, 1)
                dve.wait_ge(dve_chain, chain[0])

            def root(var, r, v, t):
                yield nc.vector.tensor_scalar(v, var, EPS, None, ALU.add)
                yield nc.vector.tensor_scalar(t.bitcast(I32), v.bitcast(I32), 1, None, ALU.logical_shift_right)
                yield nc.vector.tensor_scalar(r.bitcast(I32), t.bitcast(I32), -1, ROOT_MAGIC, ALU.mult, ALU.add)
                for _ in range(NEWTON):
                    yield nc.vector.tensor_tensor(t, v, r, ALU.mult)
                    yield nc.vector.scalar_tensor_tensor(out=t, in0=t, scalar=-0.5, in1=r, op0=ALU.mult, op1=ALU.mult)
                    yield nc.vector.scalar_tensor_tensor(out=r, in0=t, scalar=1.5, in1=r, op0=ALU.add, op1=ALU.mult)

            def statistics(n, tiles):
                dve.wait_ge(x_in[n], 16)
                for t in tiles:
                    ins = nc.vector.bn_stats(stats[:, t, :], x_all[:, t, :])
                link(ins)

            def aggregate(tiles):
                for t in tiles:
                    ins = nc.vector.bn_aggr(mv[:, t, :], stats[:, t, :])
                ins.then_inc(var_ready, 1)

            def x_root(n, tiles):
                dve.wait_ge(var_ready, n + 1)
                return root(mv[:, tiles, 1:2].rearrange("p t o -> p (t o)"), rstd[:, tiles],
                            nt[:, 0, tiles], nt[:, 1, tiles])

            def refine(n, tiles):
                for ins in x_root(n, tiles):
                    link(ins)

            def normalise(i, b):
                for t in range(TB):
                    row = x_all[:, bass.ds((2 * i + b) * TB + t, 1), :].rearrange("p o d -> p (o d)")
                    ins = nc.vector.tensor_scalar(
                        xn[:, b, t, :], row,
                        mv[:, bass.ds((2 * i + b) * TB + t, 1), 0:1].rearrange("p t o -> p (t o)"),
                        rstd[:, bass.ds((2 * i + b) * TB + t, 1)], ALU.subtract, ALU.mult)
                ins.then_inc(xn_ready, 1)

            def cut_wqo(n):
                dve.wait_ge(wqo_hi, n + 1)
                nc.vector.tensor_tensor(wqo_sb[1][:, n, :, :].rearrange("p k d -> p (k d)"),
                                        stage[:, 0, n * KC * DIM:(n + 1) * KC * DIM],
                                        wqo_sb[0][:, n, :, :].rearrange("p k d -> p (k d)"), ALU.subtract
                                        ).then_inc(wqo_lo, 1)

            def inputs_lo(i, b):
                dve.wait_ge(xnT_hi, 2 * i + b + 1)
                nc.vector.tensor_tensor(xnT[1][:, :, :].rearrange("p k s -> p (k s)"), bank[2][:, :],
                                        xnT[0][:, :, :].rearrange("p k s -> p (k s)"), ALU.subtract
                                        ).then_inc(xnT_lo, 1)

            def values(b):
                dve.wait_ge(v_ps, b + 1)
                nc.vector.tensor_tensor(v_sb[:, b, :], h_ps[0:KEYS, b % 2, 0:DIM], bv_row[:, :], ALU.add
                                        ).then_inc(v_rdy, 1)

            statistics(0, range(TP))
            aggregate(range(TP))
            refine(0, slice(0, TP))
            normalise(0, 0)
            cut_wqo(0)
            normalise(0, 1)
            cut_wqo(1)
            inputs_lo(0, 0)
            dve.wait_ge(vecs_rdy, 1)
            link(nc.vector.tensor_copy(gw[0][:, :, :], gw32))
            nc.vector.tensor_tensor(gw[1][:, :, :], gw32, gw[0][:, :, :], ALU.subtract).then_inc(gw_cut, 1)
            statistics(1, range(TP, 2 * TP))
            aggregate(range(TP, 2 * TP))
            refine(1, slice(TP, 2 * TP))
            dve.wait_ge(bv_in, 16)
            values(0)
            values(1)

            def sums(i, b, k):
                dve.wait_ge(p_exp, (2 * i + b) * 4 + k + 1)
                nc.vector.tensor_reduce(out=rsum[:, b, k, :], in_=by_head(probs[:, b, k, :]), axis=AX_X, op=ALU.add
                                        ).then_inc(p_sum, 1)
                dve.wait_ge(p_sum, (2 * i + b) * 4 + k + 1)
                nc.vector.reciprocal(rinv[:, b, k, :], rsum[:, b, k, :]).then_inc(p_rinv, 1)

            def norm2(i, beside):
                dve.wait_ge(var2_ready, i + 1)
                beside = x_root(2, slice(2 * TP, TILES)) if beside else None
                for n, ins in enumerate(root(mv2[:, :, 1:2].rearrange("p t o -> p (t o)"), rstd2[:, :],
                                             nt2[:, 0, :], nt2[:, 1, :])):
                    ins.then_inc(newton, 1)
                    if beside:
                        link(next(beside))
                    dve.wait_ge(newton, ROOT_OPS * i + n + 1)
                dve.wait_ge(xn2_kept, 16 * i)
                for t in range(TP):
                    row = x_all[:, bass.ds(i * TP + t, 1), :].rearrange("p o d -> p (o d)")
                    ins = nc.vector.tensor_scalar(xn2[:, t, :], row, mv2[:, t, 0:1], rstd2[:, t:t + 1],
                                                  ALU.subtract, ALU.mult)
                ins.then_inc(xn2_ready, 1)

            def norm2_lo(i, kc):
                dve.wait_ge(x2T_hi, KC * i + kc + 1)
                nc.vector.tensor_tensor(x2T[1][:, kc, :], bank[2 + kc][:, :], x2T[0][:, kc, :],
                                        ALU.subtract).then_inc(x2T_lo, 1)

            def iteration(i, prev, ahead, order=ORDER):
                for step, j, b, k, early in steps(order, i, prev, ahead):
                    if step == "norm":
                        normalise(j, b)
                    if step == "in":
                        inputs_lo(j, b)
                    if (step, k) == ("stats", 2):
                        statistics(2, range(2 * TP, TILES))
                    if (step, k) == ("stats", 3):
                        aggregate(range(2 * TP, TILES))
                    if step == "sums":
                        sums(j, b, k)
                    second_half(step, j, b, k, early)
                    if step == "soft":
                        quarter = (2 * j + b) * 4 + k
                        for half in range(2):
                            dve.wait_ge(s_ps, quarter * 2 + half + 1)
                            nc.vector.tensor_reduce(
                                out=smax[:, b, k, half * HH:(half + 1) * HH], in_=by_head(bank[half][:, 0:HALF]),
                                axis=AX_X, op=ALU.max).then_inc(s_max, 1)
                        if not early:
                            dve.wait_ge(pT_ps, (2 * j + b - 1) * CHUNKS)
                        for half in range(2):
                            dve.wait_ge(s_max, quarter * 2 + half + 1)
                            m = smax[:, b, k, half * HH:(half + 1) * HH].unsqueeze(2).to_broadcast([P, HH, KEYS])
                            nc.vector.tensor_tensor(by_head(probs[:, b, k, half * HALF:(half + 1) * HALF]),
                                                    by_head(bank[half][:, 0:HALF]), m, ALU.subtract
                                                    ).then_inc(s_shifted, 1)
                        if k >= 1:
                            sums(j, b, k - 1)
                        if early and b == 0 and k < 3:
                            values(2 * k + 2)
                            values(2 * k + 3)
                    if step == "h":
                        if is_last(j) and k == 0:
                            choose()
                        hidden_lo(j * HC + k, k, PTOK)
                        if is_last(j) and k in CUT_AFTER:
                            expert_lo(*CUT_AFTER[k])
                        if is_last(j) and k == 0:
                            sort()
                    if step == "y" and k == HC - 1:
                        add_shared(j)

            def second_half(step, j, b, k, early):
                if step == "values":
                    dve.wait_ge(o_hi, 2 * j + b + 1)
                    nc.vector.tensor_tensor(oT[1][:, :, :].rearrange("p g s -> p (g s)"), bank[3][:, :],
                                            oT[0][:, :, :].rearrange("p g s -> p (g s)"), ALU.subtract
                                            ).then_inc(o_lo, 1)
                if step == "out":
                    dve.wait_ge(proj_ps, 2 * j + b + 1)
                    dve.wait_ge(x_biased, TB * (2 * j + b + 1))
                    rows = x_all[:, bass.ds((2 * j + b) * TB, TB), :].rearrange("p t d -> p (t d)")
                    nc.vector.scalar_tensor_tensor(out=rows, in0=bank[2][:, :], scalar=gains[:, 0:1], in1=rows,
                                                   op0=ALU.mult, op1=ALU.add).then_inc(x1_ready, 1)
                    dve.wait_ge(gains_ready, 1)
                    dve.wait_ge(x1_ready, 2 * j + b + 1)
                    for t in range(TB):
                        row = x_all[:, bass.ds((2 * j + b) * TB + t, 1), :].rearrange("p o d -> p (o d)")
                        ins = nc.vector.bn_stats(stats2[:, b * TB + t, :], row)
                    ins.then_inc(stats2_rdy, 1)
                    if b == 1:
                        dve.wait_ge(stats2_rdy, 2 * j + 2)
                        nc.vector.memset(fill[:, :], 0.0)
                        for t in range(TP):
                            ins = nc.vector.bn_aggr(mv2[:, t, :], stats2[:, t, :])
                        ins.then_inc(var2_ready, 1)
                if step == "root":
                    norm2(j, early)
                if step == "norm2":
                    norm2_lo(j, k)

            def hidden_lo(q, c, width):
                dve.wait_ge(h_32, q + 1)
                nc.vector.tensor_tensor(hT[1][:, c % HB, 0:width], h32[:, c % 2, 0:width], hT[0][:, c % HB, 0:width],
                                        ALU.subtract).then_inc(h_lo, 1)

            def add_shared(j):
                dve.wait_ge(y_used, (j + 1) * HC)
                dve.wait_ge(x1_biased, TP * (j + 1))
                for h in range(2):
                    rows = x_all[:, bass.ds(j * TP + h * TB, TB), :].rearrange("p t d -> p (t d)")
                    ins = nc.vector.scalar_tensor_tensor(
                        out=rows, in0=y_ps[:, h * TB:(h + 1) * TB, :].rearrange("p t d -> p (t d)"),
                        scalar=gains[:, 1:2], in1=rows, op0=ALU.mult, op1=ALU.add)
                ins.then_inc(y_out, 1)

            def choose():
                dve.wait_ge(gate_rdy, PAIRS)
                dve.wait_ge(empty_made, 2)
                nc.vector.tensor_tensor(chosen[:, :], gate_sb[:, :, 1:2].rearrange("p t o -> p (t o)"),
                                        gate_sb[:, :, 0:1].rearrange("p t o -> p (t o)"), ALU.is_gt
                                        ).then_inc(chosen_rdy, 1)
                link(nc.vector.tensor_scalar(relu_b1[:, :, :], b1_sb[:, 1:1 + EXPERTS, :], 0.0, None, ALU.max))
                link(nc.vector.tensor_copy(relu_b1p[0][:, :, :], relu_b1[:, :, :]))
                nc.vector.tensor_tensor(relu_b1p[1][:, :, :], relu_b1[:, :, :], relu_b1p[0][:, :, :], ALU.subtract
                                        ).then_inc(rb_cut, 1)

            def sort():
                dve.wait_ge(counts_ps, 1)
                nc.vector.tensor_copy(rank1[:, :], bank[3][:, 64:64 + TILES])
                link(nc.vector.tensor_copy(tile_sum[:, :], bank[3][:, 128:128 + TILES]))
                link(nc.vector.tensor_tensor_scan(prefix[:, :], tile_sum[:, :], zero_tile[:, :], 0.0, ALU.add, ALU.add))
                link(nc.vector.tensor_tensor(rank1[:, 1:TILES], rank1[:, 1:TILES], prefix[:, 0:TILES - 1], ALU.add))
                link(nc.vector.tensor_tensor(rank0[:, :], number[:, :], rank1[:, :], ALU.subtract))
                link(nc.vector.tensor_scalar(count0[:, :], prefix[:, TILES - 1:TILES], -1.0, float(TOKENS),
                                             ALU.mult, ALU.add))
                link(nc.vector.tensor_scalar(past[:, :], seams[:, :], count0[:, :], None, ALU.is_lt))
                link(nc.vector.tensor_reduce(out=tiles0[:, :], in_=past[:, :], axis=AX_X, op=ALU.add))
                link(nc.vector.tensor_scalar(tiles0[:, :], tiles0[:, :], 1.0, None, ALU.add))
                nc.vector.tensor_copy(tiles0_int[:, :], tiles0[:, :]).then_inc(seam_rdy, 1)
                link(nc.vector.tensor_scalar(base1[:, :], tiles0[:, :], float(RTOK), None, ALU.mult))
                link(nc.vector.scalar_tensor_tensor(out=moved[:, :], in0=rank1[:, :], scalar=base1[:, :],
                                                    in1=rank0[:, :], op0=ALU.add, op1=ALU.subtract))
                link(nc.vector.tensor_tensor(moved[:, :], moved[:, :], chosen[:, :], ALU.mult))
                link(nc.vector.tensor_tensor(place[:, :], rank0[:, :], moved[:, :], ALU.add))
                nc.vector.tensor_copy(place_int[:, :], place[:, :]).then_inc(places_rdy, 1)

            def expert_lo(e, n):
                dve.wait_ge(w_hi, 3 + 2 * e + n)
                hi, lo = ((ew1_sb[m][:, e, :, :], ew2_sb[m][:, e, :, :])[n].rearrange("p k h -> p (k h)")
                          for m in range(2))
                nc.vector.tensor_tensor(lo, stage[:, n, :], hi, ALU.subtract).then_inc(w_lo, 1)

            iteration(0, False, True, START)
            with dve.Fori(1, PAIRS - 1) as i:
                iteration(i, True, True)
            iteration(PAIRS - 1, True, False, END)

            def sorted_lo(j):
                dve.wait_ge(xsT_hi, j + 1)
                nc.vector.tensor_tensor(xsT[1][:, bass.ds(j % 2, 1), :, :].rearrange("p o k s -> p (o k s)"),
                                        bank[2][:, :],
                                        xsT[0][:, bass.ds(j % 2, 1), :, :].rearrange("p o k s -> p (o k s)"),
                                        ALU.subtract).then_inc(xsT_lo, 1)

            sorted_lo(0)
            tiles_of_0 = dve.value_load(tiles0_int[0:1, 0:1], min_val=1, max_val=RTILES - 1)

            def routed(j, e):
                for c in range(HC):
                    hidden_lo(PAIRS * HC + j * HC + c, c, RTOK)
                    if c == 0:
                        dve.wait_ge(xs_in, 16 * (j + 1))
                        dve.wait_ge(gathered, 32 * j)
                        nc.vector.tensor_copy(gather_token[:, :], xs[:, :, DIM:ROW].rearrange("p t o -> p (t o)")
                                              ).then_inc(ids_copied, 1)
                    if c == 5:
                        dve.wait_ge(ids_copied, j + 1)
                        dve.wait_ge(rows_out, 32 * j)
                        nc.vector.tensor_copy(scatter_token[:, :], gather_token[:, :]).then_inc(scatter_ids, 1)
                    if c == 6:
                        sorted_lo(j + 1)
                dve.wait_ge(y_used, PAIRS * HC + (j + 1) * HC)
                dve.wait_ge(part_rdy, RT * (j + 1))
                dve.wait_ge(rows_out, 32 * j)
                nc.vector.scalar_tensor_tensor(
                    out=final[:, :, :].rearrange("p t d -> p (t d)"),
                    in0=y_ps[:, 0:RT, :].rearrange("p t d -> p (t d)"), scalar=gains[:, 1:2],
                    in1=part[:, :, :].rearrange("p t d -> p (t d)"), op0=ALU.mult, op1=ALU.add
                ).then_inc(final_rdy, 1)

            with dve.Fori(0, tiles_of_0) as j:
                routed(j, 0)
            with dve.Fori(tiles_of_0, RTILES) as j:
                routed(j, 1)

        @block.tensor
        def _(pe):
            def mm(out_, lhsT, rhs, start, stop, **kw):
                return nc.tensor.matmul(out_, lhsT, rhs, start=start, stop=stop, **kw)

            def cut(out_, lhs, rhs, start, stop, **kw):
                for n, (a, b) in enumerate(((0, 0), (1, 0), (0, 1))):
                    ins = mm(out_, lhs(a), rhs(b), start and n == 0, stop and n == 2, **kw)
                return ins

            pe.wait_ge(consts_made, 1)
            pe.wait_ge(context_in, 16)
            for n in range(CKC * 2):
                for q in range(4):
                    ins = nc.tensor.transpose(bank[n][0:CK, q * KEYS:(q + 1) * KEYS],
                                              y_sb[:, (n % 2) * 4 + q, (n // 2) * CK:(n // 2 + 1) * CK],
                                              ident[0:KEYS, 0:KEYS])
                ins.then_inc(yT_ps, 1)
            pe.wait_ge(yT_sb, 1)
            pe.wait_ge(vecs_in, 16 * 5)
            nc.tensor.transpose(bank[0][:, 0:VECS], vec_rows[:, :], ident[0:VECS, 0:VECS]).then_inc(vecs_ps, 1)
            pe.wait_ge(wk_in, 16)
            for half in range(2):
                pe.wait_ge(yT_sb, 3 + half)
                for g in range(GROUPS):
                    for k in range(CKC):
                        ins = mm(keys_bank(half, g), wk_sb[:, k, g * P:(g + 1) * P],
                                 yT[:, k, half * YH:(half + 1) * YH], k == 0, k == CKC - 1)
                    ins.then_inc(kT_ps, 1)

            def values(b):
                if b == 0:
                    pe.wait_ge(wv_in, 16)
                    pe.wait_ge(kT_sb, 3)
                if b >= 2:
                    pe.wait_ge(v_rdy, b - 1)
                for k in range(CKC):
                    ins = mm(h_ps[0:KEYS, b % 2, 0:DIM], yT[:, k, b * KEYS:(b + 1) * KEYS], wv_sb[:, k, :],
                             k == 0, k == CKC - 1)
                ins.then_inc(v_ps, 1)

            def inputs(i, b):
                pe.wait_ge(xn_ready, 2 * i + b + 1)
                for kc in range(KC):
                    for t in range(TB):
                        ins = nc.tensor.transpose(bank[2][:, kc * SEQ + t * P:kc * SEQ + (t + 1) * P],
                                                  xn[:, b, t, kc * P:(kc + 1) * P], ident[:, :])
                ins.then_inc(xnT_ps, 1)

            def queries(i, b, prev):
                if prev and b == 0:
                    pe.wait_ge(gate_rdy, i - 1)
                elif prev:
                    pe.wait_ge(q_sb, GROUPS * (2 * i + 1))
                elif (i, b) == (0, 0):
                    pe.wait_ge(wqo_lo, 1)
                elif (i, b) == (1, 1):
                    pe.wait_ge(o_lo, 1)
                else:
                    pe.wait_ge(q_sb, GROUPS * (2 * i + b))
                pe.wait_ge(xnT_lo, 2 * i + b + 1)
                for g in range(GROUPS):
                    for kc in range(KC):
                        ins = cut(bank[3][:, g * SEQ:(g + 1) * SEQ],
                                  lambda m: wqo_sb[m][:, 0, kc, g * P:(g + 1) * P],
                                  lambda m: xnT[m][:, kc, :], kc == 0, kc == KC - 1)
                ins.then_inc(q_ps, 1)

            def attention(step, j, b, k, first, ahead, more_scores, start):
                if step == "turn":
                    for u in TURNS[k]:
                        if u == 0:
                            pe.wait_ge(p_ready, (2 * j + b) * 4 + 2)
                        if u == 2:
                            pe.wait_ge(p_ready, (2 * j + b) * 4 + 4)
                        if u >= 2:
                            pe.wait_ge(pT_sb, 2 * ((2 * j + b) * CHUNKS + u - 1))
                        elif start:
                            pe.wait_ge(*{(0, 0): ((xnT_lo, 3), (q_sb, GROUPS * 3)),
                                         (0, 1): ((x1_ready, 1), (q_sb, GROUPS * 4)),
                                         (1, 0): ((x1_ready, 2), (o_lo, 2))}[j, b][u])
                        elif b == 1 and ahead:
                            pe.wait_ge(*((xnT_lo, 2 * j + 3), (q_sb, GROUPS * (2 * j + 3)))[u])
                        elif b == 1:
                            pe.wait_ge(*((x1_ready, 2 * j + 1), (gate_rdy, j))[u])
                        else:
                            pe.wait_ge(*((xnT_lo, 2 * j + 2), (q_sb, GROUPS * (2 * j + 2)))[u])
                        for v in range(2):
                            ch = 2 * u + v
                            g, c = ch // CHUNKS, ch % CHUNKS
                            for t in range(TB):
                                ins = nc.tensor.transpose(
                                    bank[2 + u % 2][0:ROWS[c], v * SEQ + t * P:v * SEQ + (t + 1) * P],
                                    probs[:, b, g * TB + t, c * P:c * P + ROWS[c]], ident[:, :])
                        ins.then_inc(pT_ps, 1)
                if step == "values":
                    pe.wait_ge(v_in[b], 16 * len(PIECES) * (j + 1))
                    pe.wait_ge(pT_sb, 2 * CHUNKS * (2 * j + b + 1))
                    for g in range(GROUPS):
                        for c in range(CHUNKS):
                            ins = mm(bank[3][:, g * SEQ:(g + 1) * SEQ], v_diag[0:ROWS[c], b, g, c, :],
                                     pT[0:ROWS[c], g * CHUNKS + c, :], c == 0, c == CHUNKS - 1)
                    ins.then_inc(o_ps, 1)
                if step == "out":
                    if first:
                        pe.wait_ge(wqo_lo, 2)
                    elif b == 0:
                        pe.wait_ge(x2T_lo, KC * (j - 1) + 1)
                    pe.wait_ge(o_lo, 2 * j + b + 1)
                    for t in range(TB):
                        for kc in range(KC):
                            ins = cut(bank[2][:, t * DIM:(t + 1) * DIM], lambda m: oT[m][:, kc, t * P:(t + 1) * P],
                                      lambda m: wqo_sb[m][:, 1, kc, :], kc == 0, kc == KC - 1)
                    ins.then_inc(proj_ps, 1)
                if step == "norm2":
                    pe.wait_ge(xn2_ready, j + 1)
                    if k == 1 and more_scores:
                        pe.wait_ge(o_lo, 2 * j + 3)
                    for t in range(TP):
                        ins = nc.tensor.transpose(bank[2 + k][:, t * P:(t + 1) * P],
                                                  xn2[:, t, k * P:(k + 1) * P], ident[:, :])
                    ins.then_inc(x2T_ps, 1)
                if step == "gate":
                    pe.wait_ge(x2T_lo, KC * (j + 1))
                    for kc in range(KC):
                        ins = cut(bank[3][0:EXPERTS, :], lambda m: gw[m][:, :, kc], lambda m: x2T[m][:, kc, :],
                                  kc == 0, kc == KC - 1)
                    ins.then_inc(gate_ps, 1)
                if step == "gate_turn":
                    pe.wait_ge(consts_made, 1)
                    pe.wait_ge(gate_copied, j + 1)
                    for t in range(TP):
                        ins = nc.tensor.transpose(bank[3][:, t * EXPERTS:(t + 1) * EXPERTS],
                                                  gate_rows[:, t * P:(t + 1) * P], ident[0:EXPERTS, 0:EXPERTS])
                    ins.then_inc(gate_turned, 1)

            def iteration(i, prev, ahead, order=ORDER):
                for step, j, b, k, early in steps(order, i, prev, ahead):
                    if step == "in":
                        if prev:
                            pe.wait_ge(x1_ready, 2 * j - 1 + b)
                        inputs(j, b)
                    if step == "query":
                        queries(j, b, prev)
                    if step == "scores":
                        t, g = k % TB, k // TB
                        quarter = (2 * j + b) * 4 + k
                        if k == 0:
                            pe.wait_ge(q_sb, GROUPS * (2 * j + b + 1))
                            pe.wait_ge(k_in[b], 16 * HG * (j + 1))
                        for half in range(2):
                            if not early or (b, k) != (0, 0):
                                pe.wait_ge(s_shifted, quarter * 2 - 1 + half)
                            mm(bank[half][:, 0:HALF], qT[:, b, g, t * P:(t + 1) * P],
                               k_diag[:, b, g, half * HALF:(half + 1) * HALF], True, True).then_inc(s_ps, 1)
                        if early and b == 0 and k < 3:
                            values(2 * k + 2)
                            values(2 * k + 3)
                    attention(step, j, b, k, early and b == 0, ahead, not is_last(j), not prev)
                    if step == "count":
                        pe.wait_ge(chosen_rdy, 1)
                        pe.wait_ge(empty_made, 2)
                        mm(bank[3][:, 64:64 + TILES], before[:, :], chosen[:, :], True, True)
                        mm(bank[3][:, 128:128 + TILES], ones[:, :], chosen[:, :], True, True).then_inc(counts_ps, 1)
                    if step == "h":
                        shared_h(j, k)
                    if step == "y":
                        shared_y(j, k)

            def shared_h(j, k):
                if k == 0:
                    pe.wait_ge(w_lo, 2)
                    pe.wait_ge(x2T_lo, KC * (j + 1))
                pe.wait_ge(h_32, j * HC + k - 1 if k >= 2 else j * HC)
                for kc in range(KC):
                    ins = cut(h_ps[:, k % 2, :], lambda m: sw1_sb[m][:, kc, k * P:(k + 1) * P],
                              lambda m: x2T[m][:, kc, :], kc == 0, kc == KC - 1)
                ins.then_inc(h_in_ps, 1)

            def shared_y(j, c):
                pe.wait_ge(h_lo, j * HC + c + 1)
                if c == 0:
                    pe.wait_ge(y_out, j)
                for t in range(TP):
                    ins = cut(y_ps[:, t, :], lambda m: hT[m][:, c % HB, t * P:(t + 1) * P],
                              lambda m: sw2_sb[m][:, c, :], c == 0 and t % 2 == 0, c == HC - 1,
                              skip_group_check=True)
                ins.then_inc(y_used, 1)

            inputs(0, 0)
            queries(0, 0, False)
            values(0)
            values(1)
            iteration(0, False, True, START)
            with pe.Fori(1, PAIRS - 1) as i:
                iteration(i, True, True)
            iteration(PAIRS - 1, True, False, END)

            def other(e):
                pe.wait_ge(w_lo, 4 + 2 * e)
                for c in range(HC):
                    ins = cut(bank[3][:, e * DIM:(e + 1) * DIM],
                              lambda m: relu_b1p[m][:, e, c:c + 1].to_broadcast([P, P]),
                              lambda m: ew2_sb[m][:, e, c, :], c == 0, c == HC - 1)
                ins.then_inc(other_ps, 1)

            def sorted_transposed(j):
                pe.wait_ge(xs_in, 16 * (j + 1))
                pe.wait_ge(xsT_lo, j)
                for kc in range(KC):
                    for t in range(RT):
                        ins = nc.tensor.transpose(bank[2][:, kc * RTOK + t * P:kc * RTOK + (t + 1) * P],
                                                  xs[:, t, kc * P:(kc + 1) * P], ident[:, :])
                ins.then_inc(xsT_ps, 1)

            pe.wait_ge(rb_cut, 1)
            pe.wait_ge(places_rdy, 1)
            other(0)
            sorted_transposed(0)
            other(1)
            pe.wait_ge(y_out, PAIRS)
            pe.wait_ge(seam_rdy, 1)
            tiles_of_0 = pe.value_load(tiles0_int[0:1, 0:1], min_val=1, max_val=RTILES - 1)

            def routed(j, e):
                q = PAIRS * HC + j * HC
                pe.wait_ge(xsT_lo, j + 1)
                for n in range(HC + 3):
                    if n < HC:
                        pe.wait_ge(h_32, q + n - 3)
                        for kc in range(KC):
                            ins = cut(hidden_bank(n % 4)[:, 0:RTOK],
                                      lambda m: ew1_sb[m][:, e, kc, n * P:(n + 1) * P],
                                      lambda m: xsT[m][:, bass.ds(j % 2, 1), kc, :].rearrange("p o s -> p (o s)"),
                                      kc == 0, kc == KC - 1)
                        ins.then_inc(h_in_ps, 1)
                    if n == 6:
                        sorted_transposed(j + 1)
                    if n >= 3:
                        c = n - 3
                        pe.wait_ge(h_lo, q + c + 1)
                        if c == 0:
                            pe.wait_ge(final_rdy, j)
                        for t in range(RT):
                            ins = cut(y_ps[:, t, :], lambda m: hT[m][:, c % HB, t * P:(t + 1) * P],
                                      lambda m: ew2_sb[m][:, e, c, :], c == 0 and t == 0, c == HC - 1,
                                      skip_group_check=True)
                        ins.then_inc(y_used, 1)

            with pe.Fori(0, tiles_of_0) as j:
                routed(j, 0)
            with pe.Fori(tiles_of_0, RTILES) as j:
                routed(j, 1)


_INS = ["x", "ctx_768", "g_xattn", "g_ffn", "L0_xattn_wq", "L0_xattn_bq", "L0_xattn_wk", "L0_xattn_bk",
        "L0_xattn_wv", "L0_xattn_bv", "L0_xattn_wo", "L0_xattn_bo", "L0_ffn_gate_w", "L0_ffn_w1", "L0_ffn_b1",
        "L0_ffn_w2", "L0_ffn_b2", "L0_ffn_sw1", "L0_ffn_sb1", "L0_ffn_sw2", "L0_ffn_sb2"]


def kernel(**inputs):
    import numpy as np
    from concourse import bacc
    from concourse.bass_utils import run_bass_kernel_spmd

    nc = bacc.Bacc("TRN2", target_bir_lowering=False, num_devices=1)
    arrays, args = {}, []
    for name in _INS:
        a = np.ascontiguousarray(inputs[name])
        arrays[f"in_{name}"] = a
        args.append(nc.dram_tensor(f"in_{name}", a.shape, mybir.dt.from_np(a.dtype), kind="ExternalInput").ap())
    out = nc.dram_tensor("out", (TOKENS, DIM), F32, kind="ExternalOutput").ap()
    build(nc, *args, out)
    r = run_bass_kernel_spmd(nc, [arrays], core_ids=[0])
    return r.results[0]["out"].reshape(BATCHES, SEQ, DIM)
```
